# Optimizing a Trainium2 kernel written in Bass

```python
import numpy as np
import jax
import jax.numpy as jnp

def _softmax(x, axis=-1):
    return jax.nn.softmax(x, axis=axis)

def _gelu(x):
    return jax.nn.gelu(x, approximate=True)

def _silu(x):
    return jax.nn.silu(x)

def _sigmoid(x):
    return jax.nn.sigmoid(x)

def _layernorm(x, axis=-1, eps=1e-05):
    m = jnp.mean(x, axis=axis, keepdims=True)
    v = jnp.var(x, axis=axis, keepdims=True)
    return (x - m) / jnp.sqrt(v + eps)

def _scatter_add(tgt, idx, src, axis=0):
    return tgt.at[idx].add(src)

def _segment_sum(src, seg, n):
    return jax.ops.segment_sum(src, seg, n)
kernel_name = 'mk_decoder_preln_d2_seqx_r8_105e98'

def setup_inputs(seed: int=0):
    np.random.seed(seed)
    _w = jnp.asarray

    def _rec_inputs():
        import jax
        import jax.numpy as jnp
        _rk = jax.random.key(seed)
        x = -0.0003929 + 0.9999 * jax.random.normal(jax.random.fold_in(_rk, 1), (16, 128, 256), jnp.float32)
        _lenS = 128 - jax.random.randint(jax.random.fold_in(_rk, 7), (16,), 0, max(1, 128 // 4) + 1, jnp.int32)
        _lenS2 = 128 - jax.random.randint(jax.random.fold_in(_rk, 8), (16,), 0, max(1, 128 // 4) + 1, jnp.int32)
        _ctx_1024P = jax.random.normal(jax.random.fold_in(_rk, 11), (16, 16, 128), jnp.float32)
        _ctx_1024c = jax.random.dirichlet(jax.random.fold_in(_rk, 511), 0.3 * jnp.ones((16,), jnp.float32), (16, 128))
        _ctx_1024t = jnp.einsum('bsk,bkd->bsd', _ctx_1024c, _ctx_1024P)
        _ctx_1024t = _ctx_1024t * jax.lax.rsqrt(jnp.mean(jnp.square(_ctx_1024t)) + 1e-12) * 0.953939
        ctx_1024 = 0.000227908 + 0.99994 * (_ctx_1024t + 0.3 * jax.random.normal(jax.random.fold_in(_rk, 611), (16, 128, 128), jnp.float32))
        _validS = jnp.arange(128)[None, :] < _lenS[:, None]
        _validS2 = jnp.arange(128)[None, :] < _lenS2[:, None]
        _causal = jnp.tril(jnp.ones((128, 128), dtype=bool))
        mask_BxS2_bf1 = jnp.ones((16, 128), dtype=bool)
        return (x, ctx_1024, mask_BxS2_bf1)
    x, ctx_1024, mask_BxS2_bf1 = _rec_inputs()

    def _L0_attn_setup():
        import jax, jax.numpy as jnp
        import numpy as np
        B, S, E, H = (2, 256, 256, 16)
        D = E // H
        ROPE_BASE = 10000.0

        def rotate_half(x):
            x1 = x[..., ::2]
            x2 = x[..., 1::2]
            return jnp.stack((-x2, x1), axis=-1).reshape(x.shape[:-1] + (x.shape[-1],))

        def rope_cos_sin(seq_len, head_dim, start_pos=0):
            inv_freq = 1.0 / ROPE_BASE ** (jnp.arange(0, head_dim, 2, dtype=jnp.float32) / head_dim)
            positions = jnp.arange(start_pos, start_pos + seq_len, dtype=jnp.float32)
            freqs = jnp.outer(positions, inv_freq)
            emb = jnp.concatenate([freqs, freqs], axis=-1)
            return (emb[None, None].astype(jnp.float32), emb)
        key = jax.random.key(seed)
        k1, k2, k3 = jax.random.split(key, 3)
        x = jax.random.normal(k1, (B, S, E), dtype=jnp.float32)
        Wqkv = jax.random.normal(k2, (3 * E, E), dtype=jnp.float32) * E ** (-0.5)
        Wout = jax.random.normal(k3, (E, E), dtype=jnp.float32) * E ** (-0.5)
        return {'x': x, 'Wqkv': Wqkv, 'Wout': Wout}
    _L0_attn_all = _L0_attn_setup()
    _L0_attn_in = {k: v for k, v in _L0_attn_all.items() if k in ('Wqkv', 'Wout')}
    del _L0_attn_all

    def _L0_xattn_setup():
        import jax, jax.numpy as jnp
        import numpy as np
        EPS = 1e-05

        def rmsnorm(x, g, eps=EPS):
            var = jnp.mean(jnp.square(x), axis=-1, keepdims=True)
            return x * jax.lax.rsqrt(var + eps) * g
        key = jax.random.key(seed)
        ks = jax.random.split(key, 8)
        B, Sq, Skv = (2, 512, 64)
        dim, cdim, H, D = (256, 128, 16, 128)
        inner = H * D
        s = lambda f: 1.0 / np.sqrt(f)
        return {'hidden_states': jax.random.normal(ks[0], (B, Sq, dim), jnp.float32), 'encoder_hidden_states': jax.random.normal(ks[1], (B, Skv, cdim), jnp.float32), 'Wq': jax.random.normal(ks[2], (dim, inner), jnp.float32) * s(dim), 'Wk': jax.random.normal(ks[3], (cdim, inner), jnp.float32) * s(cdim), 'Wv': jax.random.normal(ks[4], (cdim, inner), jnp.float32) * s(cdim), 'Wo': jax.random.normal(ks[5], (inner, dim), jnp.float32) * s(inner), 'gq': jnp.ones((D,), jnp.float32), 'gk': jnp.ones((D,), jnp.float32)}
    _L0_xattn_all = _L0_xattn_setup()
    _L0_xattn_in = {k: v for k, v in _L0_xattn_all.items() if k in ('Wq', 'Wk', 'Wv', 'Wo', 'gq', 'gk')}
    del _L0_xattn_all

    def _L0_ffn_setup():
        import jax, jax.numpy as jnp
        import numpy as np
        HIDDEN = 256
        INTER = 1024
        MOE_INTER = 128
        N_ROUTED = 8
        NUM_LOCAL = 8
        TOP_K = 2
        B, S = (4, 256)

        def _mlp(x, gw, uw, dw):
            g = x @ gw.T
            u = x @ uw.T
            return g * jax.nn.sigmoid(g) * u @ dw.T
        key = jax.random.key(seed)
        ks = jax.random.split(key, 8)
        std = 0.02
        return {'hidden_states': jax.random.normal(ks[0], (B, S, HIDDEN), jnp.float32), 'router_weight': jax.random.normal(ks[1], (N_ROUTED, HIDDEN), jnp.float32) * std, 'sh_gate': jax.random.normal(ks[2], (INTER, HIDDEN), jnp.float32) * std, 'sh_up': jax.random.normal(ks[3], (INTER, HIDDEN), jnp.float32) * std, 'sh_down': jax.random.normal(ks[4], (HIDDEN, INTER), jnp.float32) * std, 'r_gate': jax.random.normal(ks[5], (MOE_INTER, HIDDEN), jnp.float32) * std, 'r_up': jax.random.normal(ks[6], (MOE_INTER, HIDDEN), jnp.float32) * std, 'r_down': jax.random.normal(ks[7], (HIDDEN, MOE_INTER), jnp.float32) * std}
    _L0_ffn_all = _L0_ffn_setup()
    _L0_ffn_in = {k: v for k, v in _L0_ffn_all.items() if k in ('router_weight', 'sh_gate', 'sh_up', 'sh_down', 'r_gate', 'r_up', 'r_down')}
    del _L0_ffn_all

    def _L1_attn_setup():
        import jax, jax.numpy as jnp
        import numpy as np
        D_MODEL, H, G = (256, 32, 8)
        D_K = D_MODEL // H
        GROUP_SIZE = H // G
        B, S = (2, 256)
        key = jax.random.key(seed)
        ks = jax.random.split(key, 9)
        sd = 1.0 / np.sqrt(D_MODEL)
        x = jax.random.normal(ks[0], (B, S, D_MODEL), dtype=jnp.float32)
        Wq = jax.random.normal(ks[1], (D_MODEL, D_MODEL), dtype=jnp.float32) * sd
        bq = jax.random.normal(ks[2], (D_MODEL,), dtype=jnp.float32) * 0.01
        Wk = jax.random.normal(ks[3], (D_MODEL, G * D_K), dtype=jnp.float32) * sd
        bk = jax.random.normal(ks[4], (G * D_K,), dtype=jnp.float32) * 0.01
        Wv = jax.random.normal(ks[5], (D_MODEL, G * D_K), dtype=jnp.float32) * sd
        bv = jax.random.normal(ks[6], (G * D_K,), dtype=jnp.float32) * 0.01
        Wo = jax.random.normal(ks[7], (D_MODEL, D_MODEL), dtype=jnp.float32) * sd
        bo = jax.random.normal(ks[8], (D_MODEL,), dtype=jnp.float32) * 0.01
        return {'x': x, 'Wq': Wq, 'bq': bq, 'Wk': Wk, 'bk': bk, 'Wv': Wv, 'bv': bv, 'Wo': Wo, 'bo': bo}
    _L1_attn_all = _L1_attn_setup()
    _L1_attn_in = {k: v for k, v in _L1_attn_all.items() if k in ('Wq', 'bq', 'Wk', 'bk', 'Wv', 'bv', 'Wo', 'bo')}
    del _L1_attn_all

    def _L1_xattn_setup():
        import jax, jax.numpy as jnp
        import numpy as np
        N_HEADS = 16
        N_KV_HEADS = 8
        HEAD_DIM = 128
        D_TEXT = 256
        D_VISION = 128
        GROUPS = N_HEADS // N_KV_HEADS
        key = jax.random.key(seed)
        ks = jax.random.split(key, 6)
        B, T_text, T_vis = (4, 256, 72)
        text_hidden = jax.random.normal(ks[0], (B, T_text, D_TEXT), dtype=jnp.float32)
        vision_tokens = jax.random.normal(ks[1], (B, T_vis, D_VISION), dtype=jnp.float32)
        vision_mask = jnp.ones((B, T_vis), dtype=bool)
        s = 0.02
        Wq = jax.random.normal(ks[2], (D_TEXT, N_HEADS * HEAD_DIM), dtype=jnp.float32) * s
        Wk = jax.random.normal(ks[3], (D_VISION, N_KV_HEADS * HEAD_DIM), dtype=jnp.float32) * s
        Wv = jax.random.normal(ks[4], (D_VISION, N_KV_HEADS * HEAD_DIM), dtype=jnp.float32) * s
        Wo = jax.random.normal(ks[5], (N_HEADS * HEAD_DIM, D_TEXT), dtype=jnp.float32) * s
        return {'text_hidden': text_hidden, 'vision_tokens': vision_tokens, 'vision_mask': vision_mask, 'Wq': Wq, 'Wk': Wk, 'Wv': Wv, 'Wo': Wo}
    _L1_xattn_all = _L1_xattn_setup()
    _L1_xattn_in = {k: v for k, v in _L1_xattn_all.items() if k in ('Wq', 'Wk', 'Wv', 'Wo')}
    del _L1_xattn_all

    def _L1_ffn_setup():
        import jax, jax.numpy as jnp
        import numpy as np
        _FP8_MAX = 448.0
        _BLOCK = 32
        _EPS = 1e-30

        def _mx_dequant(t):
            rows, feat = t.shape
            blocks = t.reshape(rows, feat // _BLOCK, _BLOCK)
            max_abs = jnp.max(jnp.abs(blocks), axis=-1)
            scales = jnp.maximum(max_abs / _FP8_MAX, _EPS)
            q = (blocks / scales[..., None]).astype(jnp.float8_e4m3fn).astype(jnp.float32)
            return (q * scales[..., None]).reshape(rows, feat)

        def _mx_linear(x2d, w):
            return _mx_dequant(x2d) @ _mx_dequant(w).T
        key = jax.random.key(seed)
        k1, k2, k3, k4 = jax.random.split(key, 4)
        B, S, H, I = (2, 128, 256, 1024)
        return {'x': jax.random.normal(k1, (B, S, H), dtype=jnp.float32), 'gate_w': jax.random.normal(k2, (I, H), dtype=jnp.float32) * 0.02, 'up_w': jax.random.normal(k3, (I, H), dtype=jnp.float32) * 0.02, 'down_w': jax.random.normal(k4, (H, I), dtype=jnp.float32) * 0.02}
    _L1_ffn_all = _L1_ffn_setup()
    _L1_ffn_in = {k: v for k, v in _L1_ffn_all.items() if k in ('gate_w', 'up_w', 'down_w')}
    del _L1_ffn_all
    return {'x': x, 'ctx_1024': ctx_1024, 'mask_BxS2_bf1': mask_BxS2_bf1, 'L0_attn_Wqkv': _L0_attn_in['Wqkv'], 'L0_attn_Wout': _L0_attn_in['Wout'], 'L0_xattn_Wq': _L0_xattn_in['Wq'], 'L0_xattn_Wk': _L0_xattn_in['Wk'], 'L0_xattn_Wv': _L0_xattn_in['Wv'], 'L0_xattn_Wo': _L0_xattn_in['Wo'], 'L0_xattn_gq': _L0_xattn_in['gq'], 'L0_xattn_gk': _L0_xattn_in['gk'], 'L0_ffn_router_weight': _L0_ffn_in['router_weight'], 'L0_ffn_sh_gate': _L0_ffn_in['sh_gate'], 'L0_ffn_sh_up': _L0_ffn_in['sh_up'], 'L0_ffn_sh_down': _L0_ffn_in['sh_down'], 'L0_ffn_r_gate': _L0_ffn_in['r_gate'], 'L0_ffn_r_up': _L0_ffn_in['r_up'], 'L0_ffn_r_down': _L0_ffn_in['r_down'], 'L1_attn_Wq': _L1_attn_in['Wq'], 'L1_attn_bq': _L1_attn_in['bq'], 'L1_attn_Wk': _L1_attn_in['Wk'], 'L1_attn_bk': _L1_attn_in['bk'], 'L1_attn_Wv': _L1_attn_in['Wv'], 'L1_attn_bv': _L1_attn_in['bv'], 'L1_attn_Wo': _L1_attn_in['Wo'], 'L1_attn_bo': _L1_attn_in['bo'], 'L1_xattn_Wq': _L1_xattn_in['Wq'], 'L1_xattn_Wk': _L1_xattn_in['Wk'], 'L1_xattn_Wv': _L1_xattn_in['Wv'], 'L1_xattn_Wo': _L1_xattn_in['Wo'], 'L1_ffn_gate_w': _L1_ffn_in['gate_w'], 'L1_ffn_up_w': _L1_ffn_in['up_w'], 'L1_ffn_down_w': _L1_ffn_in['down_w']}

def reference(x, ctx_1024, mask_BxS2_bf1, L0_attn_Wqkv, L0_attn_Wout, L0_xattn_Wq, L0_xattn_Wk, L0_xattn_Wv, L0_xattn_Wo, L0_xattn_gq, L0_xattn_gk, L0_ffn_router_weight, L0_ffn_sh_gate, L0_ffn_sh_up, L0_ffn_sh_down, L0_ffn_r_gate, L0_ffn_r_up, L0_ffn_r_down, L1_attn_Wq, L1_attn_bq, L1_attn_Wk, L1_attn_bk, L1_attn_Wv, L1_attn_bv, L1_attn_Wo, L1_attn_bo, L1_xattn_Wq, L1_xattn_Wk, L1_xattn_Wv, L1_xattn_Wo, L1_ffn_gate_w, L1_ffn_up_w, L1_ffn_down_w):
    import jax
    import jax.numpy as jnp

    def _L0_attn_ref(x, Wqkv, Wout):
        import jax, jax.numpy as jnp
        import numpy as np
        B, S, E, H = (2, 256, 256, 16)
        D = E // H
        ROPE_BASE = 10000.0

        def rotate_half(x):
            x1 = x[..., ::2]
            x2 = x[..., 1::2]
            return jnp.stack((-x2, x1), axis=-1).reshape(x.shape[:-1] + (x.shape[-1],))

        def rope_cos_sin(seq_len, head_dim, start_pos=0):
            inv_freq = 1.0 / ROPE_BASE ** (jnp.arange(0, head_dim, 2, dtype=jnp.float32) / head_dim)
            positions = jnp.arange(start_pos, start_pos + seq_len, dtype=jnp.float32)
            freqs = jnp.outer(positions, inv_freq)
            emb = jnp.concatenate([freqs, freqs], axis=-1)
            return (emb[None, None].astype(jnp.float32), emb)
        batch, seq_len, emb = x.shape
        scale = D ** (-0.5)
        qkv = x @ Wqkv.T
        qkv = qkv.reshape(batch, seq_len, 3, H, D)
        qkv = jnp.transpose(qkv, (2, 0, 3, 1, 4))
        q, k, v = (qkv[0], qkv[1], qkv[2])
        inv_freq = 1.0 / ROPE_BASE ** (jnp.arange(0, D, 2, dtype=jnp.float32) / D)
        positions = jnp.arange(seq_len, dtype=jnp.float32)
        freqs = jnp.outer(positions, inv_freq)
        emb_ang = jnp.concatenate([freqs, freqs], axis=-1)
        cos = jnp.cos(emb_ang)[None, None]
        sin = jnp.sin(emb_ang)[None, None]
        q = q * cos + rotate_half(q) * sin
        k = k * cos + rotate_half(k) * sin
        scores = jnp.einsum('bhqd,bhkd->bhqk', q, k) * scale
        causal = jnp.arange(seq_len)[None, :] > jnp.arange(seq_len)[:, None]
        scores = jnp.where(causal[None, None], -jnp.inf, scores)
        attn = jax.nn.softmax(scores, axis=-1)
        out = jnp.einsum('bhqk,bhkd->bhqd', attn, v)
        out = jnp.transpose(out, (0, 2, 1, 3)).reshape(batch, seq_len, emb)
        return out @ Wout.T

    def _L0_xattn_ref(hidden_states, encoder_hidden_states, Wq, Wk, Wv, Wo, gq, gk):
        import jax, jax.numpy as jnp
        import numpy as np
        EPS = 1e-05

        def rmsnorm(x, g, eps=EPS):
            var = jnp.mean(jnp.square(x), axis=-1, keepdims=True)
            return x * jax.lax.rsqrt(var + eps) * g
        B, Sq, _ = hidden_states.shape
        Skv = encoder_hidden_states.shape[1]
        D = gq.shape[0]
        H = Wq.shape[1] // D
        scale = 1.0 / np.sqrt(D)
        q = (hidden_states @ Wq).reshape(B, Sq, H, D)
        k = (encoder_hidden_states @ Wk).reshape(B, Skv, H, D)
        v = (encoder_hidden_states @ Wv).reshape(B, Skv, H, D)
        q = rmsnorm(q, gq)
        k = rmsnorm(k, gk)
        scores = jnp.einsum('bqhd,bkhd->bhqk', q, k) * scale
        attn = jax.nn.softmax(scores, axis=-1)
        out = jnp.einsum('bhqk,bkhd->bqhd', attn, v)
        out = out.reshape(B, Sq, H * D)
        return out @ Wo

    def _L0_ffn_ref(hidden_states, router_weight, sh_gate, sh_up, sh_down, r_gate, r_up, r_down):
        import jax, jax.numpy as jnp
        import numpy as np
        HIDDEN = 256
        INTER = 1024
        MOE_INTER = 128
        N_ROUTED = 8
        NUM_LOCAL = 8
        TOP_K = 2
        B, S = (4, 256)

        def _mlp(x, gw, uw, dw):
            g = x @ gw.T
            u = x @ uw.T
            return g * jax.nn.sigmoid(g) * u @ dw.T
        Bsz, Seq, H = hidden_states.shape
        x = hidden_states.reshape(-1, H)
        logits = x.astype(jnp.float32) @ router_weight.astype(jnp.float32).T
        topk_vals, topk_idx = jax.lax.top_k(logits, TOP_K)
        topk_w = jax.nn.softmax(topk_vals, axis=-1)
        slot_mask = (topk_idx < NUM_LOCAL).astype(topk_w.dtype)
        comb_w = jnp.sum(topk_w * slot_mask, axis=-1).astype(x.dtype)
        shared = _mlp(x, sh_gate, sh_up, sh_down)
        routed = _mlp(x, r_gate, r_up, r_down) * comb_w[:, None]
        return (shared + routed).reshape(Bsz, Seq, H)

    def _L1_attn_ref(x, Wq, bq, Wk, bk, Wv, bv, Wo, bo):
        import jax, jax.numpy as jnp
        import numpy as np
        D_MODEL, H, G = (256, 32, 8)
        D_K = D_MODEL // H
        GROUP_SIZE = H // G
        B, S = (2, 256)
        Bsz, Sln, _ = x.shape
        Q = (x @ Wq + bq).reshape(Bsz, Sln, H, D_K).transpose(0, 2, 1, 3)
        K = (x @ Wk + bk).reshape(Bsz, Sln, G, D_K).transpose(0, 2, 1, 3)
        V = (x @ Wv + bv).reshape(Bsz, Sln, G, D_K).transpose(0, 2, 1, 3)
        Qg = Q.reshape(Bsz, G, GROUP_SIZE, Sln, D_K)
        scores = jnp.einsum('bgmqd,bgkd->bgmqk', Qg, K) / jnp.sqrt(jnp.float32(D_K))
        attn = jax.nn.softmax(scores, axis=-1)
        out = jnp.einsum('bgmqk,bgkd->bgmqd', attn, V)
        out = out.reshape(Bsz, H, Sln, D_K).transpose(0, 2, 1, 3).reshape(Bsz, Sln, D_MODEL)
        return out @ Wo + bo

    def _L1_xattn_ref(text_hidden, vision_tokens, vision_mask, Wq, Wk, Wv, Wo):
        import jax, jax.numpy as jnp
        import numpy as np
        N_HEADS = 16
        N_KV_HEADS = 8
        HEAD_DIM = 128
        D_TEXT = 256
        D_VISION = 128
        GROUPS = N_HEADS // N_KV_HEADS
        B, T_text, _ = text_hidden.shape
        T_vis = vision_tokens.shape[1]
        scale = jnp.float32(np.sqrt(HEAD_DIM))
        q = (text_hidden @ Wq).reshape(B, T_text, N_HEADS, HEAD_DIM).transpose(0, 2, 1, 3)
        k = (vision_tokens @ Wk).reshape(B, T_vis, N_KV_HEADS, HEAD_DIM).transpose(0, 2, 1, 3)
        v = (vision_tokens @ Wv).reshape(B, T_vis, N_KV_HEADS, HEAD_DIM).transpose(0, 2, 1, 3)
        k = jnp.repeat(k, GROUPS, axis=1)
        v = jnp.repeat(v, GROUPS, axis=1)
        scores = jnp.einsum('bhtd,bhsd->bhts', q, k) / scale
        mask = vision_mask[:, None, None, :]
        scores = jnp.where(mask, scores, -jnp.inf)
        attn = jax.nn.softmax(scores, axis=-1)
        attn = jnp.nan_to_num(attn, nan=0.0)
        out = jnp.einsum('bhts,bhsd->bhtd', attn, v)
        out = out.transpose(0, 2, 1, 3).reshape(B, T_text, N_HEADS * HEAD_DIM)
        return out @ Wo

    def _L1_ffn_ref(x, gate_w, up_w, down_w):
        import jax, jax.numpy as jnp
        import numpy as np
        _FP8_MAX = 448.0
        _BLOCK = 32
        _EPS = 1e-30

        def _mx_dequant(t):
            rows, feat = t.shape
            blocks = t.reshape(rows, feat // _BLOCK, _BLOCK)
            max_abs = jnp.max(jnp.abs(blocks), axis=-1)
            scales = jnp.maximum(max_abs / _FP8_MAX, _EPS)
            q = (blocks / scales[..., None]).astype(jnp.float8_e4m3fn).astype(jnp.float32)
            return (q * scales[..., None]).reshape(rows, feat)

        def _mx_linear(x2d, w):
            return _mx_dequant(x2d) @ _mx_dequant(w).T
        B, S, H = x.shape
        x2d = x.reshape(B * S, H)
        gate = _mx_linear(x2d, gate_w)
        up = _mx_linear(x2d, up_w)
        h = jax.nn.silu(gate) * up
        out = _mx_linear(h, down_w)
        return out.reshape(B, S, H)
    x = x + _L0_attn_ref(_layernorm(x, axis=-1), L0_attn_Wqkv, L0_attn_Wout)
    x = x + _L0_xattn_ref(_layernorm(x, axis=-1), ctx_1024, L0_xattn_Wq, L0_xattn_Wk, L0_xattn_Wv, L0_xattn_Wo, L0_xattn_gq, L0_xattn_gk)
    x = x + _L0_ffn_ref(_layernorm(x, axis=-1), L0_ffn_router_weight, L0_ffn_sh_gate, L0_ffn_sh_up, L0_ffn_sh_down, L0_ffn_r_gate, L0_ffn_r_up, L0_ffn_r_down)
    x = x + _L1_attn_ref(_layernorm(x, axis=-1), L1_attn_Wq, L1_attn_bq, L1_attn_Wk, L1_attn_bk, L1_attn_Wv, L1_attn_bv, L1_attn_Wo, L1_attn_bo)
    x = x + _L1_xattn_ref(_layernorm(x, axis=-1), ctx_1024, mask_BxS2_bf1, L1_xattn_Wq, L1_xattn_Wk, L1_xattn_Wv, L1_xattn_Wo)
    x = x + _L1_ffn_ref(_layernorm(x, axis=-1), L1_ffn_gate_w, L1_ffn_up_w, L1_ffn_down_w)
    return x

_drawn_inputs = setup_inputs


def setup_inputs(seed=0):
    import zlib

    import numpy as np

    out = dict(_drawn_inputs(seed))
    spreads = {'L0_xattn_gq': (1.0, 0.2), 'L0_xattn_gk': (1.0, 0.2)}
    factors = {'L0_ffn_router_weight': 64.0,
     'L0_ffn_r_gate': 5.89,
     'L0_ffn_r_up': 5.821,
     'L0_ffn_r_down': 5.836,
     'L1_attn_bq': 64.0,
     'L1_attn_bk': 64.0,
     'L1_attn_bv': 6.402,
     'L1_attn_bo': 7.492,
     'L1_xattn_Wq': 8.0,
     'L1_xattn_Wk': 8.0,
     'L0_ffn_sh_gate': 5.456,
     'L0_ffn_sh_up': 5.395,
     'L0_ffn_sh_down': 5.399,
     'L1_ffn_gate_w': 5.441,
     'L1_ffn_up_w': 5.386,
     'L1_ffn_down_w': 5.346}
    for name, (base, spread) in spreads.items():
        noise = np.random.default_rng([zlib.crc32(name.encode()), seed]).standard_normal(out[name].shape)
        drawn = base * np.exp(spread * noise) if base else spread * noise
        out[name] = jnp.asarray(drawn.astype(out[name].dtype))
    for name, factor in factors.items():
        out[name] = (out[name] * factor).astype(out[name].dtype)
    return out
```

```python
import numpy as np
import concourse.bass as bass
from concourse import mybir
from contextlib import ExitStack

F32 = mybir.dt.float32
BF16 = mybir.dt.bfloat16
ALU = mybir.AluOpType
ACT = mybir.ActivationFunctionType
AX = mybir.AxisListType

P = 128
BATCHES = 16
EMBED = 256
EC = EMBED // P
LN_EPS = 1e-5
NEG = -1e30


def nonneg(count):
    return max(count, 0) if isinstance(count, int) else count


class Chain:

    def __init__(self, engine, sem, per):
        self.engine, self.sem, self.per = engine, sem, per

    def start(self, batch):
        self.base, self.done = batch * self.per, 0

    def __call__(self, instruction):
        self.done += 1
        assert self.done <= self.per
        instruction.then_inc(self.sem, 1)
        self.engine.wait_ge(self.sem, self.base + self.done)


def pipeline(engine, step):
    step(0, 0, True, False, False)
    step(1, 1, True, True, False)
    step(2, 0, True, True, True)
    step(3, 1, True, True, True)
    with engine.Fori(4, BATCHES - 1, 2) as t:
        step(t, 0, True, True, True)
        step(t + 1, 1, True, True, True)
    step(BATCHES, 0, False, True, True)
    step(BATCHES + 1, 1, False, False, True)


SEMAPHORES = 44


class Core:

    def __init__(self, nc, ctx):
        self.nc, self.ctx = nc, ctx
        self.x = ctx.enter_context(nc.sbuf_tensor("x", [P, BATCHES * EMBED], F32))
        self.mean = ctx.enter_context(nc.sbuf_tensor("mean", [P, BATCHES], F32))
        self.variance = ctx.enter_context(nc.sbuf_tensor("variance", [P, BATCHES], F32))
        self.rstd = ctx.enter_context(nc.sbuf_tensor("rstd", [P, BATCHES], F32))
        self.minus_half = ctx.enter_context(nc.sbuf_tensor("minus_half", [P, BATCHES], F32))
        self.ident = ctx.enter_context(nc.sbuf_tensor("ident", [P, P], F32))
        self.ident_bf = ctx.enter_context(nc.sbuf_tensor("ident_bf", [P, P], BF16))
        self.minus_ident_bf = ctx.enter_context(nc.sbuf_tensor("minus_ident_bf", [P, P], BF16))
        self.ones_bf = ctx.enter_context(nc.sbuf_tensor("ones_bf", [P, P], BF16))
        self.ones = ctx.enter_context(nc.sbuf_tensor("ones", [P, P], F32))
        self.region = [ctx.enter_context(nc.sbuf_tensor("weights_even", [P, 10240], F32)),
                       ctx.enter_context(nc.sbuf_tensor("weights_odd", [P, 12288], F32))]
        self.banks = [ctx.enter_context(nc.psum_tensor(f"bank{n}", [P, 512], F32)) for n in range(8)]
        self.semaphores = [[ctx.enter_context(nc.semaphore(f"layer_{parity}_{k}")) for k in range(SEMAPHORES)]
                           for parity in ("even", "odd")]
        self.x_loaded = ctx.enter_context(nc.semaphore("x_loaded"))
        self.weights_loaded = [ctx.enter_context(nc.semaphore(f"weights_loaded_{n}")) for n in range(6)]

    def batch_x(self, b):
        return self.x[:, bass.ds(b * EMBED, EMBED)]

    def column(self, tensor, b):
        return tensor[:, bass.ds(b, 1)]


class Layer:

    def __init__(self, core, n, name, ctx):
        self.parity, self.used = n % 2, 0
        self.core, self.nc, self.name, self.ctx = core, core.nc, name, ctx
        self.h = self.sbuf("h", [P, EMBED], F32)
        self.hT = self.sbuf("hT", [P, EC, P], F32)
        self.new_x = self.sbuf("new_x", [P, EMBED], F32)
        self.stats = self.sbuf("stats", [P, 6], F32)
        self.mean_var = self.sbuf("mean_var", [P, 2], F32)
        self.variance_ready = self.sem("variance_ready")
        self.rstd_ready = self.sem("rstd_ready")
        self.h_ready = self.sem("h_ready")
        self.hT_filled = self.sem("hT_filled")
        self.hT_ready = self.sem("hT_ready")
        self.y_filled = self.sem("y_filled")
        self.x_updated = self.sem("x_updated")
        self.tail_chain = self.sem("tail_chain")

    def sbuf(self, name, shape, dtype=F32):
        return self.ctx.enter_context(self.nc.sbuf_tensor(f"{self.name}_{name}", shape, dtype))

    def sem(self, name):
        self.used += 1
        return self.core.semaphores[self.parity][self.used - 1]

    def clear_last_layers_semaphores(self, sp):
        last = [s.num for s in self.core.semaphores[1 - self.parity]]
        assert last == list(range(last[0], last[0] + SEMAPHORES))
        sp.sem_clear(range(last[0], last[0] + SEMAPHORES))

    def dve_norm_setup(self, dve):
        dve.tensor_scalar(self.core.variance[:, :], self.core.variance[:, :], LN_EPS, None, ALU.add)\
           .then_inc(self.variance_ready, 1)
        dve.wait_ge(self.rstd_ready, 1)

    def pool_rstd(self, pool):
        pool.wait_ge(self.variance_ready, 1)
        pool.tensor_tensor(self.core.rstd[:, :], self.core.variance[:, :], self.core.minus_half[:, :],
                           ALU.pow).then_inc(self.rstd_ready, 1)

    def dve_normalise(self, dve, b):
        dve.wait_ge(self.hT_filled, nonneg(b))
        dve.tensor_scalar(self.h[:, :], self.core.batch_x(b), self.core.column(self.core.mean, b),
                          self.core.column(self.core.rstd, b), ALU.subtract, ALU.mult)\
           .then_inc(self.h_ready, 1)

    def pe_transpose_h(self, pe, b, bank):
        pe.wait_ge(self.h_ready, b + 1)
        for c in range(EC):
            last = pe.transpose(bank[:, c * P:(c + 1) * P], self.h[:, c * P:(c + 1) * P],
                                self.core.ident[:, :])
        last.then_inc(self.hT_filled, 1)

    def act_copy_hT(self, act, b, bank):
        act.wait_ge(self.hT_filled, b + 1)
        act.activation(self.hT[:, :, :], bank[:, 0:EMBED].rearrange("p (c t) -> p c t", c=EC),
                       ACT.Copy).then_inc(self.hT_ready, 1)

    def dve_update_x(self, dve, b, y, chain, scale=None):
        dve.wait_ge(self.y_filled, b + 1)
        x = self.core.batch_x(b)
        if scale is None:
            update = dve.tensor_tensor(self.new_x[:, :], x, y, ALU.add)
        else:
            update = dve.scalar_tensor_tensor(self.new_x[:, :], y, scale, x, ALU.mult, ALU.add)
        update.then_inc(self.x_updated, 1)
        dve.wait_ge(self.x_updated, b + 1)
        self.dve_statistics(dve, b, chain)

    def dve_statistics(self, dve, b, chain):
        chain(dve.bn_stats(self.stats[:, :], self.new_x[:, :]))
        dve.tensor_scalar(self.core.batch_x(b), self.new_x[:, :], 1.0, None, ALU.mult)
        chain(dve.bn_aggr(self.mean_var[:, :], self.stats[:, :]))
        dve.tensor_scalar(self.core.column(self.core.mean, b), self.mean_var[:, 0:1], 1.0, None, ALU.mult)
        chain(dve.tensor_scalar(self.core.column(self.core.variance, b), self.mean_var[:, 1:2], 1.0,
                                None, ALU.mult))


STATISTICS_STEPS = 3


def setup(nc, core, x_dram, ident_dram, weights):
    with ExitStack() as ctx:
        layer = Layer(core, 1, "setup", ctx)
        ident_loaded = layer.sem("ident_loaded")
        made = layer.sem("made")
        block = ctx.enter_context(nc.Block())

        @block.sync
        def _(sp):
            sp.dma_start(core.ident[:, :], ident_dram).then_inc(ident_loaded, 16)
            sp.dma_start(core.x[:, :].rearrange("p (b e) -> p b e", b=BATCHES),
                         x_dram.rearrange("b p e -> p b e")).then_inc(core.x_loaded, 16)

        @block.gpsimd
        def _(pool):
            pool.memset(core.minus_half[:, :], -0.5)
            pool.memset(core.ones_bf[:, :], 1.0)
            pool.memset(core.ones[:, :], 1.0).then_inc(made, 1)

        @block.scalar
        def _(act):
            act.wait_ge(ident_loaded, 16)
            act.activation(core.ident_bf[:, :], core.ident[:, :], ACT.Copy)
            act.activation(core.minus_ident_bf[:, :], core.ident[:, :], ACT.Copy, scale=-1.0).then_inc(made, 1)

        @block.vector
        def _(dve):
            dve.wait_ge(core.x_loaded, 16)
            chain = Chain(dve, layer.tail_chain, STATISTICS_STEPS + 1)
            with dve.Fori(0, BATCHES, 1) as b:
                chain.start(b)
                chain(dve.tensor_scalar(layer.new_x[:, :], core.batch_x(b), 1.0, None, ALU.mult))
                layer.dve_statistics(dve, b, chain)


def load_weights(sp, core, n, dram, parts=2):
    columns = dram.shape[1]
    for k in range(parts):
        a, e = columns * k // parts, columns * (k + 1) // parts
        sp.dma_start(core.region[n % 2][:, a:e], dram[:, a:e], max_dma_last_dim=8192)\
          .then_inc(core.weights_loaded[n], 16)
    return parts


WEIGHT_PARTS = 2


def causal_attention(nc, core, dram, weights, next_weights):
    HEADS, D = 16, 16
    GROUPS = 4
    PER = HEADS // GROUPS
    SCALE = float(D) ** -0.5
    VW = D + 1
    n = 0
    with ExitStack() as ctx:
        layer = Layer(core, n, "causal", ctx)
        sem, sbuf = layer.sem, layer.sbuf
        region = core.region[n]
        w = region[:, 0:6 * EC * EMBED].rearrange("p (k c n) -> p k c n", k=6, c=EC)
        wq, wq_swapped, wk, wk_swapped, wv, wo = (w[:, k] for k in range(6))
        cosine, sine = sbuf("cosine", [P, EC * P]), sbuf("sine", [P, EC * P])
        later, earlier = sbuf("later", [P, P]), sbuf("earlier", [P, P])
        own = sbuf("own", [P, P // D])
        parity = sbuf("parity", [P, 2])
        mask_qk = sbuf("mask_qk", [P, PER, P], BF16)
        mask_kq = sbuf("mask_kq", [P, PER, P], BF16)
        q_cos, q_sin = sbuf("q_cos", [P, EC * P]), sbuf("q_sin", [P, EC * P])
        k_cos, k_sin = sbuf("k_cos", [P, EC * P]), sbuf("k_sin", [P, EC * P])
        qT = [sbuf(f"qT{s}", [P, EC, P]) for s in range(2)]
        qT_bf = [sbuf(f"qT_bf{s}", [P, EC, P], BF16) for s in range(2)]
        q_own = [sbuf(f"q_own{s}", [P, EC, P // D, P]) for s in range(2)]
        kT = [sbuf(f"kT{s}", [P, EC, P]) for s in range(2)]
        kT_bf = [sbuf(f"kT_bf{s}", [P, EC, 2, P], BF16) for s in range(2)]
        values = [sbuf(f"values{s}", [P, HEADS, VW]) for s in range(2)]
        maxima = [sbuf(f"maxima{s}", [P, GROUPS, PER], BF16) for s in range(2)]
        probs = sbuf("probs", [P, GROUPS, PER * P])
        reciprocal = sbuf("reciprocal", [P, HEADS])
        heads = sbuf("heads", [P, HEADS, D])
        headsT = sbuf("headsT", [P, EC, P])

        bank_hv, bank_q, bank_k = core.banks[0:3]
        bank_scores, bank_scoresT, bank_out = core.banks[3:5], core.banks[5:7], core.banks[7]
        half_tail = bank_hv[:, EMBED:2 * EMBED]

        constants_loaded = sem("constants_loaded")
        constants_ready = sem("constants_ready")
        q_filled, q_read = sem("q_filled"), sem("q_read")
        k_filled, k_read = sem("k_filled"), sem("k_read")
        q_ready = sem("q_ready")
        q_own_ready = sem("q_own_ready")
        k_ready, k_bf_ready = sem("k_ready"), sem("k_bf_ready")
        v_filled, v_ready = sem("v_filled"), sem("v_ready")
        scores_filled, max_ready = sem("scores_filled"), sem("max_ready")
        scoresT_filled, probs_ready = sem("scoresT_filled"), sem("probs_ready")
        out_filled = sem("out_filled")
        heads_ready, headsT_filled, headsT_ready = sem("heads_ready"), sem("headsT_filled"), sem("headsT_ready")
        heads_chain = sem("heads_chain")
        block = ctx.enter_context(nc.Block())

        @block.sync
        def _(sp):
            layer.clear_last_layers_semaphores(sp)
            sp.dma_start(cosine[:, :], dram["cosine"]).then_inc(constants_loaded, 16)
            sp.dma_start(sine[:, :], dram["sine"]).then_inc(constants_loaded, 16)
            sp.dma_start(later[:, :], dram["later"]).then_inc(constants_loaded, 16)
            sp.dma_start(earlier[:, :], dram["earlier"]).then_inc(constants_loaded, 16)
            sp.dma_start(own[:, :], dram["causal_own"]).then_inc(constants_loaded, 16)
            sp.dma_start(parity[:, :], dram["parity"]).then_inc(constants_loaded, 16)
            load_weights(sp, core, n, weights)
            load_weights(sp, core, n + 1, next_weights)

        @block.gpsimd
        def _(pool):
            for s in range(2):
                pool.memset(values[s][:, :, D:VW], 1.0)
            pool.wait_ge(constants_loaded, 6 * 16)
            for g in range(PER):
                pool.tensor_copy(mask_qk[:, g, :], later[:, :])
                last = pool.tensor_copy(mask_kq[:, g, :], earlier[:, :])
            last.then_inc(constants_ready, 1)
            layer.pool_rstd(pool)

            def step(t, s, front, middle, tail):
                if front:
                    b = t
                    pool.wait_ge(q_read, b + 1)
                    pool.wait_ge(scoresT_filled, nonneg(GROUPS * (b - 1)))
                    pool.tensor_tensor(qT[s][:, :, :], q_cos[:, :], q_sin[:, :], ALU.add)
                    pool.tensor_tensor(qT_bf[s][:, :, :], q_cos[:, :], q_sin[:, :], ALU.add)\
                        .then_inc(q_ready, 1)
                    pool.wait_ge(k_read, b + 1)
                    pool.tensor_tensor(kT[s][:, :, :], k_cos[:, :], k_sin[:, :], ALU.add).then_inc(k_ready, 1)
                    pool.wait_ge(k_ready, b + 1)
                    for h in range(2):
                        last = pool.tensor_tensor(kT_bf[s][:, :, h, :], kT[s][:, :, :],
                                                  parity[:, h:h + 1].unsqueeze(2).to_broadcast([P, EC, P]), ALU.mult)
                    last.then_inc(k_bf_ready, 1)
            pipeline(pool, step)

        @block.scalar
        def _(act):
            act.wait_ge(constants_loaded, 6 * 16)

            def step(t, s, front, middle, tail):
                if front:
                    act.wait_ge(v_filled, nonneg(t))
                    layer.act_copy_hT(act, t, bank_hv)

                def exponentials(g):
                    i = GROUPS * (t - 1) + g
                    act.wait_ge(scoresT_filled, i + 1)
                    act.wait_ge(out_filled, nonneg(i - GROUPS + 1))
                    act.activation(probs[:, g, :], bank_scoresT[g % 2][:, :], ACT.Exp, scale=SCALE)\
                       .then_inc(probs_ready, 1)
                if middle:
                    exponentials(0)
                    exponentials(1)
                if tail:
                    b = t - 2
                    act.wait_ge(headsT_filled, b + 1)
                    act.wait_ge(layer.y_filled, nonneg(b))
                    act.activation(headsT[:, :, :], half_tail.rearrange("p (c t) -> p c t", c=EC),
                                   ACT.Copy).then_inc(headsT_ready, 1)
                if front:
                    b = t
                    act.wait_ge(q_ready, b + 1)
                    act.wait_ge(scoresT_filled, nonneg(GROUPS * (b - 1)))
                    for h in range(P // D // 2):
                        act.activation(q_own[s][:, :, h, :], qT[s][:, :, :], ACT.Copy, scale=own[:, h:h + 1])
                if middle:
                    exponentials(2)
                if front:
                    for h in range(P // D // 2, P // D):
                        last = act.activation(q_own[s][:, :, h, :], qT[s][:, :, :], ACT.Copy, scale=own[:, h:h + 1])
                    last.then_inc(q_own_ready, 1)
                if middle:
                    exponentials(3)
                if front:
                    b = t
                    act.wait_ge(v_filled, b + 1)
                    act.wait_ge(out_filled, nonneg(GROUPS * (b - 1)))
                    act.activation(values[s][:, :, 0:D], bank_hv[:, 0:EMBED].rearrange("p (h d) -> p h d", h=HEADS),
                                   ACT.Copy).then_inc(v_ready, 1)
            pipeline(act, step)

        @block.vector
        def _(dve):
            layer.dve_norm_setup(dve)
            dve.wait_ge(constants_loaded, 6 * 16)
            heads_step = Chain(dve, heads_chain, 1)
            tail_step = Chain(dve, layer.tail_chain, STATISTICS_STEPS)

            def step(t, s, front, middle, tail):
                if front:
                    layer.dve_normalise(dve, t)

                def row_maxima(g):
                    i = GROUPS * (t - 1) + g
                    dve.wait_ge(scores_filled, i + 1)
                    dve.wait_ge(scoresT_filled, nonneg(GROUPS * (t - 2)))
                    dve.tensor_reduce(maxima[1 - s][:, g, :], bank_scores[g % 2].rearrange("p (h k) -> p h k", h=PER),
                                      AX.X, ALU.max).then_inc(max_ready, 1)

                def turn(bank, filled, used, with_cos, with_sin, read):
                    dve.wait_ge(filled, t + 1)
                    dve.wait_ge(used, nonneg(t))
                    dve.tensor_tensor(with_cos[:, :], bank[:, 0:EC * P], cosine[:, :], ALU.mult)
                    dve.tensor_tensor(with_sin[:, :], bank[:, EC * P:2 * EC * P], sine[:, :], ALU.mult)\
                       .then_inc(read, 1)
                if middle:
                    row_maxima(0)
                    row_maxima(1)
                if tail:
                    b = t - 2
                    heads_step.start(b)
                    dve.wait_ge(out_filled, GROUPS * (b + 1))
                    out = bank_out[:, 0:HEADS * VW].rearrange("p (h d) -> p h d", h=HEADS)
                    heads_step(dve.reciprocal(reciprocal[:, :].unsqueeze(2), out[:, :, D:VW]))
                    dve.wait_ge(headsT_filled, nonneg(b))
                    dve.tensor_tensor(heads[:, :, :], out[:, :, 0:D],
                                      reciprocal[:, :].unsqueeze(2).to_broadcast([P, HEADS, D]), ALU.mult)\
                       .then_inc(heads_ready, 1)
                if middle:
                    row_maxima(2)
                if front:
                    turn(bank_q, q_filled, q_ready, q_cos, q_sin, q_read)
                if middle:
                    row_maxima(3)
                if front:
                    turn(bank_k, k_filled, k_ready, k_cos, k_sin, k_read)
                if tail:
                    tail_step.start(t - 2)
                    layer.dve_update_x(dve, t - 2, half_tail, tail_step)
            pipeline(dve, step)

        @block.tensor
        def _(pe):
            pe.wait_ge(core.weights_loaded[n], 16 * WEIGHT_PARTS)
            pe.wait_ge(constants_ready, 1)

            def step(t, s, front, middle, tail):
                def scores(g):
                    i = GROUPS * (t - 1) + g
                    pe.wait_ge(max_ready, nonneg(i - 1))
                    rows = slice(32 * g, 32 * g + 32)
                    pe.matmul(bank_scores[g % 2][:, :], core.ident_bf[:, :], mask_qk[:, :, :],
                              start=True, stop=False)
                    for c in range(EC):
                        last = pe.matmul(bank_scores[g % 2][:, 2 * c * P:2 * (c + 1) * P], qT_bf[1 - s][rows, c, :],
                                         kT_bf[1 - s][rows, c, :, :], start=False, stop=(c == EC - 1))
                    last.then_inc(scores_filled, 1)

                def scores_transposed(g):
                    i = GROUPS * (t - 1) + g
                    pe.wait_ge(max_ready, i + 1)
                    pe.wait_ge(probs_ready, nonneg(i - 1))
                    bank = bank_scoresT[g % 2]
                    pe.matmul(bank[:, :], core.ident_bf[:, :], mask_kq[:, :, :], start=True, stop=False)
                    for j in range(PER):
                        pe.matmul(bank[:, j * P:(j + 1) * P], maxima[1 - s][:, g, j:j + 1].to_broadcast([P, P]),
                                  core.minus_ident_bf[:, :], start=False, stop=False)
                    for c in range(EC):
                        last = pe.matmul(bank[:, 2 * c * P:2 * (c + 1) * P], kT[1 - s][:, c, :],
                                         q_own[1 - s][:, c, 2 * g:2 * (g + 1), :], start=False, stop=(c == EC - 1))
                    last.then_inc(scoresT_filled, 1)

                def weigh_values(g, b=t - 1, s=1 - s):
                    i = GROUPS * b + g
                    pe.wait_ge(probs_ready, i + 1)
                    for j in range(PER):
                        h = (j // 2 * GROUPS + g) * 2 + j % 2
                        last = pe.matmul(bank_out[:, h * VW:(h + 1) * VW], probs[:, g, j * P:(j + 1) * P],
                                         values[s][:, h, :], start=True, stop=True)
                    last.then_inc(out_filled, 1)

                def project(bank, weights):
                    for k, wt in enumerate(weights):
                        for m in range(EC):
                            at = (k * EC + m) * P
                            for c in range(EC):
                                last = pe.matmul(bank[:, at:at + P], wt[:, c, m * P:(m + 1) * P], layer.hT[:, c, :],
                                                 start=(c == 0), stop=(c == EC - 1))
                    return last

                if middle:
                    pe.wait_ge(q_ready, nonneg(t))
                    pe.wait_ge(k_bf_ready, nonneg(t))
                    scores(0)
                    scores(1)
                if tail:
                    weigh_values(3, t - 2, s)
                if front:
                    pe.wait_ge(v_ready, nonneg(t))
                    layer.pe_transpose_h(pe, t, bank_hv)
                if middle:
                    pe.wait_ge(q_own_ready, nonneg(t))
                    scores_transposed(0)
                    scores(2)
                if front:
                    pe.wait_ge(layer.hT_ready, t + 1)
                    pe.wait_ge(q_read, nonneg(t))
                    project(bank_q, (wq, wq_swapped)).then_inc(q_filled, 1)
                if middle:
                    scores_transposed(1)
                    scores(3)
                    pe.wait_ge(v_ready, nonneg(t))
                if tail:
                    pe.wait_ge(heads_ready, nonneg(t - 1))
                    pe.wait_ge(layer.x_updated, nonneg(t - 2))
                    flat = heads[:, :, :].rearrange("p h d -> p (h d)")
                    for c in range(EC):
                        last = pe.transpose(half_tail[:, c * P:(c + 1) * P], flat[:, c * P:(c + 1) * P],
                                            core.ident[:, :])
                    last.then_inc(headsT_filled, 1)
                if middle:
                    pe.wait_ge(heads_ready, nonneg(t - 1))
                    weigh_values(0)
                if front:
                    pe.wait_ge(k_read, nonneg(t))
                    project(bank_k, (wk, wk_swapped)).then_inc(k_filled, 1)
                if middle:
                    scores_transposed(2)
                    weigh_values(1)
                if tail:
                    pe.wait_ge(headsT_ready, nonneg(t - 1))
                    for c in range(EC):
                        last = pe.matmul(half_tail, headsT[:, c, :], wo[:, c, :],
                                         start=(c == 0), stop=(c == EC - 1))
                    last.then_inc(layer.y_filled, 1)
                if middle:
                    scores_transposed(3)
                    weigh_values(2)
                if front:
                    pe.wait_ge(layer.x_updated, nonneg(t - 1))
                    for c in range(EC):
                        last = pe.matmul(bank_hv[:, 0:EMBED], layer.hT[:, c, :], wv[:, c, :],
                                         start=(c == 0), stop=(c == EC - 1))
                    last.then_inc(v_filled, 1)
            pipeline(pe, step)


def cross_attention(nc, core, n, dram, next_weights, normed):
    HEADS, D = 16, P
    KV_HEADS = HEADS if normed else HEADS // 2
    SHARE = HEADS // KV_HEADS
    GROUPS = 4
    PER = HEADS // GROUPS
    KV_GROUPS = KV_HEADS // PER
    VW = D + 1
    SCALE = float(D) ** -0.5
    RMS_EPS = 1e-5
    LEAST_SUM = 1e-30
    with ExitStack() as ctx:
        layer = Layer(core, n, f"cross{n}", ctx)
        sem, sbuf = layer.sem, layer.sbuf
        region = core.region[n % 2]
        at = 0

        def weight(columns, pattern=None, **sizes):
            nonlocal at
            part = region[:, at:at + columns]
            at += columns
            return part.rearrange(pattern, **sizes) if pattern else part
        wq = weight(EC * HEADS * D, "p (c n) -> p c n", c=EC)
        wk = weight(KV_HEADS * D)
        wv = weight(KV_HEADS * D)
        wo = weight(HEADS * EMBED, "p (h n) -> p h n", h=HEADS)

        context = [sbuf(f"context{s}", [P, P]) for s in range(2)]
        contextT = sbuf("contextT", [P, P])
        qT, qT_bf = sbuf("qT", [P, HEADS, P]), sbuf("qT_bf", [P, HEADS, P], BF16)
        kT, kT_bf = sbuf("kT", [P, KV_HEADS, P]), sbuf("kT_bf", [P, KV_HEADS, P], BF16)
        values = sbuf("values", [P, KV_HEADS, VW])
        maxima = [sbuf(f"maxima{s}", [P, HEADS], BF16) for s in range(2)]
        probs = sbuf("probs", [P, HEADS, P])
        sums = sbuf("sums", [P, HEADS])
        reciprocal = sbuf("reciprocal", [P, HEADS])
        heads = [sbuf(f"heads{s}", [P, PER, D]) for s in range(2)]
        headsT = sbuf("headsT", [P, HEADS, P])
        if normed:
            q_scaled, k_scaled = sbuf("q_scaled", [P, PER, D]), sbuf("k_scaled", [P, PER, D])
            squares = [sbuf(f"squares_{x}", [P, PER, D], BF16) for x in "qk"]
            mean_q, mean_k = sbuf("mean_q", [P, HEADS]), sbuf("mean_k", [P, HEADS])
            mean_eps = [sbuf(f"mean_eps_{x}", [P, HEADS]) for x in "qk"]
            rms_q, rms_k = sbuf("rms_q", [P, HEADS]), sbuf("rms_k", [P, HEADS])
            eps = sbuf("eps", [P, PER])
            gains = sbuf("gains", [P, 2])
            gain = sbuf("gain", [P, 1])
        else:
            mask = sbuf("mask", [P, BATCHES], mybir.dt.uint8)
            key_bias = sbuf("key_bias", [P, BATCHES])
            batch_bias = [sbuf(f"batch_bias{s}", [P, 1]) for s in range(2)]
            mask_diagonal = [sbuf(f"mask_diagonal{s}", [P, P], BF16) for s in range(2)]

        bank_project, bank_turn, bank_scores, bank_scoresT = core.banks[0:2], core.banks[2], core.banks[3], core.banks[4]
        bank_out, bank_y = core.banks[5:7], core.banks[7]

        context_loaded = [sem(f"context_loaded{s}") for s in range(2)]
        small_loaded, small_ready = sem("small_loaded"), sem("small_ready")
        q_filled, k_filled, v_filled = sem("q_filled"), sem("k_filled"), sem("v_filled")
        q_summed, k_summed = sem("q_summed"), sem("k_summed")
        rms_q_ready, rms_k_ready = sem("rms_q_ready"), sem("rms_k_ready")
        q_read, k_read, v_ready = sem("q_read"), sem("k_read"), sem("v_ready")
        qT_filled, kT_filled = sem("qT_filled"), sem("kT_filled")
        qT_ready, kT_ready = sem("qT_ready"), sem("kT_ready")
        qT_bf_ready, kT_bf_ready = sem("qT_bf_ready"), sem("kT_bf_ready")
        scores_filled, max_ready = sem("scores_filled"), sem("max_ready")
        scoresT_filled, probs_ready = sem("scoresT_filled"), sem("probs_ready")
        out_filled = sem("out_filled")
        heads_ready, headsT_filled, headsT_ready = sem("heads_ready"), sem("headsT_filled"), sem("headsT_ready")
        middle_chain, pool_chain, mask_ready = sem("middle_chain"), sem("pool_chain"), sem("mask_ready")
        block = ctx.enter_context(nc.Block())

        @block.sync
        def _(sp):
            layer.clear_last_layers_semaphores(sp)
            if normed:
                sp.dma_start(gains[:, :], dram["gains"]).then_inc(small_loaded, 16)
            else:
                sp.dma_start(mask[:, :], dram["mask"]).then_inc(small_loaded, 16)

            def step(t, s, front, middle, tail):
                if front:
                    sp.wait_ge(layer.hT_filled, nonneg(t - 1))
                    sp.dma_start(context[s][:, :], dram["context"][bass.ds(t, 1), :, :].rearrange("b p c -> (b p) c"))\
                      .then_inc(context_loaded[s], 16)
            step(0, 0, True, False, False)
            step(1, 1, True, False, False)
            if next_weights is not None:
                load_weights(sp, core, n + 1, next_weights)
            with sp.Fori(2, BATCHES - 1, 2) as t:
                step(t, 0, True, False, False)
                step(t + 1, 1, True, False, False)

        @block.gpsimd
        def _(pool):
            pool.memset(values[:, :, D:VW], 1.0)
            if normed:
                pool.memset(eps[:, :], RMS_EPS)
                pool.wait_ge(small_loaded, 16)
                pool.tensor_tensor(gain[:, :], gains[:, 0:1], gains[:, 1:2], ALU.mult).then_inc(small_ready, 1)
            else:
                pool.memset(reciprocal[:, :], 0.0).then_inc(small_ready, 1)
            layer.pool_rstd(pool)
            eps_added = Chain(pool, pool_chain, 2 * GROUPS) if normed else None

            def step(t, s, front, middle, tail):
                if not front:
                    return
                b = t

                def rms(summed, mean, mean_eps, out, ready, g):
                    cols = slice(g * PER, (g + 1) * PER)
                    pool.wait_ge(summed, GROUPS * b + g + 1)
                    pool.wait_ge(q_read, nonneg(GROUPS * (b - 1) + g + 1))
                    pool.wait_ge(k_read, nonneg(GROUPS * (b - 1) + g + 1))
                    eps_added(pool.tensor_tensor(mean_eps[:, cols], mean[:, cols], eps[:, :], ALU.add))
                    pool.tensor_tensor(out[:, cols], mean_eps[:, cols], core.minus_half[:, 0:PER], ALU.pow)\
                        .then_inc(ready, 1)

                def narrow(source, ready, to, done, g, groups):
                    pool.wait_ge(ready, groups * b + g + 1)
                    pool.wait_ge(scores_filled, nonneg(GROUPS * (b - 1) + (g + 1) * (GROUPS // groups)))
                    pool.tensor_tensor(to[:, g * PER:(g + 1) * PER, :], source[:, g * PER:(g + 1) * PER, :],
                                       core.ones[:, 0:1].unsqueeze(2).to_broadcast([P, PER, P]), ALU.mult)\
                        .then_inc(done, 1)
                if normed:
                    eps_added.start(b)
                for g in range(GROUPS):
                    if normed:
                        rms(q_summed, mean_q, mean_eps[0], rms_q, rms_q_ready, g)
                        if g:
                            narrow(qT, qT_ready, qT_bf, qT_bf_ready, g - 1, GROUPS)
                            narrow(kT, kT_ready, kT_bf, kT_bf_ready, g - 1, GROUPS)
                        rms(k_summed, mean_k, mean_eps[1], rms_k, rms_k_ready, g)
                    else:
                        narrow(qT, qT_ready, qT_bf, qT_bf_ready, g, GROUPS)
                        if g % 2:
                            narrow(kT, kT_ready, kT_bf, kT_bf_ready, g // 2, KV_GROUPS)
                if normed:
                    narrow(qT, qT_ready, qT_bf, qT_bf_ready, GROUPS - 1, GROUPS)
                    narrow(kT, kT_ready, kT_bf, kT_bf_ready, GROUPS - 1, GROUPS)
            pipeline(pool, step)

        @block.scalar
        def _(act):
            act.wait_ge(small_ready, 1)

            def step(t, s, front, middle, tail):
                def heads_to_sbuf(b, g):
                    act.wait_ge(headsT_filled, GROUPS * b + g + 1)
                    if g == 0:
                        act.wait_ge(layer.y_filled, nonneg(b))
                    act.activation(headsT[:, g * PER:(g + 1) * PER, :], bank_turn.rearrange("p (h q) -> p h q", h=PER),
                                   ACT.Copy).then_inc(headsT_ready, 1)

                def exponentials(g):
                    i = GROUPS * (t - 1) + g
                    act.wait_ge(scoresT_filled, i + 1)
                    act.wait_ge(out_filled, nonneg(i - GROUPS + 1))
                    act.activation(probs[:, g * PER:(g + 1) * PER, :], bank_scoresT.rearrange("p (h q) -> p h q", h=PER),
                                   ACT.Exp, scale=SCALE, bias=0.0 if normed else batch_bias[1 - s][:, 0:1])\
                       .then_inc(probs_ready, 1)

                def mean_squares(filled, bank, squares, mean, summed, used, g):
                    i = GROUPS * t + g
                    act.wait_ge(filled, i + 1)
                    act.wait_ge(used, nonneg(i - GROUPS + 1))
                    act.wait_ge(summed, nonneg(i))
                    for j in range(PER):
                        last = act.activation(squares[:, j, :], bank[:, j * P:(j + 1) * P], ACT.Square,
                                              scale=float(D) ** -0.5,
                                              accum_out=mean[:, g * PER + j:g * PER + j + 1])
                    last.then_inc(summed, 1)

                def to_sbuf(filled, bank, to, ready, b, g, groups, scale=1.0):
                    act.wait_ge(filled, groups * b + g + 1)
                    act.wait_ge(scoresT_filled, nonneg(GROUPS * (b - 1) + (g + 1) * (GROUPS // groups)))
                    act.wait_ge(qT_bf_ready if to is qT else kT_bf_ready, nonneg(groups * (b - 1) + g + 1))
                    act.activation(to[:, g * PER:(g + 1) * PER, :], bank.rearrange("p (h q) -> p h q", h=PER),
                                   ACT.Copy, scale=scale).then_inc(ready, 1)

                def values_to_sbuf(g):
                    act.wait_ge(v_filled, KV_GROUPS * t + g + 1)
                    act.wait_ge(out_filled, nonneg(GROUPS * (t - 1) + (g + 1) * SHARE))
                    act.activation(values[:, g * PER:(g + 1) * PER, 0:D],
                                   bank_y.rearrange("p (h d) -> p h d", h=PER), ACT.Copy)\
                       .then_inc(v_ready, 1)

                if middle and normed:
                    to_sbuf(qT_filled, bank_turn, qT, qT_ready, t - 1, GROUPS - 1, GROUPS)
                if tail:
                    heads_to_sbuf(t - 2, GROUPS - 1)
                if middle and normed:
                    to_sbuf(kT_filled, bank_turn, kT, kT_ready, t - 1, GROUPS - 1, GROUPS, gain[:, 0:1])
                if front:
                    act.wait_ge(layer.hT_filled, t + 1)
                    act.wait_ge(v_filled, nonneg(KV_GROUPS * t))
                    act.activation(contextT[:, :], bank_turn[:, EMBED:EMBED + P], ACT.Copy)
                    act.activation(layer.hT[:, :, :], bank_turn[:, 0:EMBED].rearrange("p (c t) -> p c t", c=EC),
                                   ACT.Copy).then_inc(layer.hT_ready, 1)
                if middle:
                    exponentials(0)
                for g in range(GROUPS):
                    if front and normed:
                        if g:
                            to_sbuf(qT_filled, bank_turn, qT, qT_ready, t, g - 1, GROUPS)
                        mean_squares(q_filled, bank_project[0], squares[0], mean_q, q_summed, rms_q_ready, g)
                    if front and not normed:
                        to_sbuf(q_filled, bank_project[0], qT, qT_ready, t, g, GROUPS)
                    if middle and g < GROUPS - 1:
                        exponentials(g + 1)
                    if front and normed:
                        if g:
                            to_sbuf(kT_filled, bank_turn, kT, kT_ready, t, g - 1, GROUPS, gain[:, 0:1])
                        mean_squares(k_filled, bank_project[1], squares[1], mean_k, k_summed, rms_k_ready, g)
                    if front and not normed and g % 2:
                        to_sbuf(k_filled, bank_project[1], kT, kT_ready, t, g // 2, KV_GROUPS)
                    if middle and g:
                        heads_to_sbuf(t - 1, g - 1)
                    if front and (g + 1) % SHARE == 0:
                        values_to_sbuf(g // SHARE)
            pipeline(act, step)

        @block.vector
        def _(dve):
            if not normed:
                dve.wait_ge(small_loaded, 16)
                dve.tensor_scalar(key_bias[:, :], mask[:, :], 1.0, -NEG, ALU.subtract, ALU.mult)\
                   .then_inc(mask_ready, 1)
                dve.wait_ge(mask_ready, 1)
            layer.dve_norm_setup(dve)
            STEPS = 2 * GROUPS
            middle_step = Chain(dve, middle_chain, STEPS)
            tail_step = Chain(dve, layer.tail_chain, STATISTICS_STEPS)

            def step(t, s, front, middle, tail):
                def row_maxima(g):
                    i = GROUPS * (t - 1) + g
                    dve.wait_ge(scores_filled, i + 1)
                    dve.wait_ge(scoresT_filled, nonneg(GROUPS * (t - 2)))
                    with nc.allow_low_precision("the maximum only shifts a softmax's exponents"):
                        dve.tensor_reduce(maxima[1 - s][:, g * PER:(g + 1) * PER],
                                          bank_scores.rearrange("p (h k) -> p h k", h=PER),
                                          AX.X, ALU.max).then_inc(max_ready, 1)

                def scale_rows(ready, rms, filled, out, read, bank, g):
                    i = GROUPS * t + g
                    dve.wait_ge(ready, i + 1)
                    dve.wait_ge(filled, nonneg(i))
                    dve.tensor_tensor(out[:, :, :], bank.rearrange("p (h d) -> p h d", h=PER),
                                      rms[:, g * PER:(g + 1) * PER].unsqueeze(2).to_broadcast([P, PER, D]),
                                      ALU.mult).then_inc(read, 1)

                def normalise_heads(g):
                    i = GROUPS * (t - 1) + g
                    dve.wait_ge(out_filled, i + 1)
                    for j in range(2):
                        out = bank_out[j][:, 0:2 * VW].rearrange("p (h d) -> p h d", h=2)
                        last = dve.tensor_scalar(sums[:, g * PER + 2 * j:g * PER + 2 * j + 2].unsqueeze(2),
                                                 out[:, :, D:VW], LEAST_SUM, None, ALU.max)
                    middle_step(last)
                    middle_step(dve.reciprocal(reciprocal[:, g * PER:(g + 1) * PER],
                                               sums[:, g * PER:(g + 1) * PER]))
                    dve.wait_ge(headsT_filled, nonneg(i - 1))
                    for j in range(2):
                        out = bank_out[j][:, 0:2 * VW].rearrange("p (h d) -> p h d", h=2)
                        a = g * PER + 2 * j
                        last = dve.tensor_tensor(heads[g % 2][:, 2 * j:2 * j + 2, :], out[:, :, 0:D],
                                                 reciprocal[:, a:a + 2].unsqueeze(2).to_broadcast([P, 2, D]),
                                                 ALU.mult)
                    last.then_inc(heads_ready, 1)

                if middle:
                    middle_step.start(t - 1)
                if front:
                    layer.dve_normalise(dve, t)
                    if not normed:
                        dve.wait_ge(scoresT_filled, nonneg(GROUPS * (t - 1)))
                        dve.wait_ge(probs_ready, nonneg(GROUPS * (t - 1)))
                        dve.tensor_scalar(batch_bias[s][:, :], core.column(key_bias, t), 1.0, None, ALU.mult)
                        dve.tensor_scalar(mask_diagonal[s][:, :], core.ident[:, :], core.column(key_bias, t), None,
                                          ALU.mult).then_inc(mask_ready, 1)
                if middle:
                    row_maxima(0)
                    row_maxima(1)
                if tail:
                    tail_step.start(t - 2)
                    layer.dve_update_x(dve, t - 2, bank_y[:, 0:EMBED], tail_step)
                for g in range(GROUPS):
                    if front and normed:
                        scale_rows(rms_q_ready, rms_q, qT_filled, q_scaled, q_read, bank_project[0], g)
                    if middle:
                        normalise_heads(g)
                        if g + 2 < GROUPS:
                            row_maxima(g + 2)
                    if front and normed:
                        scale_rows(rms_k_ready, rms_k, kT_filled, k_scaled, k_read, bank_project[1], g)
            pipeline(dve, step)

        @block.tensor
        def _(pe):
            pe.wait_ge(core.weights_loaded[n], 16 * WEIGHT_PARTS)
            pe.wait_ge(small_ready, 1)
            q_done, k_done = (q_read, k_read) if normed else (qT_ready, kT_ready)

            def step(t, s, front, middle, tail):
                if normed and isinstance(t, int) and t == 1:
                    turned = (kT_ready, GROUPS - 1)
                else:
                    turned = (headsT_ready, GROUPS * (t - 2) + GROUPS - 1)

                def turn(sources, filled, ready, count):
                    nonlocal turned
                    pe.wait_ge(turned[0], nonneg(turned[1]))
                    for j, source in enumerate(sources):
                        last = pe.transpose(bank_turn[:, j * P:(j + 1) * P], source, core.ident[:, :])
                    last.then_inc(filled, 1)
                    turned = (ready, count)

                def scores(g):
                    i = GROUPS * (t - 1) + g
                    pe.wait_ge(max_ready, nonneg(i))
                    pe.wait_ge(qT_bf_ready, nonneg(i + 1))
                    pe.wait_ge(kT_bf_ready, nonneg(KV_GROUPS * (t - 1) + g // SHARE + 1))
                    if not normed:
                        if g == 0:
                            pe.wait_ge(mask_ready, t + 1)
                        pe.matmul(bank_scores[:, :], core.ones_bf[:, :],
                                  mask_diagonal[1 - s][:, :].unsqueeze(1).to_broadcast([P, PER, P]),
                                  start=True, stop=False)
                    for j in range(PER):
                        h = g * PER + j
                        last = pe.matmul(bank_scores[:, j * P:(j + 1) * P], qT_bf[:, h, :], kT_bf[:, h // SHARE, :],
                                         start=(normed and j == 0), stop=(j == PER - 1), skip_group_check=normed)
                    last.then_inc(scores_filled, 1)

                def scores_transposed(g):
                    i = GROUPS * (t - 1) + g
                    pe.wait_ge(max_ready, i + 1)
                    pe.wait_ge(probs_ready, nonneg(i))
                    for j in range(PER):
                        h = g * PER + j
                        pe.matmul(bank_scoresT[:, j * P:(j + 1) * P], maxima[1 - s][:, h:h + 1].to_broadcast([P, P]),
                                  core.minus_ident_bf[:, :], start=(j == 0), stop=False, skip_group_check=True)
                    for j in range(PER):
                        h = g * PER + j
                        last = pe.matmul(bank_scoresT[:, j * P:(j + 1) * P], kT[:, h // SHARE, :], qT[:, h, :],
                                         start=False, stop=(j == PER - 1), skip_group_check=True)
                    last.then_inc(scoresT_filled, 1)

                def weigh_values(g):
                    i = GROUPS * (t - 1) + g
                    pe.wait_ge(probs_ready, i + 1)
                    pe.wait_ge(heads_ready, nonneg(i))
                    if g == 0:
                        pe.wait_ge(v_ready, nonneg(KV_GROUPS * t))
                    for j in range(PER):
                        h = g * PER + j
                        last = pe.matmul(bank_out[j // 2][:, j % 2 * VW:(j % 2 + 1) * VW], probs[:, h, :],
                                         values[:, h // SHARE, :], start=True, stop=True)
                    last.then_inc(out_filled, 1)

                def turn_heads(b, g):
                    pe.wait_ge(heads_ready, GROUPS * b + g + 1)
                    turn([heads[g % 2][:, j, :] for j in range(PER)], headsT_filled, headsT_ready, GROUPS * b + g + 1)

                def add_output(b, heads_range):
                    for h in heads_range:
                        last = pe.matmul(bank_y[:, 0:EMBED], headsT[:, h, :], wo[:, h, :],
                                         start=(h == 0), stop=(h == HEADS - 1))
                    return last

                def project_q(g):
                    if g == 0:
                        pe.wait_ge(layer.hT_ready, t + 1)
                    pe.wait_ge(q_done, nonneg(GROUPS * t + g))
                    if normed:
                        for c in range(EC):
                            last = pe.matmul(bank_project[0][:, :], layer.hT[:, c, :],
                                             wq[:, c, g * PER * D:(g + 1) * PER * D],
                                             start=(c == 0), stop=(c == EC - 1))
                    else:
                        for j in range(PER):
                            for c in range(EC):
                                h = g * PER + j
                                last = pe.matmul(bank_project[0][:, j * P:(j + 1) * P], wq[:, c, h * D:(h + 1) * D],
                                                 layer.hT[:, c, :], start=(c == 0), stop=(c == EC - 1))
                    last.then_inc(q_filled, 1)

                def project_k(g):
                    pe.wait_ge(k_done, nonneg(KV_GROUPS * t + g))
                    if normed:
                        last = pe.matmul(bank_project[1][:, :], contextT[:, :], wk[:, g * PER * D:(g + 1) * PER * D],
                                         start=True, stop=True)
                    else:
                        for j in range(PER):
                            h = g * PER + j
                            last = pe.matmul(bank_project[1][:, j * P:(j + 1) * P], wk[:, h * D:(h + 1) * D],
                                             contextT[:, :], start=True, stop=True)
                    last.then_inc(k_filled, 1)

                def project_v(g):
                    if g == 0:
                        pe.wait_ge(layer.x_updated, nonneg(t - 1))
                    pe.wait_ge(v_ready, nonneg(KV_GROUPS * t + g))
                    pe.matmul(bank_y[:, :], contextT[:, :], wv[:, g * PER * D:(g + 1) * PER * D],
                              start=True, stop=True).then_inc(v_filled, 1)

                def turn_q(b, g):
                    pe.wait_ge(q_read, GROUPS * b + g + 1)
                    turn([q_scaled[:, j, :] for j in range(PER)], qT_filled, qT_ready, GROUPS * b + g + 1)

                def turn_k(b, g):
                    pe.wait_ge(k_read, GROUPS * b + g + 1)
                    turn([k_scaled[:, j, :] for j in range(PER)], kT_filled, kT_ready, GROUPS * b + g + 1)

                if middle:
                    scores(0)
                    if normed:
                        turn_q(t - 1, GROUPS - 1)
                if tail:
                    pe.wait_ge(layer.x_updated, nonneg(t - 2))
                    if middle:
                        pe.wait_ge(v_ready, nonneg(KV_GROUPS * t))
                    add_output(t - 2, range(0, PER))
                    turn_heads(t - 2, GROUPS - 1)
                    add_output(t - 2, range(PER, 2 * PER))
                if middle and normed:
                    turn_k(t - 1, GROUPS - 1)
                if tail:
                    add_output(t - 2, range(2 * PER, 3 * PER))
                if front:
                    pe.wait_ge(layer.h_ready, t + 1)
                    pe.wait_ge(context_loaded[s], nonneg(16 * ((t - s) // 2 + 1) if isinstance(t, int) else (t - s) * 8 + 16))
                    turn([layer.h[:, 0:P], layer.h[:, P:2 * P], context[s][:, :]], layer.hT_filled,
                         layer.hT_ready, t + 1)
                if middle:
                    scores_transposed(0)
                    scores(1)
                if tail:
                    pe.wait_ge(headsT_ready, nonneg(GROUPS * (t - 1)))
                    add_output(t - 2, range(3 * PER, HEADS)).then_inc(layer.y_filled, 1)
                for g in range(GROUPS):
                    if front:
                        project_q(g)
                        if normed and g:
                            turn_q(t, g - 1)
                    if middle and g + 1 < GROUPS:
                        scores_transposed(g + 1)
                    if middle:
                        weigh_values(g)
                    if front:
                        if normed and g:
                            turn_k(t, g - 1)
                        if (g + 1) % SHARE == 0:
                            project_k(g // SHARE)
                    if middle and g:
                        turn_heads(t - 1, g - 1)
                    if front and (g + 1) % SHARE == 0:
                        project_v(g // SHARE)
                    if middle and g + 2 < GROUPS:
                        scores(g + 2)
            pipeline(pe, step)


def gated_mlp(nc, core, dram, next_weights):
    n = 2
    INTER, ROUTED, EXPERTS = 1024, 128, 8
    TILES = INTER // P
    HALVES = 2
    PER = TILES // HALVES
    with ExitStack() as ctx:
        layer = Layer(core, n, "mlp", ctx)
        sem, sbuf = layer.sem, layer.sbuf
        region = core.region[n % 2]
        at = 0

        def weight(chunk, width):
            nonlocal at
            part = region[:, at:at + chunk * width].rearrange("p (c n) -> p c n", c=chunk)
            at += chunk * width
            return part
        w_gate, w_up, w_down = weight(EC, INTER), weight(EC, INTER), weight(TILES, EMBED)
        r_gate, r_up, r_down, router = weight(EC, ROUTED), weight(EC, ROUTED), weight(1, EMBED), weight(EC, EXPERTS)
        tanh = [sbuf(f"tanh{j}", [P, 512]) for j in range(HALVES + 1)]
        gated = [sbuf(f"gated{j}", [P, 512]) for j in range(HALVES + 1)]
        inner = sbuf("inner", [P, TILES + 1, P])
        top = sbuf("top", [P, EXPERTS])
        gap, ratio, both, share, weight_half = (sbuf(f"router{k}", [P, 1]) for k in range(5))
        x_routed = sbuf("x_routed", [P, EMBED])

        bank_h, bank_routed, bank_y = core.banks[0], core.banks[5], core.banks[6]
        bank_gate, bank_up = [core.banks[1], core.banks[3]], [core.banks[2], core.banks[4]]
        PARTS = HALVES + 1
        part_filled, tanh_ready = sem("part_filled"), sem("tanh_ready")
        gated_ready, inner_ready = sem("gated_ready"), sem("inner_ready")
        router_chain, gap_ready, ratio_ready = sem("router_chain"), sem("gap_ready"), sem("ratio_ready")
        block = ctx.enter_context(nc.Block())

        def gate_of(j):
            return bank_gate[j][:, :] if j < HALVES else bank_routed[:, 0:ROUTED]

        def up_of(j):
            return bank_up[j][:, :] if j < HALVES else bank_routed[:, ROUTED:2 * ROUTED]
        ORDER = [HALVES, 0, 1]

        @block.sync
        def _(sp):
            layer.clear_last_layers_semaphores(sp)
            load_weights(sp, core, n + 1, next_weights)

        @block.gpsimd
        def _(pool):
            layer.pool_rstd(pool)

        @block.scalar
        def _(act):
            def step(t, s, front, middle, tail):
                if front:
                    act.wait_ge(part_filled, nonneg(PARTS * t))
                    layer.act_copy_hT(act, t, bank_h)
                    for k, j in enumerate(ORDER):
                        width = 512 if j < HALVES else ROUTED
                        act.wait_ge(part_filled, PARTS * t + k + 1)
                        act.wait_ge(gated_ready, nonneg(PARTS * (t - 1) + k + 1))
                        act.activation(tanh[j][:, 0:width], gate_of(j), ACT.Tanh, scale=0.5).then_inc(tanh_ready, 1)
                        if k == 0:
                            act.wait_ge(gap_ready, t + 1)
                            act.wait_ge(router_chain, nonneg(3 * t))
                            act.activation(ratio[:, :], gap[:, :], ACT.Exp).then_inc(ratio_ready, 1)
            pipeline(act, step)

        @block.vector
        def _(dve):
            layer.dve_norm_setup(dve)
            router_step = Chain(dve, router_chain, 3)
            tail_step = Chain(dve, layer.tail_chain, STATISTICS_STEPS + 1)

            def step(t, s, front, middle, tail):
                def gate(b, k):
                    i, j = PARTS * b + k, ORDER[k]
                    width = 512 if j < HALVES else ROUTED
                    tiles = inner[:, j * PER:j * PER + width // P, :].rearrange("p j t -> p (j t)")
                    if k == 0:
                        dve.wait_ge(layer.y_filled, nonneg(b))
                        dve.wait_ge(gap_ready, nonneg(b))
                        dve.wait_ge(ratio_ready, nonneg(b))
                    dve.wait_ge(tanh_ready, i + 1)
                    dve.wait_ge(inner_ready, nonneg(i - PARTS + 1))
                    dve.scalar_tensor_tensor(gated[j][:, 0:width], tanh[j][:, 0:width], 1.0, gate_of(j),
                                             ALU.add, ALU.mult).then_inc(gated_ready, 1)
                    if k == 0:
                        dve.max(top[:, :], bank_routed[:, 2 * ROUTED:2 * ROUTED + EXPERTS])
                    dve.wait_ge(gated_ready, i + 1)
                    dve.tensor_tensor(tiles, gated[j][:, 0:width], up_of(j), ALU.mult).then_inc(inner_ready, 1)
                    if k == 0:
                        dve.wait_ge(inner_ready, i + 1)
                        dve.tensor_tensor(gap[:, :], top[:, 1:2], top[:, 0:1], ALU.subtract)\
                           .then_inc(gap_ready, 1)
                if front:
                    layer.dve_normalise(dve, t)
                if middle:
                    gate(t - 1, PARTS - 1)
                    b = t - 1
                    router_step.start(b)
                    tail_step.start(b)
                    dve.wait_ge(ratio_ready, b + 1)
                    dve.wait_ge(layer.y_filled, b + 1)
                    router_step(dve.tensor_scalar(both[:, :], ratio[:, :], 1.0, 2.0, ALU.add, ALU.mult))
                    router_step(dve.reciprocal(share[:, :], both[:, :]))
                    router_step(dve.scalar_tensor_tensor(weight_half[:, :], ratio[:, :], share[:, 0:1], share[:, :],
                                                         ALU.mult, ALU.add))
                    tail_step(dve.scalar_tensor_tensor(x_routed[:, :], bank_y[:, EMBED:2 * EMBED], weight_half[:, 0:1],
                                                       core.batch_x(b), ALU.mult, ALU.add))
                    dve.scalar_tensor_tensor(layer.new_x[:, :], bank_y[:, 0:EMBED], 0.5, x_routed[:, :],
                                             ALU.mult, ALU.add).then_inc(layer.x_updated, 1)
                    dve.wait_ge(layer.x_updated, b + 1)
                    layer.dve_statistics(dve, b, tail_step)
                if front:
                    gate(t, 0)
                    gate(t, 1)
            pipeline(dve, step)

        @block.tensor
        def _(pe):
            pe.wait_ge(core.weights_loaded[n], 16 * WEIGHT_PARTS)

            def step(t, s, front, middle, tail):
                if front:
                    pe.wait_ge(layer.hT_ready, nonneg(t))
                    layer.pe_transpose_h(pe, t, bank_h)
                if middle:
                    b = t - 1
                    pe.wait_ge(layer.x_updated, nonneg(b))
                    pe.wait_ge(inner_ready, PARTS * b + 1)
                    pe.matmul(bank_y[:, EMBED:2 * EMBED], inner[:, TILES, :], r_down[:, 0, :], start=True, stop=True)
                    for j in range(HALVES):
                        pe.wait_ge(inner_ready, nonneg(PARTS * b + j + 2))
                        for m in range(j * PER, (j + 1) * PER):
                            last = pe.matmul(bank_y[:, 0:EMBED], inner[:, m, :], w_down[:, m, :],
                                             start=(m == 0), stop=(m == TILES - 1))
                    last.then_inc(layer.y_filled, 1)
                if front:
                    pe.wait_ge(layer.hT_ready, t + 1)

                    def project(out, wt, m):
                        for c in range(EC):
                            last = pe.matmul(out, wt[:, c, m * P:(m + 1) * P], layer.hT[:, c, :],
                                             start=(c == 0), stop=(c == EC - 1))
                        return last
                    for k, j in enumerate(ORDER):
                        if j == HALVES:
                            pe.wait_ge(gap_ready, nonneg(t))
                            pe.wait_ge(inner_ready, nonneg(PARTS * (t - 1) + k + 1))
                            project(bank_routed[:, 0:ROUTED], r_gate, 0)
                            project(bank_routed[:, ROUTED:2 * ROUTED], r_up, 0)
                            for c in range(EC):
                                last = pe.matmul(bank_routed[:, 2 * ROUTED:2 * ROUTED + EXPERTS], layer.hT[:, c, :],
                                                 router[:, c, :], start=(c == 0), stop=(c == EC - 1))
                        else:
                            pe.wait_ge(inner_ready, nonneg(PARTS * (t - 1) + k + 1))
                            for m in range(PER):
                                project(bank_gate[j][:, m * P:(m + 1) * P], w_gate, j * PER + m)
                            for m in range(PER):
                                last = project(bank_up[j][:, m * P:(m + 1) * P], w_up, j * PER + m)
                        last.then_inc(part_filled, 1)
            pipeline(pe, step)


def grouped_attention(nc, core, dram, next_weights):
    n = 3
    HEADS, D = 32, 8
    GROUPS = 8
    PER = HEADS // GROUPS
    ROWS = PER * D
    SLOTS = P // ROWS
    SCALE = float(D) ** -0.5
    VW = D + 1
    with ExitStack() as ctx:
        layer = Layer(core, n, "grouped", ctx)
        sem, sbuf = layer.sem, layer.sbuf
        region = core.region[n % 2]
        wq, wk, wo = (region[:, k * EC * EMBED:(k + 1) * EC * EMBED].rearrange("p (c n) -> p c n", c=EC)
                      for k in range(3))
        wv = region[:, 3 * EC * EMBED:3 * EC * EMBED + EC * GROUPS * D].rearrange("p (c n) -> p c n", c=EC)
        CHUNK_HEADS = SLOTS * PER
        columns = sbuf("columns", [P, 2 * EC + CHUNK_HEADS + PER])
        bias_q, bias_k = columns[:, 0:EC], columns[:, EC:2 * EC]
        own = columns[:, 2 * EC:2 * EC + CHUNK_HEADS]
        own_in_slots = columns[:, 2 * EC + CHUNK_HEADS:]
        rows = sbuf("rows", [1, GROUPS * D + EMBED])
        bias_v, bias_o = rows[:, 0:GROUPS * D], rows[:, GROUPS * D:GROUPS * D + EMBED]
        qT = [sbuf(f"qT{s}", [P, EC, P]) for s in range(2)]
        qT_bf = [sbuf(f"qT_bf{s}", [P, EC, P], BF16) for s in range(2)]
        q_own = [sbuf(f"q_own{s}", [P, EC, CHUNK_HEADS, P]) for s in range(2)]
        kT = [sbuf(f"kT{s}", [P, EC, P]) for s in range(2)]
        kT_bf = [sbuf(f"kT_bf{s}", [P, EC, PER, P], BF16) for s in range(2)]
        values = [sbuf(f"values{s}", [P, GROUPS, VW]) for s in range(2)]
        maxima = [sbuf(f"maxima{s}", [P, HEADS], BF16) for s in range(2)]
        probs = sbuf("probs", [P, GROUPS, PER * P])
        reciprocal = sbuf("reciprocal", [P, HEADS])
        heads = sbuf("heads", [P, HEADS, D])
        headsT = sbuf("headsT", [P, EC, P])

        bank_hv, bank_q, bank_k = core.banks[0:3]
        bank_scores, bank_scoresT, bank_out = core.banks[3:5], core.banks[5:7], core.banks[7]
        half_tail = bank_hv[:, EMBED:2 * EMBED]

        constants_loaded, constants_ready = sem("constants_loaded"), sem("constants_ready")
        q_filled, q_ready, q_bf_ready = sem("q_filled"), sem("q_ready"), sem("q_bf_ready")
        q_own_ready, k_filled = sem("q_own_ready"), sem("k_filled")
        k_ready, k_bf_ready = sem("k_ready"), sem("k_bf_ready")
        v_filled, v_ready = sem("v_filled"), sem("v_ready")
        scores_filled, max_ready = sem("scores_filled"), sem("max_ready")
        scoresT_filled, probs_ready = sem("scoresT_filled"), sem("probs_ready")
        out_filled = sem("out_filled")
        heads_ready, headsT_filled, headsT_ready = sem("heads_ready"), sem("headsT_filled"), sem("headsT_ready")
        heads_chain = sem("heads_chain")
        block = ctx.enter_context(nc.Block())

        @block.sync
        def _(sp):
            layer.clear_last_layers_semaphores(sp)
            sp.dma_start(columns[:, :], dram["grouped_columns"]).then_inc(constants_loaded, 16)
            sp.dma_start(rows[:, :], dram["grouped_rows"]).then_inc(constants_loaded, 16)
            load_weights(sp, core, n + 1, next_weights)

        @block.gpsimd
        def _(pool):
            for s in range(2):
                last = pool.memset(values[s][:, :, D:VW], 1.0)
            last.then_inc(constants_ready, 1)
            layer.pool_rstd(pool)
            pool.wait_ge(constants_loaded, 2 * 16)

            def step(t, s, front, middle, tail):
                if front:
                    pool.wait_ge(q_ready, t + 1)
                    pool.wait_ge(scores_filled, nonneg(GROUPS * (t - 1)))
                    pool.tensor_tensor(qT_bf[s][:, :, :], qT[s][:, :, :],
                                       core.ones[:, 0:1].unsqueeze(2).to_broadcast([P, EC, P]), ALU.mult)\
                        .then_inc(q_bf_ready, 1)
                    pool.wait_ge(k_ready, t + 1)
                    for m in range(PER):
                        last = pool.tensor_tensor(kT_bf[s][:, :, m, :], kT[s][:, :, :],
                                                  own_in_slots[:, m:m + 1].unsqueeze(2).to_broadcast([P, EC, P]), ALU.mult)
                    last.then_inc(k_bf_ready, 1)
            pipeline(pool, step)

        @block.scalar
        def _(act):
            act.wait_ge(constants_loaded, 2 * 16)
            act.wait_ge(constants_ready, 1)

            def step(t, s, front, middle, tail):
                def exponentials(g):
                    i = GROUPS * (t - 1) + g
                    act.wait_ge(scoresT_filled, i + 1)
                    act.wait_ge(out_filled, nonneg(i - GROUPS + 1))
                    act.activation(probs[:, g, :], bank_scoresT[g % 2][:, :], ACT.Exp, scale=SCALE)\
                       .then_inc(probs_ready, 1)

                def own_queries(first, end):
                    for h in range(first, end):
                        last = act.activation(q_own[s][:, :, h, :], qT[s][:, :, :], ACT.Copy, scale=own[:, h:h + 1])
                    return last
                if front:
                    act.wait_ge(v_filled, nonneg(t))
                    layer.act_copy_hT(act, t, bank_hv)
                if middle:
                    exponentials(0)
                    exponentials(1)
                if front:
                    act.wait_ge(q_ready, t + 1)
                    act.wait_ge(scoresT_filled, nonneg(GROUPS * (t - 1)))
                    own_queries(0, 4)
                if middle:
                    exponentials(2)
                if tail:
                    act.wait_ge(headsT_filled, nonneg(t - 1))
                    act.wait_ge(layer.y_filled, nonneg(t - 2))
                    act.activation(headsT[:, :, :], half_tail.rearrange("p (c t) -> p c t", c=EC),
                                   ACT.Copy).then_inc(headsT_ready, 1)
                if front:
                    own_queries(4, 8)
                if middle:
                    exponentials(3)
                if front:
                    own_queries(8, 12)
                if middle:
                    exponentials(4)
                if front:
                    own_queries(12, CHUNK_HEADS).then_inc(q_own_ready, 1)
                if middle:
                    for g in range(5, GROUPS):
                        exponentials(g)
                if front:
                    act.wait_ge(v_filled, t + 1)
                    act.wait_ge(out_filled, nonneg(GROUPS * (t - 1)))
                    act.activation(values[s][:, :, 0:D],
                                   bank_hv[:, 0:GROUPS * D].rearrange("p (h d) -> p h d", h=GROUPS), ACT.Copy)\
                       .then_inc(v_ready, 1)
            pipeline(act, step)

        @block.vector
        def _(dve):
            layer.dve_norm_setup(dve)
            dve.wait_ge(constants_loaded, 2 * 16)
            heads_step = Chain(dve, heads_chain, 1)
            tail_step = Chain(dve, layer.tail_chain, STATISTICS_STEPS)

            def step(t, s, front, middle, tail):
                def row_maxima(g):
                    i = GROUPS * (t - 1) + g
                    dve.wait_ge(scores_filled, i + 1)
                    dve.wait_ge(scoresT_filled, nonneg(GROUPS * (t - 2)))
                    with nc.allow_low_precision("the maximum only shifts a softmax's exponents"):
                        dve.tensor_reduce(maxima[1 - s][:, g * PER:(g + 1) * PER],
                                          bank_scores[g % 2].rearrange("p (h k) -> p h k", h=PER),
                                          AX.X, ALU.max).then_inc(max_ready, 1)

                def add_bias(bank, filled, to, bias, ready):
                    dve.wait_ge(filled, t + 1)
                    for c in range(EC):
                        last = dve.tensor_scalar(to[:, c, :], bank[:, c * P:(c + 1) * P], bias[:, c:c + 1], None,
                                                 ALU.add)
                    last.then_inc(ready, 1)
                if front:
                    layer.dve_normalise(dve, t)
                if middle:
                    row_maxima(0)
                    row_maxima(1)
                if tail:
                    b = t - 2
                    heads_step.start(b)
                    dve.wait_ge(out_filled, GROUPS * (b + 1))
                    out = bank_out[:, 0:HEADS * VW].rearrange("p (h d) -> p h d", h=HEADS)
                    heads_step(dve.reciprocal(reciprocal[:, :].unsqueeze(2), out[:, :, D:VW]))
                    dve.wait_ge(headsT_filled, nonneg(b))
                    dve.tensor_tensor(heads[:, :, :], out[:, :, 0:D],
                                      reciprocal[:, :].unsqueeze(2).to_broadcast([P, HEADS, D]), ALU.mult)\
                       .then_inc(heads_ready, 1)
                if middle:
                    row_maxima(2)
                if front:
                    dve.wait_ge(scoresT_filled, nonneg(GROUPS * (t - 1)))
                    dve.wait_ge(q_bf_ready, nonneg(t - 1))
                    add_bias(bank_q, q_filled, qT[s], bias_q, q_ready)
                if middle:
                    row_maxima(3)
                if front:
                    dve.wait_ge(k_bf_ready, nonneg(t - 1))
                    add_bias(bank_k, k_filled, kT[s], bias_k, k_ready)
                if middle:
                    for g in range(4, GROUPS - 1):
                        row_maxima(g)
                if tail:
                    tail_step.start(t - 2)
                    layer.dve_update_x(dve, t - 2, half_tail, tail_step)
                if middle:
                    row_maxima(GROUPS - 1)
            pipeline(dve, step)

        @block.tensor
        def _(pe):
            pe.wait_ge(core.weights_loaded[n], 16 * WEIGHT_PARTS)
            pe.wait_ge(constants_loaded, 2 * 16)
            pe.wait_ge(constants_ready, 1)

            def step(t, s, front, middle, tail):
                def scores(g):
                    i = GROUPS * (t - 1) + g
                    pe.wait_ge(max_ready, nonneg(i - 1))
                    slot, c = slice(ROWS * (g % SLOTS), ROWS * (g % SLOTS + 1)), g // SLOTS
                    pe.matmul(bank_scores[g % 2][:, :], qT_bf[1 - s][slot, c, :], kT_bf[1 - s][slot, c, :, :],
                              start=True, stop=True).then_inc(scores_filled, 1)

                def scores_transposed(g):
                    i = GROUPS * (t - 1) + g
                    pe.wait_ge(max_ready, i + 1)
                    pe.wait_ge(probs_ready, nonneg(i - 1))
                    c = g // SLOTS
                    bank = bank_scoresT[g % 2]
                    for m in range(PER):
                        h = g * PER + m
                        pe.matmul(bank[:, m * P:(m + 1) * P], maxima[1 - s][:, h:h + 1].to_broadcast([P, P]),
                                  core.minus_ident_bf[:, :], start=(m == 0), stop=False, skip_group_check=True)
                    first = g % SLOTS * PER
                    pe.matmul(bank[:, :], kT[1 - s][:, c, :], q_own[1 - s][:, c, first:first + PER, :],
                              start=False, stop=True, skip_group_check=True).then_inc(scoresT_filled, 1)

                def weigh_values(g, b=t - 1, s=1 - s):
                    i = GROUPS * b + g
                    pe.wait_ge(probs_ready, i + 1)
                    if g == 0:
                        pe.wait_ge(v_ready, nonneg(t))
                        pe.wait_ge(heads_ready, nonneg(t - 1))
                    for m in range(PER):
                        h = g * PER + m
                        last = pe.matmul(bank_out[:, h * VW:(h + 1) * VW], probs[:, g, m * P:(m + 1) * P],
                                         values[s][:, g, :], start=True, stop=True)
                    last.then_inc(out_filled, 1)

                def project(bank, wt):
                    for m in range(EC):
                        for c in range(EC):
                            last = pe.matmul(bank[:, m * P:(m + 1) * P], wt[:, c, m * P:(m + 1) * P],
                                             layer.hT[:, c, :], start=(c == 0), stop=(c == EC - 1))
                    return last

                def transpose_heads():
                    pe.wait_ge(heads_ready, nonneg(t - 1))
                    pe.wait_ge(layer.x_updated, nonneg(t - 2))
                    flat = heads[:, :, :].rearrange("p h d -> p (h d)")
                    for c in range(EC):
                        last = pe.transpose(half_tail[:, c * P:(c + 1) * P], flat[:, c * P:(c + 1) * P],
                                            core.ident[:, :])
                    last.then_inc(headsT_filled, 1)

                def project_heads():
                    pe.wait_ge(headsT_ready, nonneg(t - 1))
                    pe.matmul(half_tail, core.ones[0:1, :], bias_o, start=True, stop=False)
                    for c in range(EC):
                        last = pe.matmul(half_tail, headsT[:, c, :], wo[:, c, :], start=False, stop=(c == EC - 1))
                    last.then_inc(layer.y_filled, 1)

                if middle:
                    pe.wait_ge(q_bf_ready, nonneg(t))
                    pe.wait_ge(k_bf_ready, nonneg(t))
                    scores(0)
                    scores(1)
                if tail:
                    weigh_values(7, t - 2, s)
                if front:
                    pe.wait_ge(v_ready, nonneg(t))
                    layer.pe_transpose_h(pe, t, bank_hv)
                if middle:
                    pe.wait_ge(q_own_ready, nonneg(t))
                    scores_transposed(0)
                    scores(2)
                if front:
                    pe.wait_ge(layer.hT_ready, t + 1)
                    pe.wait_ge(q_ready, nonneg(t))
                    project(bank_q, wq).then_inc(q_filled, 1)
                if middle:
                    scores_transposed(1)
                    weigh_values(0)
                    scores(3)
                if front:
                    pe.wait_ge(k_ready, nonneg(t))
                    project(bank_k, wk).then_inc(k_filled, 1)
                if middle:
                    scores_transposed(2)
                    weigh_values(1)
                    scores(4)
                if tail:
                    transpose_heads()
                if middle:
                    scores_transposed(3)
                    weigh_values(2)
                    scores(5)
                    scores_transposed(4)
                    weigh_values(3)
                    scores(6)
                if tail:
                    project_heads()
                if middle:
                    scores_transposed(5)
                    weigh_values(4)
                    scores(7)
                    scores_transposed(6)
                    weigh_values(5)
                    scores_transposed(7)
                    weigh_values(6)
                if front:
                    pe.wait_ge(layer.x_updated, nonneg(t - 1))
                    pe.matmul(bank_hv[:, 0:GROUPS * D], core.ones[0:1, :], bias_v, start=True, stop=False)
                    for c in range(EC):
                        last = pe.matmul(bank_hv[:, 0:GROUPS * D], layer.hT[:, c, :], wv[:, c, :],
                                         start=False, stop=(c == EC - 1))
                    last.then_inc(v_filled, 1)
            pipeline(pe, step)


def mx_mlp(nc, core, dram, out):
    n = 5
    INTER = 1024
    TILES = INTER // P
    BLOCK = 32
    FP8_MAX, LEAST_SCALE = 448.0, 1e-30
    LEAST_NORMAL = 2.0 ** -6
    ROUNDER = 1.5 * 2.0 ** 20
    EXPONENT_BITS = 0x7F800000
    I32 = mybir.dt.int32
    PIECE = 1024
    WEIGHT_PIECES = 3 * EC * INTER // PIECE
    HALVES = INTER // 512
    with ExitStack() as ctx:
        layer = Layer(core, n, "mx", ctx)
        sem, sbuf = layer.sem, layer.sbuf
        raw = core.region[n % 2]
        turned = core.region[1 - n % 2]
        w_gate = turned[:, 0:EC * INTER].rearrange("p (c n) -> p c n", c=EC)
        w_up = turned[:, EC * INTER:2 * EC * INTER].rearrange("p (c n) -> p c n", c=EC)
        w_down = turned[:, 2 * EC * INTER:3 * EC * INTER].rearrange("p (i n) -> p i n", i=TILES)

        class Scratch:
            def __init__(self, name, columns):
                blocks = columns // BLOCK
                self.columns, self.blocks = columns, blocks
                self.largest, self.scale, self.inverse = (sbuf(f"{name}_{x}", [P, blocks])
                                                          for x in ("largest", "scale", "inverse"))
                self.scaled = sbuf(f"{name}_scaled", [P, columns])
                self.rounder = sbuf(f"{name}_rounder", [P, columns])
        scratch = [Scratch(f"piece{s}", PIECE) for s in range(2)]
        scratch_h = Scratch("h", EMBED)
        h_q = sbuf("h_q", [P, EMBED])
        tanh = [sbuf(f"tanh{j}", [P, 512]) for j in range(HALVES)]
        gated = [sbuf(f"gated{j}", [P, 512]) for j in range(HALVES)]
        inner = [sbuf(f"inner{s}", [P, INTER]) for s in range(2)]
        inner_q = [sbuf(f"inner_q{s}", [P, INTER]) for s in range(2)]
        innerT = sbuf("innerT", [P, TILES, P])
        result = [sbuf(f"result{s}", [P, EMBED]) for s in range(2)]

        bank_h, bank_turn, bank_y = core.banks[0], core.banks[5:7], core.banks[7]
        bank_gate, bank_up = [core.banks[1], core.banks[3]], [core.banks[2], core.banks[4]]

        piece_chain, piece_scaled = sem("piece_chain"), sem("piece_scaled")
        pool_chain, piece_done = sem("pool_chain"), sem("piece_done")
        h_chain, h_scaled, h_pool_chain, h_done = sem("h_chain"), sem("h_scaled"), sem("h_pool_chain"), sem("h_done")
        weights_filled, weights_ready = sem("weights_filled"), sem("weights_ready")
        half_filled, tanh_ready = sem("half_filled"), sem("tanh_ready")
        gated_ready, inner_ready = sem("gated_ready"), sem("inner_ready")
        innerT_filled, innerT_ready = sem("innerT_filled"), sem("innerT_ready")
        result_ready = sem("result_ready")
        stored = [sem(f"stored{s}") for s in range(2)]
        block = ctx.enter_context(nc.Block())

        def dve_scale(dve, source, sc, step, least, done):
            step(dve.tensor_reduce(sc.largest[:, :], source.rearrange("p (b k) -> p b k", k=BLOCK), AX.X,
                                   ALU.max, apply_absolute_value=True))
            step(dve.tensor_scalar(sc.scale[:, :], sc.largest[:, :], 1.0 / FP8_MAX, least, ALU.mult, ALU.max))
            step(dve.reciprocal(sc.inverse[:, :], sc.scale[:, :]))
            step(dve.tensor_tensor(sc.scaled[:, :].rearrange("p (b k) -> p b k", k=BLOCK),
                                   source.rearrange("p (b k) -> p b k", k=BLOCK),
                                   sc.inverse[:, :].unsqueeze(2).to_broadcast([P, sc.blocks, BLOCK]), ALU.mult))
            step(dve.tensor_scalar(sc.rounder[:, :].bitcast(I32), sc.scaled[:, :].bitcast(I32), EXPONENT_BITS, None,
                                   ALU.bitwise_and))
            dve.tensor_scalar(sc.rounder[:, :], sc.rounder[:, :], LEAST_NORMAL, ROUNDER, ALU.max, ALU.mult)\
               .then_inc(done, 1)

        def pool_round(pool, sc, out, step, done):
            step(pool.tensor_tensor(sc.scaled[:, :], sc.scaled[:, :], sc.rounder[:, :], ALU.add))
            step(pool.tensor_tensor(sc.scaled[:, :], sc.scaled[:, :], sc.rounder[:, :], ALU.subtract))
            pool.tensor_tensor(out.rearrange("p (b k) -> p b k", k=BLOCK),
                               sc.scaled[:, :].rearrange("p (b k) -> p b k", k=BLOCK),
                               sc.scale[:, :].unsqueeze(2).to_broadcast([P, sc.blocks, BLOCK]), ALU.mult)\
                .then_inc(done, 1)

        @block.sync
        def _(sp):
            def step(t, s, front, middle, tail):
                if tail:
                    b = t - 2
                    sp.wait_ge(result_ready, b + 1)
                    sp.dma_start(out[bass.ds(b, 1), :, :].rearrange("b p e -> (b p) e"), result[s][:, :])\
                      .then_inc(stored[s], 16)
            pipeline(sp, step)
            for s in range(2):
                sp.wait_ge(stored[s], 16 * BATCHES // 2)

        @block.gpsimd
        def _(pool):
            layer.pool_rstd(pool)
            piece_step = Chain(pool, pool_chain, 2)
            h_step = Chain(pool, h_pool_chain, 2)
            for piece in range(WEIGHT_PIECES):
                piece_step.start(piece)
                pool.wait_ge(piece_scaled, piece + 1)
                pool_round(pool, scratch[piece % 2], raw[:, piece * PIECE:(piece + 1) * PIECE], piece_step, piece_done)

            def step(t, s, front, middle, tail):
                if front:
                    h_step.start(t)
                    pool.wait_ge(h_scaled, t + 1)
                    pool.wait_ge(layer.hT_filled, nonneg(t))
                    pool_round(pool, scratch_h, h_q[:, :], h_step, h_done)
                if middle:
                    b = t - 1
                    piece_step.start(b + WEIGHT_PIECES)
                    pool.wait_ge(piece_scaled, b + WEIGHT_PIECES + 1)
                    pool.wait_ge(innerT_filled, nonneg(HALVES * (b - 1)))
                    pool_round(pool, scratch[1 - s], inner_q[1 - s][:, :], piece_step, piece_done)
            pipeline(pool, step)

        @block.scalar
        def _(act):
            for k in range(3 * EC * INTER // 512):
                act.wait_ge(weights_filled, k + 1)
                act.activation(turned[:, k * 512:(k + 1) * 512], bank_gate[0][:, :] if k % 2 else bank_up[0][:, :],
                               ACT.Copy).then_inc(weights_ready, 1)

            def step(t, s, front, middle, tail):
                if middle:
                    b = t - 1
                    for j in range(HALVES):
                        i = HALVES * b + j
                        act.wait_ge(half_filled, i + 1)
                        act.wait_ge(gated_ready, nonneg(i - HALVES + 1))
                        act.activation(tanh[j][:, :], bank_gate[j][:, :], ACT.Tanh, scale=0.5).then_inc(tanh_ready, 1)
                if tail:
                    b = t - 2
                    for j in range(HALVES):
                        act.wait_ge(innerT_filled, HALVES * b + j + 1)
                        act.wait_ge(layer.y_filled, nonneg(b))
                        act.activation(innerT[:, 4 * j:4 * j + 4, :],
                                       bank_turn[j].rearrange("p (i t) -> p i t", i=4), ACT.Copy)\
                           .then_inc(innerT_ready, 1)
                if front:
                    act.wait_ge(half_filled, nonneg(HALVES * t))
                    layer.act_copy_hT(act, t, bank_h)
            pipeline(act, step)

        @block.vector
        def _(dve):
            layer.dve_norm_setup(dve)
            dve.wait_ge(core.weights_loaded[n], 16 * WEIGHT_PARTS)
            piece_step = Chain(dve, piece_chain, 5)
            h_step = Chain(dve, h_chain, 5)
            for piece in range(WEIGHT_PIECES):
                piece_step.start(piece)
                dve.wait_ge(piece_done, nonneg(piece - 1))
                dve_scale(dve, raw[:, piece * PIECE:(piece + 1) * PIECE], scratch[piece % 2], piece_step,
                          LEAST_SCALE, piece_scaled)

            def step(t, s, front, middle, tail):
                if front:
                    dve.wait_ge(h_chain, nonneg(5 * t))
                    dve.wait_ge(h_done, nonneg(t))
                    dve.tensor_scalar(layer.h[:, :], core.batch_x(t), core.column(core.mean, t),
                                      core.column(core.rstd, t), ALU.subtract, ALU.mult).then_inc(layer.h_ready, 1)
                    dve.wait_ge(layer.h_ready, t + 1)
                    h_step.start(t)
                    dve_scale(dve, layer.h[:, :], scratch_h, h_step, LEAST_SCALE, h_scaled)
                if middle:
                    b = t - 1
                    for j in range(HALVES):
                        i = HALVES * b + j
                        dve.wait_ge(tanh_ready, i + 1)
                        dve.wait_ge(inner_ready, nonneg(i - HALVES + 1))
                        dve.wait_ge(piece_scaled, nonneg(WEIGHT_PIECES + b - 1))
                        dve.scalar_tensor_tensor(gated[j][:, :], tanh[j][:, :], 1.0, bank_gate[j][:, :],
                                                 ALU.add, ALU.mult).then_inc(gated_ready, 1)
                        dve.wait_ge(gated_ready, i + 1)
                        dve.tensor_tensor(inner[1 - s][:, j * 512:(j + 1) * 512], gated[j][:, :], bank_up[j][:, :],
                                          ALU.mult).then_inc(inner_ready, 1)
                    piece = b + WEIGHT_PIECES
                    piece_step.start(piece)
                    dve.wait_ge(piece_done, nonneg(piece - 1))
                    dve.wait_ge(inner_ready, HALVES * (b + 1))
                    dve_scale(dve, inner[1 - s][:, :], scratch[1 - s], piece_step, 2 * LEAST_SCALE, piece_scaled)
                if tail:
                    b = t - 2
                    dve.wait_ge(layer.y_filled, b + 1)
                    dve.wait_ge(stored[s], nonneg(16 * (b // 2) if isinstance(b, int) else (b - s) * 8))
                    dve.scalar_tensor_tensor(result[s][:, :], bank_y[:, 0:EMBED], 0.5, core.batch_x(b),
                                             ALU.mult, ALU.add).then_inc(result_ready, 1)
            pipeline(dve, step)

        @block.tensor
        def _(pe):
            k = 0
            for w in range(2):
                for c in range(EC):
                    for half in range(2):
                        pe.wait_ge(piece_done, 2 * w + half + 1)
                        pe.wait_ge(weights_ready, nonneg(k - 1))
                        bank = bank_gate[0] if k % 2 else bank_up[0]
                        for i in range(4):
                            at = w * EC * INTER + (4 * half + i) * EMBED + c * P
                            last = pe.transpose(bank[:, i * P:(i + 1) * P], raw[:, at:at + P], core.ident[:, :])
                        last.then_inc(weights_filled, 1)
                        k += 1
            pe.wait_ge(piece_done, WEIGHT_PIECES)
            for i in range(0, TILES, 2):
                pe.wait_ge(weights_ready, nonneg(k - 1))
                bank = bank_gate[0] if k % 2 else bank_up[0]
                for j in range(2):
                    for c in range(EC):
                        at = 2 * EC * INTER + c * INTER + (i + j) * P
                        last = pe.transpose(bank[:, (j * EC + c) * P:(j * EC + c + 1) * P], raw[:, at:at + P],
                                            core.ident[:, :])
                last.then_inc(weights_filled, 1)
                k += 1
            pe.wait_ge(weights_ready, k)

            def step(t, s, front, middle, tail):
                def down(b, tiles):
                    for m in tiles:
                        if m % 4 == 0:
                            pe.wait_ge(innerT_ready, HALVES * b + m // 4 + 1)
                        last = pe.matmul(bank_y[:, 0:EMBED], innerT[:, m, :], w_down[:, m, :],
                                         start=(m == 0), stop=(m == TILES - 1))
                    return last

                if middle:
                    b = t - 1
                    pe.wait_ge(layer.hT_ready, b + 1)
                    for j in range(HALVES):
                        pe.wait_ge(inner_ready, nonneg(HALVES * (b - 1) + j + 1))
                        for bank, wt in ((bank_gate[j], w_gate), (bank_up[j], w_up)):
                            for c in range(EC):
                                last = pe.matmul(bank[:, :], layer.hT[:, c, :], wt[:, c, j * 512:(j + 1) * 512],
                                                 start=(c == 0), stop=(c == EC - 1))
                        last.then_inc(half_filled, 1)
                if tail:
                    b = t - 2
                    pe.wait_ge(piece_done, WEIGHT_PIECES + b + 1)
                    for j in range(HALVES):
                        pe.wait_ge(innerT_ready, nonneg(HALVES * (b - 1) + j + 1))
                        for i in range(4):
                            m = 4 * j + i
                            last = pe.transpose(bank_turn[j][:, i * P:(i + 1) * P], inner_q[s][:, m * P:(m + 1) * P],
                                                core.ident[:, :])
                        last.then_inc(innerT_filled, 1)
                    pe.wait_ge(result_ready, nonneg(b))
                    down(b, range(0, TILES // 2))
                if front:
                    pe.wait_ge(layer.hT_ready, nonneg(t))
                    pe.wait_ge(h_done, t + 1)
                    for c in range(EC):
                        last = pe.transpose(bank_h[:, c * P:(c + 1) * P], h_q[:, c * P:(c + 1) * P], core.ident[:, :])
                    last.then_inc(layer.hT_filled, 1)
                if tail:
                    down(t - 2, range(TILES // 2, TILES)).then_inc(layer.y_filled, 1)
            pipeline(pe, step)


def rotary_tables(tokens, embed, head_dim):
    f32 = np.float32
    inverse = f32(1.0) / f32(10000.0) ** (np.arange(0, head_dim, 2, dtype=f32) / f32(head_dim))
    angles = np.outer(np.arange(tokens, dtype=f32), inverse)
    angles = np.concatenate([angles, angles], axis=-1).astype(f32)
    feature = np.arange(embed)
    sign = np.where(feature % 2 == 0, -1, 1).astype(f32)
    cosine = np.cos(angles).astype(f32).T[feature % head_dim]
    sine = np.sin(angles).astype(f32).T[feature % head_dim] * sign[:, None]
    return [np.ascontiguousarray(a.reshape(-1, P, tokens).transpose(1, 0, 2).reshape(P, -1))
            for a in (cosine, sine)]


def constants():
    p, f = np.arange(P)[:, None], np.arange(P)[None, :]
    cosine, sine = rotary_tables(P, EMBED, 16)
    return {
        "identity": np.eye(P, dtype=np.float32),
        "cosine": cosine,
        "sine": sine,
        "later": np.where(f > p, NEG, 0).astype(np.float32),
        "earlier": np.where(f < p, NEG, 0).astype(np.float32),
        "causal_own": (p // 16 == np.arange(8)[None, :]).astype(np.float32),
        "parity": (p % 32 // 16 == np.arange(2)[None, :]).astype(np.float32),
    }


def chunks(w):
    k, n = w.shape
    return w.reshape(k // P, P, n).transpose(1, 0, 2).reshape(P, -1)


def per_query_head(w):
    return np.repeat(w.reshape(*w.shape[:-1], 8, 1, 8), 4, axis=-2).reshape(*w.shape[:-1], -1)


def packed_weights(v):
    wqkv = v["L0_attn_Wqkv"]
    swapped = wqkv.reshape(3, EMBED // 2, 2, EMBED)[:, :, ::-1].reshape(3, EMBED, EMBED)
    wq, wk, wv = wqkv.reshape(3, EMBED, EMBED)
    layers = [
        [chunks(wq.T), chunks(swapped[0].T), chunks(wk.T), chunks(swapped[1].T), chunks(wv.T),
         chunks(v["L0_attn_Wout"].T)],
        [chunks(v["L0_xattn_Wq"]), v["L0_xattn_Wk"], v["L0_xattn_Wv"], chunks(v["L0_xattn_Wo"])],
        [chunks(v["L0_ffn_sh_gate"].T), chunks(v["L0_ffn_sh_up"].T), chunks(v["L0_ffn_sh_down"].T),
         chunks(v["L0_ffn_r_gate"].T), chunks(v["L0_ffn_r_up"].T), chunks(v["L0_ffn_r_down"].T),
         chunks(v["L0_ffn_router_weight"].T)],
        [chunks(v["L1_attn_Wq"]), chunks(per_query_head(v["L1_attn_Wk"])), chunks(v["L1_attn_Wo"]),
         chunks(v["L1_attn_Wv"])],
        [chunks(v["L1_xattn_Wq"]), v["L1_xattn_Wk"], v["L1_xattn_Wv"], chunks(v["L1_xattn_Wo"])],
        [v["L1_ffn_gate_w"].reshape(-1, P, EMBED).transpose(1, 0, 2).reshape(P, -1),
         v["L1_ffn_up_w"].reshape(-1, P, EMBED).transpose(1, 0, 2).reshape(P, -1),
         v["L1_ffn_down_w"].reshape(EC, P, -1).transpose(1, 0, 2).reshape(P, -1)],
    ]
    return [np.concatenate(parts, axis=1) for parts in layers]


def build(nc, core_inputs, out):
    with ExitStack() as ctx:
        core = Core(nc, ctx)
        weights = [core_inputs[f"weights_{n}"] for n in range(6) if f"weights_{n}" in core_inputs]
        setup(nc, core, core_inputs["x"], core_inputs["identity"], weights)
        causal_attention(nc, core, core_inputs, weights[0], weights[1])
        cross_attention(nc, core, 1, core_inputs, weights[2], True)
        gated_mlp(nc, core, core_inputs, weights[3])
        grouped_attention(nc, core, core_inputs, weights[4])
        cross_attention(nc, core, 4, core_inputs, weights[5], False)
        mx_mlp(nc, core, core_inputs, out)


def kernel(**inputs):
    import concourse.bacc as bacc
    from concourse.bass_utils import run_bass_kernel_spmd

    values = {name: np.asarray(a) for name, a in inputs.items()}
    arrays = {"x": values["x"], "context": values["ctx_1024"], **constants()}
    arrays["gains"] = np.stack([values["L0_xattn_gq"], values["L0_xattn_gk"]], axis=1)
    rows_of_heads = (np.arange(P)[:, None] // 8 == np.arange(16)[None, :]).astype(np.float32)
    head_of_row = (np.arange(P)[:, None] % 32 // 8 == np.arange(4)[None, :]).astype(np.float32)
    arrays["grouped_columns"] = np.concatenate(
        [values["L1_attn_bq"].reshape(EC, P).T, per_query_head(values["L1_attn_bk"]).reshape(EC, P).T, rows_of_heads,
         head_of_row],
        axis=1)
    arrays["grouped_rows"] = np.concatenate([values["L1_attn_bv"], values["L1_attn_bo"]])[None, :]
    arrays["mask"] = values["mask_BxS2_bf1"].T.view(np.uint8)
    for n, w in enumerate(packed_weights(values)):
        arrays[f"weights_{n}"] = w
    nc = bacc.Bacc("TRN2", target_bir_lowering=False, num_devices=1)
    arrays = {name: np.ascontiguousarray(a) for name, a in arrays.items()}
    drams = {name: nc.dram_tensor(f"in_{name}", a.shape, mybir.dt.from_np(a.dtype), kind="ExternalInput").ap()
             for name, a in arrays.items()}
    out = nc.dram_tensor("out", arrays["x"].shape, F32, kind="ExternalOutput").ap()
    build(nc, drams, out)
    r = run_bass_kernel_spmd(nc, [{f"in_{name}": a for name, a in arrays.items()}], core_ids=[0])
    return r.results[0]["out"]
```

```python
import numpy as np
import concourse.bass as bass
from concourse import mybir
from contextlib import ExitStack

F32 = mybir.dt.float32
BF16 = mybir.dt.bfloat16
F32R = mybir.dt.float32r
I32 = mybir.dt.int32
HIGH_BITS = -(1 << 12)
ALU = mybir.AluOpType
ACT = mybir.ActivationFunctionType
AX = mybir.AxisListType

P = 128
BATCHES = 16
PARTS = ((0, 0), (0, 1), (1, 0))
EMBED = 256
EC = EMBED // P
LN_EPS = 1e-5
NEG = -1e30


def nonneg(count):
    return max(count, 0) if isinstance(count, int) else count


class Chain:

    def __init__(self, engine, sem, per):
        self.engine, self.sem, self.per = engine, sem, per

    def start(self, batch):
        self.base, self.done = batch * self.per, 0

    def __call__(self, instruction):
        self.done += 1
        assert self.done <= self.per
        instruction.then_inc(self.sem, 1)
        self.engine.wait_ge(self.sem, self.base + self.done)


def pipeline(engine, step):
    step(0, 0, True, False, False)
    step(1, 1, True, True, False)
    step(2, 0, True, True, True)
    step(3, 1, True, True, True)
    with engine.Fori(4, BATCHES - 1, 2) as t:
        step(t, 0, True, True, True)
        step(t + 1, 1, True, True, True)
    step(BATCHES, 0, False, True, True)
    step(BATCHES + 1, 1, False, False, True)


SEMAPHORES = 44


class Core:

    def __init__(self, nc, ctx):
        self.nc, self.ctx = nc, ctx
        self.x = ctx.enter_context(nc.sbuf_tensor("x", [P, BATCHES * EMBED], F32))
        self.mean = ctx.enter_context(nc.sbuf_tensor("mean", [P, BATCHES], F32))
        self.variance = ctx.enter_context(nc.sbuf_tensor("variance", [P, BATCHES], F32))
        self.rstd = ctx.enter_context(nc.sbuf_tensor("rstd", [P, BATCHES], F32))
        self.minus_half = ctx.enter_context(nc.sbuf_tensor("minus_half", [P, BATCHES], F32))
        self.ident = ctx.enter_context(nc.sbuf_tensor("ident", [P, P], F32))
        self.ident_bf = ctx.enter_context(nc.sbuf_tensor("ident_bf", [P, P], BF16))
        self.minus_ident_bf = ctx.enter_context(nc.sbuf_tensor("minus_ident_bf", [P, P], BF16))
        self.ones_bf = ctx.enter_context(nc.sbuf_tensor("ones_bf", [P, P], BF16))
        self.ones = ctx.enter_context(nc.sbuf_tensor("ones", [P, P], F32))
        self.region = [ctx.enter_context(nc.sbuf_tensor("weights_even", [P, 10240], F32)),
                       ctx.enter_context(nc.sbuf_tensor("weights_odd", [P, 12288], F32))]
        self.banks = [ctx.enter_context(nc.psum_tensor(f"bank{n}", [P, 512], F32)) for n in range(8)]
        self.semaphores = [[ctx.enter_context(nc.semaphore(f"layer_{parity}_{k}")) for k in range(SEMAPHORES)]
                           for parity in ("even", "odd")]
        self.x_loaded = [ctx.enter_context(nc.semaphore(f"x_loaded_{c}")) for c in range(4)]
        self.weights_loaded = [ctx.enter_context(nc.semaphore(f"weights_loaded_{n}")) for n in range(6)]

    def batch_x(self, b):
        return self.x[:, bass.ds(b * EMBED, EMBED)]

    def column(self, tensor, b):
        return tensor[:, bass.ds(b, 1)]


class Layer:

    def __init__(self, core, n, name, ctx):
        self.parity, self.used = n % 2, 0
        self.core, self.nc, self.name, self.ctx = core, core.nc, name, ctx
        self.h = self.sbuf("h", [P, EMBED], F32)
        self.hT = self.sbuf("hT", [P, EC, P], F32)
        self.new_x = self.sbuf("new_x", [P, EMBED], F32)
        self.stats = self.sbuf("stats", [P, 6], F32)
        self.mean_var = self.sbuf("mean_var", [P, 2], F32)
        self.h_ready = self.sem("h_ready")
        self.hT_filled = self.sem("hT_filled")
        self.hT_ready = self.sem("hT_ready")
        self.y_filled = self.sem("y_filled")
        self.x_updated = self.sem("x_updated")
        self.tail_chain = self.sem("tail_chain")

    def sbuf(self, name, shape, dtype=F32):
        return self.ctx.enter_context(self.nc.sbuf_tensor(f"{self.name}_{name}", shape, dtype))

    def sem(self, name):
        self.used += 1
        return self.core.semaphores[self.parity][self.used - 1]

    def clear_last_layers_semaphores(self, sp):
        last = [s.num for s in self.core.semaphores[1 - self.parity]]
        assert last == list(range(last[0], last[0] + SEMAPHORES))
        sp.sem_clear(range(last[0], last[0] + SEMAPHORES))

    def pool_rstd(self, pool, b, steps):
        pool.wait_ge(self.tail_chain, steps * (b + 1))
        pool.tensor_tensor(self.core.column(self.core.rstd, b), self.core.column(self.core.variance, b),
                           self.core.minus_half[:, 0:1], ALU.pow)

    def dve_normalise(self, dve, b):
        dve.wait_ge(self.hT_filled, nonneg(b))
        dve.tensor_scalar(self.h[:, :], self.core.batch_x(b), self.core.column(self.core.mean, b),
                          self.core.column(self.core.rstd, b), ALU.subtract, ALU.mult)\
           .then_inc(self.h_ready, 1)

    def pe_transpose_h(self, pe, b, bank):
        pe.wait_ge(self.h_ready, b + 1)
        for c in range(EC):
            last = pe.transpose(bank[:, c * P:(c + 1) * P], self.h[:, c * P:(c + 1) * P],
                                self.core.ident[:, :])
        last.then_inc(self.hT_filled, 1)

    def act_copy_hT(self, act, b, bank):
        act.wait_ge(self.hT_filled, b + 1)
        act.activation(self.hT[:, :, :], bank[:, 0:EMBED].rearrange("p (c t) -> p c t", c=EC),
                       ACT.Copy).then_inc(self.hT_ready, 1)

    def dve_update_x(self, dve, b, y, chain, scale=None):
        dve.wait_ge(self.y_filled, b + 1)
        x = self.core.batch_x(b)
        if scale is None:
            update = dve.tensor_tensor(self.new_x[:, :], x, y, ALU.add)
        else:
            update = dve.scalar_tensor_tensor(self.new_x[:, :], y, scale, x, ALU.mult, ALU.add)
        update.then_inc(self.x_updated, 1)
        dve.wait_ge(self.x_updated, b + 1)
        self.dve_statistics(dve, b, chain)

    def dve_statistics(self, dve, b, chain):
        chain(dve.bn_stats(self.stats[:, :], self.new_x[:, :]))
        dve.tensor_scalar(self.core.batch_x(b), self.new_x[:, :], 1.0, None, ALU.mult)
        chain(dve.bn_aggr(self.mean_var[:, :], self.stats[:, :]))
        dve.tensor_scalar(self.core.column(self.core.mean, b), self.mean_var[:, 0:1], 1.0, None, ALU.mult)
        chain(dve.tensor_scalar(self.core.column(self.core.variance, b), self.mean_var[:, 1:2], LN_EPS,
                                None, ALU.add))


STATISTICS_STEPS = 3


def setup(nc, core, x_dram, ident_dram, weights):
    with ExitStack() as ctx:
        layer = Layer(core, 1, "setup", ctx)
        ident_loaded = layer.sem("ident_loaded")
        made = layer.sem("made")
        block = ctx.enter_context(nc.Block())

        CHUNKS = 4
        PER = BATCHES // CHUNKS
        stats = layer.sbuf("all_stats", [P, BATCHES, 6])
        mean_var = layer.sbuf("all_mean_var", [P, BATCHES, 2])
        stats_ready, mean_var_ready = layer.sem("stats_ready"), layer.sem("mean_var_ready")
        variance_ready = layer.sem("variance_ready")

        @block.sync
        def _(sp):
            for c in range(CHUNKS):
                batches = slice(c * PER, (c + 1) * PER)
                sp.dma_start(core.x[:, :].rearrange("p (b e) -> p b e", b=BATCHES)[:, batches, :],
                             x_dram[batches].rearrange("b p e -> p b e")).then_inc(core.x_loaded[c], 16)
                if c == 0:
                    sp.dma_start(core.ident[:, :], ident_dram).then_inc(ident_loaded, 16)
            load_weights(sp, core, 0, weights[0])

        @block.gpsimd
        def _(pool):
            pool.memset(core.minus_half[:, :], -0.5)
            pool.memset(core.ones_bf[:, :], 1.0)
            pool.memset(core.ones[:, :], 1.0).then_inc(made, 1)
            pool.wait_ge(made, 1)
            pool.wait_ge(variance_ready, 1)
            pool.tensor_tensor(core.rstd[:, :], core.variance[:, :], core.minus_half[:, :], ALU.pow)

        @block.scalar
        def _(act):
            act.wait_ge(ident_loaded, 16)
            act.activation(core.ident_bf[:, :], core.ident[:, :], ACT.Copy)
            act.activation(core.minus_ident_bf[:, :], core.ident[:, :], ACT.Copy, scale=-1.0)

        @block.vector
        def _(dve):
            for b in range(BATCHES):
                if b % PER == 0:
                    dve.wait_ge(core.x_loaded[b // PER], 16)
                last = dve.bn_stats(stats[:, b, :], core.batch_x(b))
            last.then_inc(stats_ready, 1)
            dve.wait_ge(stats_ready, 1)
            for b in range(BATCHES):
                last = dve.bn_aggr(mean_var[:, b, :], stats[:, b, :])
            last.then_inc(mean_var_ready, 1)
            dve.wait_ge(mean_var_ready, 1)
            dve.tensor_scalar(core.mean[:, :].unsqueeze(2), mean_var[:, :, 0:1], 1.0, None, ALU.mult)
            dve.tensor_scalar(core.variance[:, :].unsqueeze(2), mean_var[:, :, 1:2], LN_EPS, None, ALU.add)\
               .then_inc(variance_ready, 1)


def load_weights(sp, core, n, dram, parts=2):
    columns = dram.shape[1]
    for k in range(parts):
        a, e = columns * k // parts, columns * (k + 1) // parts
        sp.dma_start(core.region[n % 2][:, a:e], dram[:, a:e], max_dma_last_dim=8192)\
          .then_inc(core.weights_loaded[n], 16)
    return parts


WEIGHT_PARTS = 2


SPLIT_COLUMNS = 8192


def causal_attention(nc, core, dram, weights, next_weights, high_weights, low_weights):
    HEADS, D = 16, 16
    GROUPS = 4
    PER = HEADS // GROUPS
    SCALE = float(D) ** -0.5
    VW = D + 1
    ROWS = PER * D // EC
    SLOT_HEADS = ROWS // D
    STACK = len(PARTS) * ROWS
    n = 0
    with ExitStack() as ctx:
        layer = Layer(core, n, "causal", ctx)
        sem, sbuf = layer.sem, layer.sbuf
        region = core.region[n]
        w = region[:, 0:6 * EC * EMBED].rearrange("p (k c n) -> p k c n", k=6, c=EC)
        wq, wq_swapped, wk, wk_swapped, wv, wo = (w[:, k] for k in range(6))
        constants = sbuf("constants", [P, dram["causal_constants"].shape[1]])
        cosine, sine = constants[:, 0:EC * P], constants[:, EC * P:2 * EC * P]
        later, earlier = (constants[:, (2 * EC + k) * P:(2 * EC + k + 1) * P] for k in range(2))
        parity = constants[:, (2 * EC + 2) * P:]
        mask_qk = sbuf("mask_qk", [P, P], BF16)
        mask_kq = sbuf("mask_kq", [P, P], BF16)
        spare = 6 * EC * EMBED

        def place(columns, pattern=None, **sizes):
            nonlocal spare
            part = region[:, spare:spare + columns]
            spare += columns
            assert spare <= region.shape[1]
            return part.rearrange(pattern, **sizes) if pattern else part
        q_cos, q_sin, k_cos, k_sin = (place(EC * P) for _ in range(4))
        qT = [place(EC * P, "p (c t) -> p c t", c=EC) for s in range(2)]
        qT_bf = [sbuf(f"qT_bf{s}", [P, EC, P], BF16) for s in range(2)]
        q_halves = place(2 * EC * P, "p (x c t) -> p x c t", x=2, c=EC)
        k_high = place(EC * P, "p (c t) -> p c t", c=EC)
        q_stack = place(EC * GROUPS * P, "p (c s t) -> p c s t", c=EC, s=GROUPS)[0:STACK]
        k_stack = [sbuf(f"k_stack{s}", [STACK, EC, GROUPS, P], F32R) for s in range(2)]
        q_own = [sbuf(f"q_own{s}", [STACK, EC * GROUPS, SLOT_HEADS, P], F32R) for s in range(2)]
        kT = [place(EC * P, "p (c t) -> p c t", c=EC) for s in range(2)]
        kT_bf = [sbuf(f"kT_bf{s}", [P, EC, 2, P], BF16) for s in range(2)]
        values = [sbuf(f"values{s}", [P, HEADS, VW]) for s in range(2)]
        maxima = [sbuf(f"maxima{s}", [P, GROUPS, PER], BF16) for s in range(2)]
        probs = place(GROUPS * PER * P, "p (g x) -> p g x", g=GROUPS)
        reciprocal = sbuf("reciprocal", [P, HEADS])
        SLICE = SPLIT_COLUMNS // BATCHES
        to_split = core.region[n + 1]
        high_slice = [place(SLICE) for s in range(2)]
        heads = sbuf("heads", [P, HEADS, D])
        headsT = sbuf("headsT", [P, EC, P])

        bank_hv, bank_q, bank_k = core.banks[0:3]
        bank_scores, bank_scoresT, bank_out = core.banks[3:5], core.banks[5:7], core.banks[7]
        half_tail = bank_hv[:, EMBED:2 * EMBED]

        constants_loaded = sem("constants_loaded")
        constants_ready = sem("constants_ready")
        q_filled, q_read = sem("q_filled"), sem("q_read")
        k_filled, k_read = sem("k_filled"), sem("k_read")
        q_ready = sem("q_ready")
        halves_chain, q_halves_ready = sem("halves_chain"), sem("q_halves_ready")
        q_stacked, k_stacked = sem("q_stacked"), sem("k_stacked")
        q_own_ready = sem("q_own_ready")
        k_ready, k_bf_ready = sem("k_ready"), sem("k_bf_ready")
        v_filled, v_ready = sem("v_filled"), sem("v_ready")
        scores_filled, max_ready = sem("scores_filled"), sem("max_ready")
        scoresT_filled, probs_ready = sem("scoresT_filled"), sem("probs_ready")
        out_filled = sem("out_filled")
        heads_ready, headsT_filled, headsT_ready = sem("heads_ready"), sem("headsT_filled"), sem("headsT_ready")
        heads_chain = sem("heads_chain")
        weights_high, weights_low, weights_split = sem("weights_high"), sem("weights_low"), sem("weights_split")
        block = ctx.enter_context(nc.Block())

        def slice_of(tensor, b):
            return tensor[:, bass.ds(b * SLICE, SLICE)]

        @block.sync
        def _(sp):
            layer.clear_last_layers_semaphores(sp)
            sp.dma_start(constants[:, :], dram["causal_constants"]).then_inc(constants_loaded, 16)
            load_weights(sp, core, n + 1, next_weights)

        @block.gpsimd
        def _(pool):
            for s in range(2):
                pool.memset(values[s][:, :, D:VW], 1.0)
            pool.wait_ge(constants_loaded, 16)
            pool.tensor_copy(mask_qk[:, :], later[:, :])
            pool.tensor_copy(mask_kq[:, :], earlier[:, :]).then_inc(constants_ready, 1)

            def step(t, s, front, middle, tail):
                if front:
                    b = t
                    pool.wait_ge(q_read, b + 1)
                    pool.wait_ge(scoresT_filled, nonneg(GROUPS * (b - 1)))
                    pool.tensor_tensor(qT[s][:, :, :], q_cos[:, :], q_sin[:, :], ALU.add)
                    pool.tensor_tensor(qT_bf[s][:, :, :], q_cos[:, :], q_sin[:, :], ALU.add)\
                        .then_inc(q_ready, 1)
                    pool.wait_ge(k_read, b + 1)
                    pool.tensor_tensor(kT[s][:, :, :], k_cos[:, :], k_sin[:, :], ALU.add).then_inc(k_ready, 1)
                    pool.wait_ge(k_ready, b + 1)
                    for h in range(2):
                        last = pool.tensor_tensor(kT_bf[s][:, :, h, :], kT[s][:, :, :],
                                                  parity[:, h:h + 1].unsqueeze(2).to_broadcast([P, EC, P]), ALU.mult)
                    last.then_inc(k_bf_ready, 1)
                if tail:
                    b = t - 2
                    layer.pool_rstd(pool, b, STATISTICS_STEPS)
                    part = slice_of(to_split, b)
                    pool.wait_ge(weights_high, b + 1)
                    pool.tensor_tensor(slice_of(low_weights, b), part, high_slice[s][:, :], ALU.subtract)\
                        .then_inc(weights_low, 1)
                    pool.wait_ge(weights_low, b + 1)
                    pool.tensor_tensor(slice_of(high_weights, b), part, slice_of(low_weights, b).bitcast(F32),
                                       ALU.subtract)\
                        .then_inc(weights_split, 1)
            pipeline(pool, step)

        @block.scalar
        def _(act):

            def step(t, s, front, middle, tail):
                if front:
                    act.wait_ge(v_filled, nonneg(t))
                    layer.act_copy_hT(act, t, bank_hv)

                def stack_queries(slot):
                    for k, (_, half) in enumerate(PARTS):
                        last = act.activation(q_stack[ROWS * k:ROWS * (k + 1), :, slot, :],
                                              q_halves[ROWS * slot:ROWS * (slot + 1), half, :, :], ACT.Copy)
                    last.then_inc(q_stacked, 1)

                def own_queries(h):
                    act.activation(q_own[s][:, :, h, :], q_stack[:, :, :, :].rearrange("p c s t -> p (c s) t"), ACT.Copy,
                                   scale=parity[0:STACK, h:h + 1]).then_inc(q_own_ready, 1)

                def exponentials(g):
                    i = GROUPS * (t - 1) + g
                    act.wait_ge(scoresT_filled, i + 1)
                    act.wait_ge(out_filled, nonneg(i - GROUPS + 1))
                    act.activation(probs[:, g, :], bank_scoresT[g % 2][:, :], ACT.Exp, scale=SCALE)\
                       .then_inc(probs_ready, 1)
                if middle:
                    exponentials(0)
                    exponentials(1)
                if tail:
                    b = t - 2
                    act.wait_ge(headsT_filled, b + 1)
                    act.wait_ge(layer.y_filled, nonneg(b))
                    act.activation(headsT[:, :, :], half_tail.rearrange("p (c t) -> p c t", c=EC),
                                   ACT.Copy).then_inc(headsT_ready, 1)
                if front:
                    b = t
                if front:
                    act.wait_ge(q_halves_ready, b + 1)
                    act.wait_ge(q_own_ready, nonneg(SLOT_HEADS * b))
                    stack_queries(0)
                    stack_queries(1)
                if middle:
                    exponentials(2)
                if front:
                    stack_queries(2)
                    stack_queries(3)
                if middle:
                    exponentials(3)
                if front:
                    act.wait_ge(constants_loaded, 16)
                    act.wait_ge(scoresT_filled, nonneg(GROUPS * (b - 1)))
                    act.wait_ge(q_stacked, GROUPS * (b + 1))
                    own_queries(0)
                    own_queries(1)
                    act.wait_ge(v_filled, b + 1)
                    act.wait_ge(out_filled, nonneg(GROUPS * (b - 1)))
                    act.activation(values[s][:, :, 0:D], bank_hv[:, 0:EMBED].rearrange("p (h d) -> p h d", h=HEADS),
                                   ACT.Copy).then_inc(v_ready, 1)
            pipeline(act, step)

        @block.vector
        def _(dve):
            heads_step = Chain(dve, heads_chain, 1)
            tail_step = Chain(dve, layer.tail_chain, STATISTICS_STEPS)

            def step(t, s, front, middle, tail):
                if front:
                    layer.dve_normalise(dve, t)

                def row_maxima(g):
                    i = GROUPS * (t - 1) + g
                    dve.wait_ge(scores_filled, i + 1)
                    dve.wait_ge(scoresT_filled, nonneg(GROUPS * (t - 2)))
                    dve.tensor_reduce(maxima[1 - s][:, g, :], bank_scores[g % 2].rearrange("p (h k) -> p h k", h=PER),
                                      AX.X, ALU.max).then_inc(max_ready, 1)

                def stack_keys(s, slot):
                    rows = slice(ROWS * slot, ROWS * (slot + 1))
                    for k, (half, _) in enumerate(PARTS):
                        to = k_stack[s][ROWS * k:ROWS * (k + 1), :, slot, :]
                        if half == 0:
                            last = dve.tensor_scalar(to, k_high[rows, :, :], 1.0, None, ALU.mult)
                        else:
                            last = dve.tensor_tensor(to, kT[s][rows, :, :], k_high[rows, :, :], ALU.subtract)
                    last.then_inc(k_stacked, 1)

                def turn(bank, filled, used, with_cos, with_sin, read):
                    dve.wait_ge(constants_loaded, 16)
                    dve.wait_ge(filled, t + 1)
                    dve.wait_ge(used, nonneg(t))
                    dve.tensor_tensor(with_cos[:, :], bank[:, 0:EC * P], cosine[:, :], ALU.mult)
                    dve.tensor_tensor(with_sin[:, :], bank[:, EC * P:2 * EC * P], sine[:, :], ALU.mult)\
                       .then_inc(read, 1)
                if middle:
                    row_maxima(0)
                    row_maxima(1)
                    stack_keys(1 - s, 2)
                    stack_keys(1 - s, 3)
                if tail:
                    b = t - 2
                    heads_step.start(b)
                    dve.wait_ge(out_filled, GROUPS * (b + 1))
                    out = bank_out[:, 0:HEADS * VW].rearrange("p (h d) -> p h d", h=HEADS)
                    heads_step(dve.reciprocal(reciprocal[:, :].unsqueeze(2), out[:, :, D:VW]))
                    dve.wait_ge(headsT_filled, nonneg(b))
                    dve.tensor_tensor(heads[:, :, :], out[:, :, 0:D],
                                      reciprocal[:, :].unsqueeze(2).to_broadcast([P, HEADS, D]), ALU.mult)\
                       .then_inc(heads_ready, 1)
                if middle:
                    row_maxima(2)
                if front:
                    turn(bank_q, q_filled, q_ready, q_cos, q_sin, q_read)
                if middle:
                    row_maxima(3)
                if front:
                    high, low = (q_halves[:, half, :, :] for half in range(2))
                    dve.wait_ge(q_ready, t + 1)
                    dve.wait_ge(q_stacked, nonneg(GROUPS * t))
                    dve.tensor_scalar(high.bitcast(I32), qT[s][:, :, :].bitcast(I32), HIGH_BITS, None,
                                      ALU.bitwise_and).then_inc(halves_chain, 1)
                    dve.wait_ge(halves_chain, 2 * t + 1)
                    dve.tensor_tensor(low, qT[s][:, :, :], high, ALU.subtract).then_inc(q_halves_ready, 1)
                    turn(bank_k, k_filled, k_ready, k_cos, k_sin, k_read)
                    dve.wait_ge(k_ready, t + 1)
                    dve.wait_ge(k_stacked, nonneg(GROUPS * t))
                    dve.tensor_scalar(k_high[:, :, :].bitcast(I32), kT[s][:, :, :].bitcast(I32), HIGH_BITS, None,
                                      ALU.bitwise_and).then_inc(halves_chain, 1)
                    dve.wait_ge(halves_chain, 2 * t + 2)
                    stack_keys(s, 0)
                if tail:
                    tail_step.start(t - 2)
                    layer.dve_update_x(dve, t - 2, half_tail, tail_step)
                if front:
                    stack_keys(s, 1)
                if tail:
                    b = t - 2
                    if isinstance(t, int) and t == 2:
                        dve.wait_ge(core.weights_loaded[n + 1], 16 * WEIGHT_PARTS)
                    dve.wait_ge(weights_low, nonneg(b - 1))
                    dve.tensor_scalar(high_slice[s][:, :].bitcast(I32), slice_of(to_split, b).bitcast(I32), HIGH_BITS,
                                      None, ALU.bitwise_and).then_inc(weights_high, 1)
            pipeline(dve, step)

        @block.tensor
        def _(pe):
            pe.wait_ge(core.weights_loaded[n], 16 * WEIGHT_PARTS)

            def step(t, s, front, middle, tail):
                def scores(g):
                    i = GROUPS * (t - 1) + g
                    pe.wait_ge(max_ready, nonneg(i - 1))
                    rows = slice(32 * g, 32 * g + 32)
                    pe.matmul(bank_scores[g % 2][:, :], core.ident_bf[:, :], mask_qk[:, :].unsqueeze(1).to_broadcast([P, PER, P]),
                              start=True, stop=False)
                    for c in range(EC):
                        last = pe.matmul(bank_scores[g % 2][:, 2 * c * P:2 * (c + 1) * P], qT_bf[1 - s][rows, c, :],
                                         kT_bf[1 - s][rows, c, :, :], start=False, stop=(c == EC - 1))
                    last.then_inc(scores_filled, 1)

                def scores_transposed(g):
                    i = GROUPS * (t - 1) + g
                    pe.wait_ge(k_stacked, i + 1)
                    pe.wait_ge(max_ready, i + 1)
                    pe.wait_ge(probs_ready, nonneg(i - 1))
                    bank = bank_scoresT[g % 2]
                    pe.matmul(bank[:, :], core.ident_bf[:, :], mask_kq[:, :].unsqueeze(1).to_broadcast([P, PER, P]),
                              start=True, stop=False)
                    for j in range(PER):
                        pe.matmul(bank[:, j * P:(j + 1) * P], maxima[1 - s][:, g, j:j + 1].to_broadcast([P, P]),
                                  core.minus_ident_bf[:, :], start=False, stop=False)
                    for c in range(EC):
                        last = pe.matmul(bank[:, 2 * c * P:2 * (c + 1) * P], k_stack[1 - s][:, c, g, :],
                                         q_own[1 - s][:, c * GROUPS + g, :, :], start=False, stop=(c == EC - 1))
                    last.then_inc(scoresT_filled, 1)

                def weigh_values(g, b=t - 1, s=1 - s):
                    i = GROUPS * b + g
                    pe.wait_ge(probs_ready, i + 1)
                    for j in range(PER):
                        h = (j // 2 * GROUPS + g) * 2 + j % 2
                        last = pe.matmul(bank_out[:, h * VW:(h + 1) * VW], probs[:, g, j * P:(j + 1) * P],
                                         values[s][:, h, :], start=True, stop=True)
                    last.then_inc(out_filled, 1)

                def project(bank, weights):
                    for k, wt in enumerate(weights):
                        for m in range(EC):
                            at = (k * EC + m) * P
                            for c in range(EC):
                                last = pe.matmul(bank[:, at:at + P], wt[:, c, m * P:(m + 1) * P], layer.hT[:, c, :],
                                                 start=(c == 0), stop=(c == EC - 1))
                    return last

                if middle:
                    pe.wait_ge(constants_ready, 1)
                    pe.wait_ge(q_ready, nonneg(t))
                    pe.wait_ge(k_bf_ready, nonneg(t))
                    scores(0)
                    scores(1)
                if tail:
                    weigh_values(3, t - 2, s)
                if front:
                    pe.wait_ge(v_ready, nonneg(t))
                    layer.pe_transpose_h(pe, t, bank_hv)
                if middle:
                    pe.wait_ge(q_own_ready, nonneg(SLOT_HEADS * t))
                    scores_transposed(0)
                    scores(2)
                if front:
                    pe.wait_ge(layer.hT_ready, t + 1)
                    pe.wait_ge(q_read, nonneg(t))
                    project(bank_q, (wq, wq_swapped)).then_inc(q_filled, 1)
                if middle:
                    scores_transposed(1)
                    scores(3)
                    pe.wait_ge(v_ready, nonneg(t))
                if tail:
                    pe.wait_ge(heads_ready, nonneg(t - 1))
                    pe.wait_ge(layer.x_updated, nonneg(t - 2))
                    flat = heads[:, :, :].rearrange("p h d -> p (h d)")
                    for c in range(EC):
                        last = pe.transpose(half_tail[:, c * P:(c + 1) * P], flat[:, c * P:(c + 1) * P],
                                            core.ident[:, :])
                    last.then_inc(headsT_filled, 1)
                if middle:
                    pe.wait_ge(heads_ready, nonneg(t - 1))
                    weigh_values(0)
                if front:
                    pe.wait_ge(k_read, nonneg(t))
                    project(bank_k, (wk, wk_swapped)).then_inc(k_filled, 1)
                if middle:
                    scores_transposed(2)
                    weigh_values(1)
                if tail:
                    pe.wait_ge(headsT_ready, nonneg(t - 1))
                    for c in range(EC):
                        last = pe.matmul(half_tail, headsT[:, c, :], wo[:, c, :],
                                         start=(c == 0), stop=(c == EC - 1))
                    last.then_inc(layer.y_filled, 1)
                if middle:
                    scores_transposed(3)
                    weigh_values(2)
                if front:
                    pe.wait_ge(layer.x_updated, nonneg(t - 1))
                    for c in range(EC):
                        last = pe.matmul(bank_hv[:, 0:EMBED], layer.hT[:, c, :], wv[:, c, :],
                                         start=(c == 0), stop=(c == EC - 1))
                    last.then_inc(v_filled, 1)
            pipeline(pe, step)


BLOCK = 32
FP8_MAX, LEAST_SCALE = 448.0, 1e-30
LEAST_NORMAL = 2.0 ** -6
ROUNDER = 1.5 * 2.0 ** 20
EXPONENT_BITS = 0x7F800000


class Scratch:

    def __init__(self, layer, name, columns):
        blocks = columns // BLOCK
        self.columns, self.blocks = columns, blocks
        self.largest, self.scale, self.inverse = (layer.sbuf(f"{name}_{x}", [P, blocks])
                                                  for x in ("largest", "scale", "inverse"))
        self.scaled = layer.sbuf(f"{name}_scaled", [P, columns])
        self.rounder = layer.sbuf(f"{name}_rounder", [P, columns])


def dve_scale(dve, source, scratch, step, least, done):
    step(dve.tensor_reduce(scratch.largest[:, :], source.rearrange("p (b k) -> p b k", k=BLOCK), AX.X,
                           ALU.max, apply_absolute_value=True))
    step(dve.tensor_scalar(scratch.scale[:, :], scratch.largest[:, :], 1.0 / FP8_MAX, least, ALU.mult, ALU.max))
    step(dve.reciprocal(scratch.inverse[:, :], scratch.scale[:, :]))
    step(dve.tensor_tensor(scratch.scaled[:, :].rearrange("p (b k) -> p b k", k=BLOCK),
                           source.rearrange("p (b k) -> p b k", k=BLOCK),
                           scratch.inverse[:, :].unsqueeze(2).to_broadcast([P, scratch.blocks, BLOCK]), ALU.mult))
    step(dve.tensor_scalar(scratch.rounder[:, :].bitcast(I32), scratch.scaled[:, :].bitcast(I32), EXPONENT_BITS, None,
                           ALU.bitwise_and))
    dve.tensor_scalar(scratch.rounder[:, :], scratch.rounder[:, :], LEAST_NORMAL, ROUNDER, ALU.max, ALU.mult)\
       .then_inc(done, 1)


def pool_round(pool, scratch, out, step, done):
    step(pool.tensor_tensor(scratch.scaled[:, :], scratch.scaled[:, :], scratch.rounder[:, :], ALU.add))
    step(pool.tensor_tensor(scratch.scaled[:, :], scratch.scaled[:, :], scratch.rounder[:, :], ALU.subtract))
    pool.tensor_tensor(out.rearrange("p (b k) -> p b k", k=BLOCK),
                       scratch.scaled[:, :].rearrange("p (b k) -> p b k", k=BLOCK),
                       scratch.scale[:, :].unsqueeze(2).to_broadcast([P, scratch.blocks, BLOCK]), ALU.mult)\
        .then_inc(done, 1)


def cross_attention(nc, core, n, dram, next_weights, normed, split_weights=None):
    HEADS, D = 16, P
    KV_HEADS = HEADS if normed else HEADS // 2
    SHARE = HEADS // KV_HEADS
    GROUPS = 4
    PER = HEADS // GROUPS
    KV_GROUPS = KV_HEADS // PER
    VW = D + 1
    SCALE = float(D) ** -0.5
    RMS_EPS = 1e-5
    LEAST_SUM = 1e-30
    with ExitStack() as ctx:
        layer = Layer(core, n, f"cross{n}", ctx)
        sem, sbuf = layer.sem, layer.sbuf
        region = core.region[n % 2]
        at = 0

        def weight(columns, pattern=None, **sizes):
            nonlocal at
            part = region[:, at:at + columns]
            at += columns
            return part.rearrange(pattern, **sizes) if pattern else part
        wq = weight(EC * HEADS * D, "p (c n) -> p c n", c=EC)
        wk = weight(KV_HEADS * D)
        wv = weight(KV_HEADS * D)
        wo = weight(HEADS * EMBED, "p (h n) -> p h n", h=HEADS)

        context = [sbuf(f"context{s}", [P, P]) for s in range(2)]
        contextT = sbuf("contextT", [P, P])
        if normed:
            qT, kT, probs, headsT = (region[:, k * HEADS * P:(k + 1) * HEADS * P].rearrange("p (h t) -> p h t", h=HEADS)
                                     for k in range(SPLIT_COLUMNS // (HEADS * P)))
        else:
            qT, kT = sbuf("qT", [P, HEADS, P]), sbuf("kT", [P, KV_HEADS, P])
            probs, headsT = sbuf("probs", [P, HEADS, P]), sbuf("headsT", [P, HEADS, P])
        qT_bf, kT_bf = sbuf("qT_bf", [P, HEADS, P], BF16), sbuf("kT_bf", [P, KV_HEADS, P], BF16)
        values = sbuf("values", [P, KV_HEADS, VW])
        maxima = [sbuf(f"maxima{s}", [P, HEADS], BF16) for s in range(2)]
        sums = sbuf("sums", [P, HEADS])
        reciprocal = sbuf("reciprocal", [P, HEADS])
        heads = [sbuf(f"heads{s}", [P, PER, D]) for s in range(2)]
        if normed:
            turned_h = sbuf("turned_h", [P, EC + 1, P])
            high = sbuf("high", [P, EC + 1, P])
            halves = [sbuf(f"halves{x}", [P, EC + 1, P], F32R) for x in range(2)]
            q_scaled, k_scaled = sbuf("q_scaled", [P, PER, D]), sbuf("k_scaled", [P, PER, D])
            squares = [sbuf(f"squares_{x}", [P, PER, D], BF16) for x in "qk"]
            mean_q, mean_k = sbuf("mean_q", [P, HEADS]), sbuf("mean_k", [P, HEADS])
            mean_eps = [sbuf(f"mean_eps_{x}", [P, HEADS]) for x in "qk"]
            rms_q, rms_k = sbuf("rms_q", [P, HEADS]), sbuf("rms_k", [P, HEADS])
            eps = sbuf("eps", [P, PER])
            gains = sbuf("gains", [P, 2])
            gain = sbuf("gain", [P, 1])
        else:
            mask = sbuf("mask", [P, BATCHES], mybir.dt.uint8)
            key_bias = sbuf("key_bias", [P, BATCHES])
            batch_bias = [sbuf(f"batch_bias{s}", [P, 1]) for s in range(2)]
            mask_diagonal = [sbuf(f"mask_diagonal{s}", [P, P], BF16) for s in range(2)]
            to_quantise = core.region[(n + 1) % 2]
            SLICE = 3 * EC * 1024 // BATCHES
            scratch = [Scratch(layer, f"weights{s}", SLICE) for s in range(2)]
            scale_chain, round_chain = sem("scale_chain"), sem("round_chain")
            slice_scaled, slice_rounded = sem("slice_scaled"), sem("slice_rounded")

        bank_project, bank_turn, bank_scores, bank_scoresT = core.banks[0:2], core.banks[2], core.banks[3], core.banks[4]
        bank_out, bank_y = core.banks[5:7], core.banks[7]

        context_loaded = [sem(f"context_loaded{s}") for s in range(2)]
        small_loaded, small_ready = sem("small_loaded"), sem("small_ready")
        q_filled, k_filled, v_filled = sem("q_filled"), sem("k_filled"), sem("v_filled")
        q_summed, k_summed = sem("q_summed"), sem("k_summed")
        rms_q_ready, rms_k_ready = sem("rms_q_ready"), sem("rms_k_ready")
        q_read, k_read, v_ready = sem("q_read"), sem("k_read"), sem("v_ready")
        qT_filled, kT_filled = sem("qT_filled"), sem("kT_filled")
        qT_ready, kT_ready = sem("qT_ready"), sem("kT_ready")
        qT_bf_ready, kT_bf_ready = sem("qT_bf_ready"), sem("kT_bf_ready")
        scores_filled, max_ready = sem("scores_filled"), sem("max_ready")
        scoresT_filled, probs_ready = sem("scoresT_filled"), sem("probs_ready")
        out_filled = sem("out_filled")
        heads_ready, headsT_filled, headsT_ready = sem("heads_ready"), sem("headsT_filled"), sem("headsT_ready")
        halves_chain, halves_ready = sem("halves_chain"), sem("halves_ready")
        middle_chain, pool_chain, mask_ready = sem("middle_chain"), sem("pool_chain"), sem("mask_ready")
        block = ctx.enter_context(nc.Block())

        @block.sync
        def _(sp):
            layer.clear_last_layers_semaphores(sp)
            if normed:
                sp.dma_start(gains[:, :], dram["gains"]).then_inc(small_loaded, 16)
            else:
                sp.dma_start(mask[:, :], dram["mask"]).then_inc(small_loaded, 16)

            def step(t, s, front, middle, tail):
                if front:
                    sp.wait_ge(layer.hT_filled, nonneg(t - 1))
                    sp.dma_start(context[s][:, :], dram["context"][bass.ds(t, 1), :, :].rearrange("b p c -> (b p) c"))\
                      .then_inc(context_loaded[s], 16)
            step(0, 0, True, False, False)
            step(1, 1, True, False, False)
            if next_weights is not None:
                load_weights(sp, core, n + 1, next_weights)
            with sp.Fori(2, BATCHES - 1, 2) as t:
                step(t, 0, True, False, False)
                step(t + 1, 1, True, False, False)

        @block.gpsimd
        def _(pool):
            pool.memset(values[:, :, D:VW], 1.0)
            if normed:
                pool.memset(eps[:, :], RMS_EPS)
                pool.wait_ge(small_loaded, 16)
                pool.tensor_tensor(gain[:, :], gains[:, 0:1], gains[:, 1:2], ALU.mult).then_inc(small_ready, 1)
            else:
                pool.memset(reciprocal[:, :], 0.0).then_inc(small_ready, 1)
            eps_added = Chain(pool, pool_chain, 2 * GROUPS) if normed else None
            round_step = None if normed else Chain(pool, round_chain, 2)

            def step(t, s, front, middle, tail):
                if tail:
                    layer.pool_rstd(pool, t - 2, STATISTICS_STEPS)
                if front:
                    narrow_and_scale(t)
                if middle and not normed:
                    round_step.start(t - 1)
                    pool.wait_ge(slice_scaled, t)
                    pool_round(pool, scratch[1 - s], to_quantise[:, bass.ds((t - 1) * SLICE, SLICE)], round_step,
                               slice_rounded)

            def narrow_and_scale(b):

                def rms(summed, mean, mean_eps, out, ready, g):
                    cols = slice(g * PER, (g + 1) * PER)
                    pool.wait_ge(summed, GROUPS * b + g + 1)
                    pool.wait_ge(q_read, nonneg(GROUPS * (b - 1) + g + 1))
                    pool.wait_ge(k_read, nonneg(GROUPS * (b - 1) + g + 1))
                    eps_added(pool.tensor_tensor(mean_eps[:, cols], mean[:, cols], eps[:, :], ALU.add))
                    pool.tensor_tensor(out[:, cols], mean_eps[:, cols], core.minus_half[:, 0:PER], ALU.pow)\
                        .then_inc(ready, 1)

                def narrow(source, ready, to, done, g, groups):
                    pool.wait_ge(ready, groups * b + g + 1)
                    pool.wait_ge(scores_filled, nonneg(GROUPS * (b - 1) + (g + 1) * (GROUPS // groups)))
                    pool.tensor_tensor(to[:, g * PER:(g + 1) * PER, :], source[:, g * PER:(g + 1) * PER, :],
                                       core.ones[:, 0:1].unsqueeze(2).to_broadcast([P, PER, P]), ALU.mult)\
                        .then_inc(done, 1)
                if normed:
                    eps_added.start(b)
                for g in range(GROUPS):
                    if normed:
                        rms(q_summed, mean_q, mean_eps[0], rms_q, rms_q_ready, g)
                        if g:
                            narrow(qT, qT_ready, qT_bf, qT_bf_ready, g - 1, GROUPS)
                            narrow(kT, kT_ready, kT_bf, kT_bf_ready, g - 1, GROUPS)
                        rms(k_summed, mean_k, mean_eps[1], rms_k, rms_k_ready, g)
                    else:
                        narrow(qT, qT_ready, qT_bf, qT_bf_ready, g, GROUPS)
                        if g % 2:
                            narrow(kT, kT_ready, kT_bf, kT_bf_ready, g // 2, KV_GROUPS)
                if normed:
                    narrow(qT, qT_ready, qT_bf, qT_bf_ready, GROUPS - 1, GROUPS)
                    narrow(kT, kT_ready, kT_bf, kT_bf_ready, GROUPS - 1, GROUPS)
            pipeline(pool, step)

        @block.scalar
        def _(act):
            act.wait_ge(small_ready, 1)

            def step(t, s, front, middle, tail):
                def heads_to_sbuf(b, g):
                    act.wait_ge(headsT_filled, GROUPS * b + g + 1)
                    if g == 0:
                        act.wait_ge(layer.y_filled, nonneg(b))
                    act.activation(headsT[:, g * PER:(g + 1) * PER, :], bank_turn.rearrange("p (h q) -> p h q", h=PER),
                                   ACT.Copy).then_inc(headsT_ready, 1)

                def exponentials(g):
                    i = GROUPS * (t - 1) + g
                    act.wait_ge(scoresT_filled, i + 1)
                    act.wait_ge(out_filled, nonneg(i - GROUPS + 1))
                    act.activation(probs[:, g * PER:(g + 1) * PER, :], bank_scoresT.rearrange("p (h q) -> p h q", h=PER),
                                   ACT.Exp, scale=SCALE, bias=0.0 if normed else batch_bias[1 - s][:, 0:1])\
                       .then_inc(probs_ready, 1)

                def mean_squares(filled, bank, squares, mean, summed, used, g):
                    i = GROUPS * t + g
                    act.wait_ge(filled, i + 1)
                    act.wait_ge(used, nonneg(i - GROUPS + 1))
                    act.wait_ge(summed, nonneg(i))
                    for j in range(PER):
                        last = act.activation(squares[:, j, :], bank[:, j * P:(j + 1) * P], ACT.Square,
                                              scale=float(D) ** -0.5,
                                              accum_out=mean[:, g * PER + j:g * PER + j + 1])
                    last.then_inc(summed, 1)

                def to_sbuf(filled, bank, to, ready, b, g, groups, scale=1.0):
                    act.wait_ge(filled, groups * b + g + 1)
                    act.wait_ge(scoresT_filled, nonneg(GROUPS * (b - 1) + (g + 1) * (GROUPS // groups)))
                    act.wait_ge(qT_bf_ready if to is qT else kT_bf_ready, nonneg(groups * (b - 1) + g + 1))
                    act.activation(to[:, g * PER:(g + 1) * PER, :], bank.rearrange("p (h q) -> p h q", h=PER),
                                   ACT.Copy, scale=scale).then_inc(ready, 1)

                def values_to_sbuf(g):
                    act.wait_ge(v_filled, KV_GROUPS * t + g + 1)
                    act.wait_ge(out_filled, nonneg(GROUPS * (t - 1) + (g + 1) * SHARE))
                    act.activation(values[:, g * PER:(g + 1) * PER, 0:D],
                                   bank_y.rearrange("p (h d) -> p h d", h=PER), ACT.Copy)\
                       .then_inc(v_ready, 1)

                if middle and normed:
                    to_sbuf(qT_filled, bank_turn, qT, qT_ready, t - 1, GROUPS - 1, GROUPS)
                if tail:
                    heads_to_sbuf(t - 2, GROUPS - 1)
                if middle and normed:
                    to_sbuf(kT_filled, bank_turn, kT, kT_ready, t - 1, GROUPS - 1, GROUPS, gain[:, 0:1])
                if front:
                    act.wait_ge(layer.hT_filled, t + 1)
                    act.wait_ge(v_filled, nonneg(KV_GROUPS * t))
                    if normed:
                        act.activation(turned_h[:, :, :], bank_turn[:, 0:EMBED + P].rearrange("p (c t) -> p c t", t=P),
                                       ACT.Copy).then_inc(layer.hT_ready, 1)
                    else:
                        act.activation(contextT[:, :], bank_turn[:, EMBED:EMBED + P], ACT.Copy)
                        act.activation(layer.hT[:, :, :], bank_turn[:, 0:EMBED].rearrange("p (c t) -> p c t", c=EC),
                                       ACT.Copy).then_inc(layer.hT_ready, 1)
                if middle:
                    exponentials(0)
                for g in range(GROUPS):
                    if front and normed:
                        if g:
                            to_sbuf(qT_filled, bank_turn, qT, qT_ready, t, g - 1, GROUPS)
                        mean_squares(q_filled, bank_project[0], squares[0], mean_q, q_summed, rms_q_ready, g)
                    if front and not normed:
                        to_sbuf(q_filled, bank_project[0], qT, qT_ready, t, g, GROUPS)
                    if middle and g < GROUPS - 1:
                        exponentials(g + 1)
                    if front and normed:
                        if g:
                            to_sbuf(kT_filled, bank_turn, kT, kT_ready, t, g - 1, GROUPS, gain[:, 0:1])
                        mean_squares(k_filled, bank_project[1], squares[1], mean_k, k_summed, rms_k_ready, g)
                    if front and not normed and g % 2:
                        to_sbuf(k_filled, bank_project[1], kT, kT_ready, t, g // 2, KV_GROUPS)
                    values_first = normed and g < GROUPS - 1
                    if front and values_first:
                        values_to_sbuf(g)
                    if middle and g:
                        heads_to_sbuf(t - 1, g - 1)
                    if front and not values_first and (g + 1) % SHARE == 0:
                        values_to_sbuf(g // SHARE)
            pipeline(act, step)

        @block.vector
        def _(dve):
            if not normed:
                dve.wait_ge(small_loaded, 16)
                dve.tensor_scalar(key_bias[:, :], mask[:, :], 1.0, -NEG, ALU.subtract, ALU.mult)\
                   .then_inc(mask_ready, 1)
                dve.wait_ge(mask_ready, 1)
            STEPS = 2 * GROUPS
            middle_step = Chain(dve, middle_chain, STEPS)
            tail_step = Chain(dve, layer.tail_chain, STATISTICS_STEPS)
            scale_step = None if normed else Chain(dve, scale_chain, 5)

            def step(t, s, front, middle, tail):
                def row_maxima(g):
                    i = GROUPS * (t - 1) + g
                    dve.wait_ge(scores_filled, i + 1)
                    dve.wait_ge(scoresT_filled, nonneg(GROUPS * (t - 2)))
                    with nc.allow_low_precision("the maximum only shifts a softmax's exponents"):
                        dve.tensor_reduce(maxima[1 - s][:, g * PER:(g + 1) * PER],
                                          bank_scores.rearrange("p (h k) -> p h k", h=PER),
                                          AX.X, ALU.max).then_inc(max_ready, 1)

                def scale_rows(ready, rms, filled, out, read, bank, g):
                    i = GROUPS * t + g
                    dve.wait_ge(ready, i + 1)
                    dve.wait_ge(filled, nonneg(i))
                    dve.tensor_tensor(out[:, :, :], bank.rearrange("p (h d) -> p h d", h=PER),
                                      rms[:, g * PER:(g + 1) * PER].unsqueeze(2).to_broadcast([P, PER, D]),
                                      ALU.mult).then_inc(read, 1)

                def normalise_heads(g):
                    i = GROUPS * (t - 1) + g
                    dve.wait_ge(out_filled, i + 1)
                    for j in range(2):
                        out = bank_out[j][:, 0:2 * VW].rearrange("p (h d) -> p h d", h=2)
                        last = dve.tensor_scalar(sums[:, g * PER + 2 * j:g * PER + 2 * j + 2].unsqueeze(2),
                                                 out[:, :, D:VW], LEAST_SUM, None, ALU.max)
                    middle_step(last)
                    middle_step(dve.reciprocal(reciprocal[:, g * PER:(g + 1) * PER],
                                               sums[:, g * PER:(g + 1) * PER]))
                    dve.wait_ge(headsT_filled, nonneg(i - 1))
                    for j in range(2):
                        out = bank_out[j][:, 0:2 * VW].rearrange("p (h d) -> p h d", h=2)
                        a = g * PER + 2 * j
                        last = dve.tensor_tensor(heads[g % 2][:, 2 * j:2 * j + 2, :], out[:, :, 0:D],
                                                 reciprocal[:, a:a + 2].unsqueeze(2).to_broadcast([P, 2, D]),
                                                 ALU.mult)
                    last.then_inc(heads_ready, 1)

                if middle:
                    middle_step.start(t - 1)
                if front:
                    layer.dve_normalise(dve, t)
                    if not normed:
                        dve.wait_ge(scoresT_filled, nonneg(GROUPS * (t - 1)))
                        dve.wait_ge(probs_ready, nonneg(GROUPS * (t - 1)))
                        dve.tensor_scalar(batch_bias[s][:, :], core.column(key_bias, t), 1.0, None, ALU.mult)
                        dve.tensor_scalar(mask_diagonal[s][:, :], core.ident[:, :], core.column(key_bias, t), None,
                                          ALU.mult).then_inc(mask_ready, 1)
                if middle:
                    row_maxima(0)
                if front and normed:
                    dve.wait_ge(layer.hT_ready, t + 1)
                    dve.wait_ge(v_filled, nonneg(KV_GROUPS * t))
                    dve.tensor_scalar(high[:, :, :].bitcast(I32), turned_h[:, :, :].bitcast(I32), HIGH_BITS, None,
                                      ALU.bitwise_and).then_inc(halves_chain, 1)
                    dve.wait_ge(halves_chain, t + 1)
                    dve.tensor_scalar(halves[0][:, :, :], high[:, :, :], 1.0, None, ALU.mult)
                    dve.tensor_tensor(halves[1][:, :, :], turned_h[:, :, :], high[:, :, :], ALU.subtract)\
                       .then_inc(halves_ready, 1)
                if middle:
                    row_maxima(1)
                if tail:
                    tail_step.start(t - 2)
                    layer.dve_update_x(dve, t - 2, bank_y[:, 0:EMBED], tail_step)
                for g in range(GROUPS):
                    if front and normed:
                        scale_rows(rms_q_ready, rms_q, qT_filled, q_scaled, q_read, bank_project[0], g)
                    if middle:
                        normalise_heads(g)
                        if g + 2 < GROUPS:
                            row_maxima(g + 2)
                    if front and normed:
                        scale_rows(rms_k_ready, rms_k, kT_filled, k_scaled, k_read, bank_project[1], g)
                if middle and not normed:
                    if isinstance(t, int) and t == 1:
                        dve.wait_ge(core.weights_loaded[n + 1], 16 * WEIGHT_PARTS)
                    scale_step.start(t - 1)
                    dve.wait_ge(slice_rounded, nonneg(t - 2))
                    dve_scale(dve, to_quantise[:, bass.ds((t - 1) * SLICE, SLICE)], scratch[1 - s], scale_step,
                              LEAST_SCALE, slice_scaled)
            pipeline(dve, step)

        @block.tensor
        def _(pe):
            pe.wait_ge(core.weights_loaded[n], 16 * WEIGHT_PARTS)
            pe.wait_ge(small_ready, 1)
            q_done, k_done = (q_read, k_read) if normed else (qT_ready, kT_ready)

            def step(t, s, front, middle, tail):
                if normed and isinstance(t, int) and t == 1:
                    turned = (kT_ready, GROUPS - 1)
                else:
                    turned = (headsT_ready, GROUPS * (t - 2) + GROUPS - 1)

                def turn(sources, filled, ready, count):
                    nonlocal turned
                    pe.wait_ge(turned[0], nonneg(turned[1]))
                    for j, source in enumerate(sources):
                        last = pe.transpose(bank_turn[:, j * P:(j + 1) * P], source, core.ident[:, :])
                    last.then_inc(filled, 1)
                    turned = (ready, count)

                def scores(g):
                    i = GROUPS * (t - 1) + g
                    pe.wait_ge(max_ready, nonneg(i))
                    pe.wait_ge(qT_bf_ready, nonneg(i + 1))
                    pe.wait_ge(kT_bf_ready, nonneg(KV_GROUPS * (t - 1) + g // SHARE + 1))
                    if not normed:
                        if g == 0:
                            pe.wait_ge(mask_ready, t + 1)
                        pe.matmul(bank_scores[:, :], core.ones_bf[:, :],
                                  mask_diagonal[1 - s][:, :].unsqueeze(1).to_broadcast([P, PER, P]),
                                  start=True, stop=False)
                    for j in range(PER):
                        h = g * PER + j
                        last = pe.matmul(bank_scores[:, j * P:(j + 1) * P], qT_bf[:, h, :], kT_bf[:, h // SHARE, :],
                                         start=(normed and j == 0), stop=(j == PER - 1), skip_group_check=normed)
                    last.then_inc(scores_filled, 1)

                def scores_transposed(g):
                    i = GROUPS * (t - 1) + g
                    pe.wait_ge(max_ready, i + 1)
                    pe.wait_ge(probs_ready, nonneg(i))
                    for j in range(PER):
                        h = g * PER + j
                        pe.matmul(bank_scoresT[:, j * P:(j + 1) * P], maxima[1 - s][:, h:h + 1].to_broadcast([P, P]),
                                  core.minus_ident_bf[:, :], start=(j == 0), stop=False, skip_group_check=True)
                    for j in range(PER):
                        h = g * PER + j
                        last = pe.matmul(bank_scoresT[:, j * P:(j + 1) * P], kT[:, h // SHARE, :], qT[:, h, :],
                                         start=False, stop=(j == PER - 1), skip_group_check=True)
                    last.then_inc(scoresT_filled, 1)

                def weigh_values(g):
                    i = GROUPS * (t - 1) + g
                    pe.wait_ge(probs_ready, i + 1)
                    pe.wait_ge(heads_ready, nonneg(i))
                    if g == 0:
                        pe.wait_ge(v_ready, nonneg(KV_GROUPS * t))
                    for j in range(PER):
                        h = g * PER + j
                        last = pe.matmul(bank_out[j // 2][:, j % 2 * VW:(j % 2 + 1) * VW], probs[:, h, :],
                                         values[:, h // SHARE, :], start=True, stop=True)
                    last.then_inc(out_filled, 1)

                def turn_heads(b, g):
                    pe.wait_ge(heads_ready, GROUPS * b + g + 1)
                    turn([heads[g % 2][:, j, :] for j in range(PER)], headsT_filled, headsT_ready, GROUPS * b + g + 1)

                def add_output(b, heads_range):
                    for h in heads_range:
                        last = pe.matmul(bank_y[:, 0:EMBED], headsT[:, h, :], wo[:, h, :],
                                         start=(h == 0), stop=(h == HEADS - 1))
                    return last

                def add_halves(out, chunks, first_column, g):
                    jobs = [(c, a, b) for c in chunks for a, b in PARTS]
                    for k, (c, a, b) in enumerate(jobs):
                        at = first_column + c % EC * HEADS * D + g * PER * D
                        last = pe.matmul(out, halves[a][:, c, :], split_weights[b][:, at:at + PER * D],
                                         start=(k == 0), stop=(k == len(jobs) - 1))
                    return last

                def project_q(g):
                    if g == 0:
                        pe.wait_ge(halves_ready if normed else layer.hT_ready, t + 1)
                    pe.wait_ge(q_done, nonneg(GROUPS * t + g))
                    if normed:
                        last = add_halves(bank_project[0][:, :], range(EC), 0, g)
                    else:
                        for j in range(PER):
                            for c in range(EC):
                                h = g * PER + j
                                last = pe.matmul(bank_project[0][:, j * P:(j + 1) * P], wq[:, c, h * D:(h + 1) * D],
                                                 layer.hT[:, c, :], start=(c == 0), stop=(c == EC - 1))
                    last.then_inc(q_filled, 1)

                def project_k(g):
                    pe.wait_ge(k_done, nonneg(KV_GROUPS * t + g))
                    if normed:
                        last = add_halves(bank_project[1][:, :], [EC], EC * HEADS * D, g)
                    else:
                        for j in range(PER):
                            h = g * PER + j
                            last = pe.matmul(bank_project[1][:, j * P:(j + 1) * P], wk[:, h * D:(h + 1) * D],
                                             contextT[:, :], start=True, stop=True)
                    last.then_inc(k_filled, 1)

                def project_v(g):
                    if g == 0:
                        pe.wait_ge(layer.x_updated, nonneg(t - 1))
                    pe.wait_ge(v_ready, nonneg(KV_GROUPS * t + g))
                    if normed:
                        last = add_halves(bank_y[:, :], [EC], (EC + 1) * HEADS * D, g)
                    else:
                        last = pe.matmul(bank_y[:, :], contextT[:, :], wv[:, g * PER * D:(g + 1) * PER * D],
                                         start=True, stop=True)
                    last.then_inc(v_filled, 1)

                def turn_q(b, g):
                    pe.wait_ge(q_read, GROUPS * b + g + 1)
                    turn([q_scaled[:, j, :] for j in range(PER)], qT_filled, qT_ready, GROUPS * b + g + 1)

                def turn_k(b, g):
                    pe.wait_ge(k_read, GROUPS * b + g + 1)
                    turn([k_scaled[:, j, :] for j in range(PER)], kT_filled, kT_ready, GROUPS * b + g + 1)

                if middle:
                    scores(0)
                    if normed:
                        turn_q(t - 1, GROUPS - 1)
                if tail:
                    if not normed:
                        turn_heads(t - 2, GROUPS - 1)
                    pe.wait_ge(layer.x_updated, nonneg(t - 2))
                    if middle:
                        pe.wait_ge(v_ready, nonneg(KV_GROUPS * t))
                    add_output(t - 2, range(0, PER))
                    if normed:
                        turn_heads(t - 2, GROUPS - 1)
                    add_output(t - 2, range(PER, 2 * PER))
                if middle and normed:
                    turn_k(t - 1, GROUPS - 1)
                if tail:
                    add_output(t - 2, range(2 * PER, 3 * PER))
                if front:
                    pe.wait_ge(layer.h_ready, t + 1)
                    pe.wait_ge(context_loaded[s], nonneg(16 * ((t - s) // 2 + 1) if isinstance(t, int) else (t - s) * 8 + 16))
                    turn([layer.h[:, 0:P], layer.h[:, P:2 * P], context[s][:, :]], layer.hT_filled,
                         layer.hT_ready, t + 1)
                if middle:
                    scores_transposed(0)
                    scores(1)
                if tail:
                    pe.wait_ge(headsT_ready, nonneg(GROUPS * (t - 1)))
                    add_output(t - 2, range(3 * PER, HEADS)).then_inc(layer.y_filled, 1)
                for g in range(GROUPS):
                    if front:
                        project_q(g)
                        if normed and g:
                            turn_q(t, g - 1)
                    if middle and g + 1 < GROUPS:
                        scores_transposed(g + 1)
                    if middle:
                        weigh_values(g)
                    if front:
                        if normed and g:
                            turn_k(t, g - 1)
                        if (g + 1) % SHARE == 0:
                            project_k(g // SHARE)
                    values_first = normed and g < GROUPS - 1
                    if front and values_first:
                        project_v(g)
                    if middle and g:
                        turn_heads(t - 1, g - 1)
                    if front and not values_first and (g + 1) % SHARE == 0:
                        project_v(g // SHARE)
                    if middle and g + 2 < GROUPS:
                        scores(g + 2)
            pipeline(pe, step)


def gated_mlp(nc, core, dram, next_weights):
    n = 2
    INTER, ROUTED, EXPERTS = 1024, 128, 8
    TILES = INTER // P
    HALVES = 2
    PER = TILES // HALVES
    with ExitStack() as ctx:
        layer = Layer(core, n, "mlp", ctx)
        sem, sbuf = layer.sem, layer.sbuf
        region = core.region[n % 2]
        at = 0

        def weight(chunk, width):
            nonlocal at
            part = region[:, at:at + chunk * width].rearrange("p (c n) -> p c n", c=chunk)
            at += chunk * width
            return part
        w_gate, w_up, w_down = weight(EC, INTER), weight(EC, INTER), weight(TILES, EMBED)
        r_gate, r_up, r_down, router = weight(EC, ROUTED), weight(EC, ROUTED), weight(1, EMBED), weight(EC, EXPERTS)
        tanh = [sbuf(f"tanh{j}", [P, 512]) for j in range(HALVES + 1)]
        gated = [sbuf(f"gated{j}", [P, 512]) for j in range(HALVES + 1)]
        inner = sbuf("inner", [P, TILES + 1, P])
        top = sbuf("top", [P, EXPERTS])
        gap, ratio, both, share, weight_half = (sbuf(f"router{k}", [P, 1]) for k in range(5))
        x_routed = sbuf("x_routed", [P, EMBED])

        bank_h, bank_routed, bank_y = core.banks[0], core.banks[5], core.banks[6]
        bank_gate, bank_up = [core.banks[1], core.banks[3]], [core.banks[2], core.banks[4]]
        PARTS = HALVES + 1
        part_filled, tanh_ready = sem("part_filled"), sem("tanh_ready")
        gated_ready, inner_ready = sem("gated_ready"), sem("inner_ready")
        router_chain, gap_ready, ratio_ready = sem("router_chain"), sem("gap_ready"), sem("ratio_ready")
        block = ctx.enter_context(nc.Block())

        def gate_of(j):
            return bank_gate[j][:, :] if j < HALVES else bank_routed[:, 0:ROUTED]

        def up_of(j):
            return bank_up[j][:, :] if j < HALVES else bank_routed[:, ROUTED:2 * ROUTED]
        ORDER = [HALVES, 0, 1]

        @block.sync
        def _(sp):
            layer.clear_last_layers_semaphores(sp)
            load_weights(sp, core, n + 1, next_weights)

        @block.gpsimd
        def _(pool):
            def step(t, s, front, middle, tail):
                if middle:
                    layer.pool_rstd(pool, t - 1, STATISTICS_STEPS + 1)
            pipeline(pool, step)

        @block.scalar
        def _(act):
            def step(t, s, front, middle, tail):
                if front:
                    act.wait_ge(part_filled, nonneg(PARTS * t))
                    layer.act_copy_hT(act, t, bank_h)
                    for k, j in enumerate(ORDER):
                        width = 512 if j < HALVES else ROUTED
                        act.wait_ge(part_filled, PARTS * t + k + 1)
                        act.wait_ge(gated_ready, nonneg(PARTS * (t - 1) + k + 1))
                        act.activation(tanh[j][:, 0:width], gate_of(j), ACT.Tanh, scale=0.5).then_inc(tanh_ready, 1)
                        if k == 0:
                            act.wait_ge(gap_ready, t + 1)
                            act.wait_ge(router_chain, nonneg(3 * t))
                            act.activation(ratio[:, :], gap[:, :], ACT.Exp).then_inc(ratio_ready, 1)
            pipeline(act, step)

        @block.vector
        def _(dve):
            router_step = Chain(dve, router_chain, 3)
            tail_step = Chain(dve, layer.tail_chain, STATISTICS_STEPS + 1)

            def step(t, s, front, middle, tail):
                def gate(b, k):
                    i, j = PARTS * b + k, ORDER[k]
                    width = 512 if j < HALVES else ROUTED
                    tiles = inner[:, j * PER:j * PER + width // P, :].rearrange("p j t -> p (j t)")
                    if k == 0:
                        dve.wait_ge(layer.y_filled, nonneg(b))
                        dve.wait_ge(gap_ready, nonneg(b))
                        dve.wait_ge(ratio_ready, nonneg(b))
                    dve.wait_ge(tanh_ready, i + 1)
                    dve.wait_ge(inner_ready, nonneg(i - PARTS + 1))
                    dve.scalar_tensor_tensor(gated[j][:, 0:width], tanh[j][:, 0:width], 1.0, gate_of(j),
                                             ALU.add, ALU.mult).then_inc(gated_ready, 1)
                    if k == 0:
                        dve.max(top[:, :], bank_routed[:, 2 * ROUTED:2 * ROUTED + EXPERTS])
                    dve.wait_ge(gated_ready, i + 1)
                    dve.tensor_tensor(tiles, gated[j][:, 0:width], up_of(j), ALU.mult).then_inc(inner_ready, 1)
                    if k == 0:
                        dve.wait_ge(inner_ready, i + 1)
                        dve.tensor_tensor(gap[:, :], top[:, 1:2], top[:, 0:1], ALU.subtract)\
                           .then_inc(gap_ready, 1)
                if front:
                    layer.dve_normalise(dve, t)
                if middle:
                    gate(t - 1, PARTS - 1)
                    b = t - 1
                    router_step.start(b)
                    tail_step.start(b)
                    dve.wait_ge(ratio_ready, b + 1)
                    dve.wait_ge(layer.y_filled, b + 1)
                    router_step(dve.tensor_scalar(both[:, :], ratio[:, :], 1.0, 2.0, ALU.add, ALU.mult))
                    router_step(dve.reciprocal(share[:, :], both[:, :]))
                    router_step(dve.scalar_tensor_tensor(weight_half[:, :], ratio[:, :], share[:, 0:1], share[:, :],
                                                         ALU.mult, ALU.add))
                    tail_step(dve.scalar_tensor_tensor(x_routed[:, :], bank_y[:, EMBED:2 * EMBED], weight_half[:, 0:1],
                                                       core.batch_x(b), ALU.mult, ALU.add))
                    dve.scalar_tensor_tensor(layer.new_x[:, :], bank_y[:, 0:EMBED], 0.5, x_routed[:, :],
                                             ALU.mult, ALU.add).then_inc(layer.x_updated, 1)
                    dve.wait_ge(layer.x_updated, b + 1)
                    layer.dve_statistics(dve, b, tail_step)
                if front:
                    gate(t, 0)
                    gate(t, 1)
            pipeline(dve, step)

        @block.tensor
        def _(pe):
            pe.wait_ge(core.weights_loaded[n], 16 * WEIGHT_PARTS)

            def step(t, s, front, middle, tail):
                if front:
                    pe.wait_ge(layer.hT_ready, nonneg(t))
                    layer.pe_transpose_h(pe, t, bank_h)
                if middle:
                    b = t - 1
                    pe.wait_ge(layer.x_updated, nonneg(b))
                    pe.wait_ge(inner_ready, PARTS * b + 1)
                    pe.matmul(bank_y[:, EMBED:2 * EMBED], inner[:, TILES, :], r_down[:, 0, :], start=True, stop=True)
                    for j in range(HALVES):
                        pe.wait_ge(inner_ready, nonneg(PARTS * b + j + 2))
                        for m in range(j * PER, (j + 1) * PER):
                            last = pe.matmul(bank_y[:, 0:EMBED], inner[:, m, :], w_down[:, m, :],
                                             start=(m == 0), stop=(m == TILES - 1))
                    last.then_inc(layer.y_filled, 1)
                if front:
                    pe.wait_ge(layer.hT_ready, t + 1)

                    def project(out, wt, m):
                        for c in range(EC):
                            last = pe.matmul(out, wt[:, c, m * P:(m + 1) * P], layer.hT[:, c, :],
                                             start=(c == 0), stop=(c == EC - 1))
                        return last
                    for k, j in enumerate(ORDER):
                        if j == HALVES:
                            pe.wait_ge(gap_ready, nonneg(t))
                            pe.wait_ge(inner_ready, nonneg(PARTS * (t - 1) + k + 1))
                            project(bank_routed[:, 0:ROUTED], r_gate, 0)
                            project(bank_routed[:, ROUTED:2 * ROUTED], r_up, 0)
                            for c in range(EC):
                                last = pe.matmul(bank_routed[:, 2 * ROUTED:2 * ROUTED + EXPERTS], layer.hT[:, c, :],
                                                 router[:, c, :], start=(c == 0), stop=(c == EC - 1))
                        else:
                            pe.wait_ge(inner_ready, nonneg(PARTS * (t - 1) + k + 1))
                            for m in range(PER):
                                project(bank_gate[j][:, m * P:(m + 1) * P], w_gate, j * PER + m)
                            for m in range(PER):
                                last = project(bank_up[j][:, m * P:(m + 1) * P], w_up, j * PER + m)
                        last.then_inc(part_filled, 1)
            pipeline(pe, step)


def grouped_attention(nc, core, dram, next_weights):
    n = 3
    HEADS, D = 32, 8
    GROUPS = 8
    PER = HEADS // GROUPS
    ROWS = PER * D
    SLOTS = P // ROWS
    SCALE = float(D) ** -0.5
    VW = 2 * D
    with ExitStack() as ctx:
        layer = Layer(core, n, "grouped", ctx)
        sem, sbuf = layer.sem, layer.sbuf
        region = core.region[n % 2]
        wq, wk, wo = (region[:, k * EC * EMBED:(k + 1) * EC * EMBED].rearrange("p (c n) -> p c n", c=EC)
                      for k in range(3))
        wv = region[:, 3 * EC * EMBED:3 * EC * EMBED + EC * GROUPS * D].rearrange("p (c n) -> p c n", c=EC)
        STACK = len(PARTS) * ROWS
        columns = sbuf("columns", [P, 2 * EC + PER])
        bias_q, bias_k = columns[:, 0:EC], columns[:, EC:2 * EC]
        own = columns[:, 2 * EC:]
        rows = sbuf("rows", [1, GROUPS * D + EMBED])
        bias_v, bias_o = rows[:, 0:GROUPS * D], rows[:, GROUPS * D:GROUPS * D + EMBED]
        qT = [sbuf(f"qT{s}", [P, EC, P]) for s in range(2)]
        qT_bf = [sbuf(f"qT_bf{s}", [P, EC, P], BF16) for s in range(2)]
        q_halves, k_high = sbuf("q_halves", [P, 2, EC, P]), sbuf("k_high", [P, EC, P])
        q_stack = sbuf("q_stack", [STACK, EC, SLOTS, P])
        k_stack = [sbuf(f"k_stack{s}", [STACK, EC, SLOTS, P], F32R) for s in range(2)]
        q_own = [sbuf(f"q_own{s}", [STACK, EC * SLOTS, PER, P], F32R) for s in range(2)]
        kT = [sbuf(f"kT{s}", [P, EC, P]) for s in range(2)]
        kT_bf = [sbuf(f"kT_bf{s}", [P, EC, PER, P], BF16) for s in range(2)]
        values = [sbuf(f"values{s}", [P, GROUPS * (P + VW)]) for s in range(2)]
        outT = sbuf("outT", [P, PER, P])
        maxima = [sbuf(f"maxima{s}", [P, HEADS], BF16) for s in range(2)]
        probs = sbuf("probs", [P, GROUPS, PER * P])
        reciprocal = sbuf("reciprocal", [P, HEADS])
        heads = sbuf("heads", [P, HEADS, D])
        headsT = sbuf("headsT", [P, EC, P])

        bank_hv, bank_q, bank_k = core.banks[0:3]
        bank_scores, bank_scoresT, bank_out = core.banks[3:5], core.banks[5:7], core.banks[7]
        half_tail = bank_hv[:, EMBED:2 * EMBED]

        constants_loaded, constants_ready = sem("constants_loaded"), sem("constants_ready")
        q_filled, q_ready, q_bf_ready = sem("q_filled"), sem("q_ready"), sem("q_bf_ready")
        halves_chain, q_halves_ready, q_stacked = sem("halves_chain"), sem("q_halves_ready"), sem("q_stacked")
        k_stacked = sem("k_stacked")
        q_own_ready, k_filled = sem("q_own_ready"), sem("k_filled")
        k_ready, k_bf_ready = sem("k_ready"), sem("k_bf_ready")
        v_filled, v_ready = sem("v_filled"), sem("v_ready")
        scores_filled, max_ready = sem("scores_filled"), sem("max_ready")
        scoresT_filled, probs_ready = sem("scoresT_filled"), sem("probs_ready")
        out_filled = sem("out_filled")
        outT_ready, out_turned = sem("outT_ready"), sem("out_turned")
        heads_ready, headsT_filled, headsT_ready = sem("heads_ready"), sem("headsT_filled"), sem("headsT_ready")
        heads_chain = sem("heads_chain")
        block = ctx.enter_context(nc.Block())

        @block.sync
        def _(sp):
            layer.clear_last_layers_semaphores(sp)
            sp.dma_start(columns[:, :], dram["grouped_columns"]).then_inc(constants_loaded, 16)
            sp.dma_start(rows[:, :], dram["grouped_rows"]).then_inc(constants_loaded, 16)
            load_weights(sp, core, n + 1, next_weights)

        @block.gpsimd
        def _(pool):
            for s in range(2):
                last = pool.memset(values[s][:, :], 0.0)
            last.then_inc(constants_ready, 1)
            pool.wait_ge(constants_ready, 1)
            for s in range(2):
                last = pool.memset(values[s].rearrange("p (g x) -> p g x", g=GROUPS)[:, :, D:D + 1], 1.0)
            last.then_inc(constants_ready, 1)
            pool.wait_ge(constants_loaded, 2 * 16)

            def step(t, s, front, middle, tail):
                if front:
                    pool.wait_ge(q_ready, t + 1)
                    pool.wait_ge(scores_filled, nonneg(GROUPS * (t - 1)))
                    pool.tensor_tensor(qT_bf[s][:, :, :], qT[s][:, :, :],
                                       core.ones[:, 0:1].unsqueeze(2).to_broadcast([P, EC, P]), ALU.mult)\
                        .then_inc(q_bf_ready, 1)
                    pool.wait_ge(k_ready, t + 1)
                    for m in range(PER):
                        last = pool.tensor_tensor(kT_bf[s][:, :, m, :], kT[s][:, :, :],
                                                  own[:, m:m + 1].unsqueeze(2).to_broadcast([P, EC, P]), ALU.mult)
                    last.then_inc(k_bf_ready, 1)
                if tail:
                    layer.pool_rstd(pool, t - 2, STATISTICS_STEPS)
            pipeline(pool, step)

        @block.scalar
        def _(act):

            def step(t, s, front, middle, tail):
                def exponentials(g):
                    i = GROUPS * (t - 1) + g
                    act.wait_ge(scoresT_filled, i + 1)
                    act.wait_ge(out_filled, nonneg(i - GROUPS + 1))
                    act.activation(probs[:, g, :], bank_scoresT[g % 2][:, :], ACT.Exp, scale=SCALE)\
                       .then_inc(probs_ready, 1)

                def stack_queries(slot):
                    for k, (_, half) in enumerate(PARTS):
                        last = act.activation(q_stack[ROWS * k:ROWS * (k + 1), :, slot, :],
                                              q_halves[ROWS * slot:ROWS * (slot + 1), half, :, :], ACT.Copy)
                    last.then_inc(q_stacked, 1)

                def copy_values():
                    act.wait_ge(constants_ready, 2)
                    act.wait_ge(v_filled, t + 1)
                    act.wait_ge(out_filled, nonneg(GROUPS * (t - 1)))
                    act.activation(values[s].rearrange("p (g x) -> p g x", g=GROUPS)[:, :, 0:D],
                                   bank_hv[:, 0:GROUPS * D].rearrange("p (h d) -> p h d", h=GROUPS), ACT.Copy)\
                       .then_inc(v_ready, 1)

                def own_queries(m):
                    act.wait_ge(constants_loaded, 2 * 16)
                    act.wait_ge(q_stacked, SLOTS * (t + 1))
                    act.activation(q_own[s][:, :, m, :], q_stack[:, :, :, :].rearrange("p c s t -> p (c s) t"), ACT.Copy,
                                   scale=own[0:STACK, m:m + 1]).then_inc(q_own_ready, 1)
                if tail:
                    b = t - 2
                    act.wait_ge(out_filled, GROUPS * (b + 1))
                    act.wait_ge(out_turned, nonneg(b))
                    act.activation(outT[:, :, :], bank_out[:, :].rearrange("p (m q) -> p m q", m=PER), ACT.Copy)\
                       .then_inc(outT_ready, 1)
                if front:
                    act.wait_ge(v_filled, nonneg(t))
                    layer.act_copy_hT(act, t, bank_hv)
                if middle:
                    exponentials(0)
                    exponentials(1)
                if front:
                    act.wait_ge(q_halves_ready, t + 1)
                    act.wait_ge(q_own_ready, nonneg(PER * t))
                    stack_queries(0)
                    stack_queries(1)
                if middle:
                    exponentials(2)
                if tail:
                    act.wait_ge(headsT_filled, nonneg(t - 1))
                    act.wait_ge(layer.y_filled, nonneg(t - 2))
                    act.activation(headsT[:, :, :], half_tail.rearrange("p (c t) -> p c t", c=EC),
                                   ACT.Copy).then_inc(headsT_ready, 1)
                if front:
                    stack_queries(2)
                    stack_queries(3)
                    first_step = isinstance(t, int) and t == 0
                    if first_step:
                        copy_values()
                if middle:
                    exponentials(3)
                if front:
                    act.wait_ge(scoresT_filled, nonneg(GROUPS * (t - 1)))
                    own_queries(0)
                if middle:
                    exponentials(4)
                if front:
                    own_queries(1)
                if middle:
                    exponentials(5)
                if front:
                    own_queries(2)
                if middle:
                    exponentials(6)
                if front:
                    own_queries(3)
                if middle:
                    exponentials(7)
                if front and not first_step:
                    copy_values()
            pipeline(act, step)

        @block.vector
        def _(dve):
            heads_step = Chain(dve, heads_chain, 1)
            tail_step = Chain(dve, layer.tail_chain, STATISTICS_STEPS)

            def step(t, s, front, middle, tail):
                def row_maxima(g):
                    i = GROUPS * (t - 1) + g
                    dve.wait_ge(scores_filled, i + 1)
                    dve.wait_ge(scoresT_filled, nonneg(GROUPS * (t - 2)))
                    with nc.allow_low_precision("the maximum only shifts a softmax's exponents"):
                        dve.tensor_reduce(maxima[1 - s][:, g * PER:(g + 1) * PER],
                                          bank_scores[g % 2].rearrange("p (h k) -> p h k", h=PER),
                                          AX.X, ALU.max).then_inc(max_ready, 1)

                def stack_keys(slot):
                    rows = slice(ROWS * slot, ROWS * (slot + 1))
                    for k, (half, _) in enumerate(PARTS):
                        to = k_stack[s][ROWS * k:ROWS * (k + 1), :, slot, :]
                        if half == 0:
                            last = dve.tensor_scalar(to, k_high[rows, :, :], 1.0, None, ALU.mult)
                        else:
                            last = dve.tensor_tensor(to, kT[s][rows, :, :], k_high[rows, :, :], ALU.subtract)
                    last.then_inc(k_stacked, 1)

                def add_bias(bank, filled, to, bias, ready):
                    dve.wait_ge(constants_loaded, 2 * 16)
                    dve.wait_ge(filled, t + 1)
                    for c in range(EC):
                        last = dve.tensor_scalar(to[:, c, :], bank[:, c * P:(c + 1) * P], bias[:, c:c + 1], None,
                                                 ALU.add)
                    last.then_inc(ready, 1)
                if front:
                    layer.dve_normalise(dve, t)
                if middle:
                    row_maxima(0)
                    row_maxima(1)
                    row_maxima(2)
                if front:
                    dve.wait_ge(scoresT_filled, nonneg(GROUPS * (t - 1)))
                    dve.wait_ge(q_bf_ready, nonneg(t - 1))
                    add_bias(bank_q, q_filled, qT[s], bias_q, q_ready)
                    high, low = (q_halves[:, half, :, :] for half in range(2))
                    dve.wait_ge(q_ready, t + 1)
                    dve.wait_ge(q_stacked, nonneg(SLOTS * t))
                    dve.tensor_scalar(high.bitcast(I32), qT[s][:, :, :].bitcast(I32), HIGH_BITS, None,
                                      ALU.bitwise_and).then_inc(halves_chain, 1)
                    dve.wait_ge(halves_chain, 2 * t + 1)
                    dve.tensor_tensor(low, qT[s][:, :, :], high, ALU.subtract).then_inc(q_halves_ready, 1)
                if tail:
                    b = t - 2
                    heads_step.start(b)
                    dve.wait_ge(out_turned, b + 1)
                    out = bank_out[:, :].rearrange("p (m g d) -> p m g d", m=PER, g=GROUPS)
                    of_heads = reciprocal[:, :].rearrange("p (m g) -> p m g", m=PER)
                    heads_step(dve.reciprocal(of_heads.unsqueeze(3), out[:, :, :, D:D + 1]))
                    dve.wait_ge(headsT_filled, nonneg(b))
                    dve.tensor_tensor(heads[:, :, :].rearrange("p (g m) d -> p m g d", m=PER), out[:, :, :, 0:D],
                                      of_heads.unsqueeze(3).to_broadcast([P, PER, GROUPS, D]), ALU.mult)\
                       .then_inc(heads_ready, 1)
                if middle:
                    row_maxima(3)
                if front:
                    dve.wait_ge(k_bf_ready, nonneg(t - 1))
                    add_bias(bank_k, k_filled, kT[s], bias_k, k_ready)
                    dve.wait_ge(k_ready, t + 1)
                    dve.wait_ge(k_stacked, nonneg(SLOTS * t))
                    dve.tensor_scalar(k_high[:, :, :].bitcast(I32), kT[s][:, :, :].bitcast(I32), HIGH_BITS, None,
                                      ALU.bitwise_and).then_inc(halves_chain, 1)
                    dve.wait_ge(halves_chain, 2 * t + 2)
                for slot in range(SLOTS):
                    if front:
                        stack_keys(slot)
                    if middle and slot < GROUPS - 1 - 4:
                        row_maxima(4 + slot)
                if tail:
                    tail_step.start(t - 2)
                    layer.dve_update_x(dve, t - 2, half_tail, tail_step)
                if middle:
                    row_maxima(GROUPS - 1)
            pipeline(dve, step)

        @block.tensor
        def _(pe):
            pe.wait_ge(core.weights_loaded[n], 16 * WEIGHT_PARTS)

            def step(t, s, front, middle, tail):
                def scores(g):
                    i = GROUPS * (t - 1) + g
                    pe.wait_ge(max_ready, nonneg(i - 1))
                    slot, c = slice(ROWS * (g % SLOTS), ROWS * (g % SLOTS + 1)), g // SLOTS
                    pe.matmul(bank_scores[g % 2][:, :], qT_bf[1 - s][slot, c, :], kT_bf[1 - s][slot, c, :, :],
                              start=True, stop=True).then_inc(scores_filled, 1)

                def scores_transposed(g):
                    i = GROUPS * (t - 1) + g
                    pe.wait_ge(max_ready, i + 1)
                    pe.wait_ge(probs_ready, nonneg(i - 1))
                    c = g // SLOTS
                    bank = bank_scoresT[g % 2]
                    for m in range(PER):
                        h = g * PER + m
                        pe.matmul(bank[:, m * P:(m + 1) * P], maxima[1 - s][:, h:h + 1].to_broadcast([P, P]),
                                  core.minus_ident_bf[:, :], start=(m == 0), stop=False, skip_group_check=True)
                    pe.matmul(bank[:, :], k_stack[1 - s][:, c, g % SLOTS, :], q_own[1 - s][:, g, :, :],
                              start=False, stop=True, skip_group_check=True).then_inc(scoresT_filled, 1)

                def weigh_values(g, b=t - 1, s=1 - s):
                    i = GROUPS * b + g
                    pe.wait_ge(probs_ready, i + 1)
                    if g == 0:
                        pe.wait_ge(v_ready, nonneg(t))
                        pe.wait_ge(heads_ready, nonneg(t - 1))
                    pe.matmul(bank_out[:, :], values[s][:, g * P:(g + 1) * P], probs[:, g, :],
                              start=(g == 0), stop=(g == GROUPS - 1)).then_inc(out_filled, 1)

                def project(bank, wt):
                    for m in range(EC):
                        for c in range(EC):
                            last = pe.matmul(bank[:, m * P:(m + 1) * P], wt[:, c, m * P:(m + 1) * P],
                                             layer.hT[:, c, :], start=(c == 0), stop=(c == EC - 1))
                    return last

                def transpose_heads():
                    pe.wait_ge(heads_ready, nonneg(t - 1))
                    pe.wait_ge(layer.x_updated, nonneg(t - 2))
                    flat = heads[:, :, :].rearrange("p h d -> p (h d)")
                    for c in range(EC):
                        last = pe.transpose(half_tail[:, c * P:(c + 1) * P], flat[:, c * P:(c + 1) * P],
                                            core.ident[:, :])
                    last.then_inc(headsT_filled, 1)

                def project_heads():
                    pe.wait_ge(headsT_ready, nonneg(t - 1))
                    pe.matmul(half_tail, core.ones[0:1, :], bias_o, start=True, stop=False)
                    for c in range(EC):
                        last = pe.matmul(half_tail, headsT[:, c, :], wo[:, c, :], start=False, stop=(c == EC - 1))
                    last.then_inc(layer.y_filled, 1)

                if middle:
                    pe.wait_ge(q_bf_ready, nonneg(t))
                    pe.wait_ge(k_bf_ready, nonneg(t))
                    scores(0)
                    scores(1)
                if tail:
                    weigh_values(7, t - 2, s)
                if front:
                    pe.wait_ge(v_ready, nonneg(t))
                    layer.pe_transpose_h(pe, t, bank_hv)
                if middle:
                    pe.wait_ge(q_own_ready, nonneg(PER * t))
                    pe.wait_ge(k_stacked, nonneg(SLOTS * t))
                    scores_transposed(0)
                    scores(2)
                if front:
                    pe.wait_ge(layer.hT_ready, t + 1)
                    pe.wait_ge(q_ready, nonneg(t))
                    project(bank_q, wq).then_inc(q_filled, 1)
                if tail:
                    pe.wait_ge(outT_ready, nonneg(t - 1))
                    for m in range(PER):
                        last = pe.transpose(bank_out[:, m * P:(m + 1) * P], outT[:, m, :], core.ident[:, :])
                    last.then_inc(out_turned, 1)
                if middle:
                    scores_transposed(1)
                    scores(3)
                if front:
                    pe.wait_ge(k_ready, nonneg(t))
                    project(bank_k, wk).then_inc(k_filled, 1)
                if middle:
                    scores_transposed(2)
                    weigh_values(0)
                    scores(4)
                if tail:
                    transpose_heads()
                if middle:
                    scores_transposed(3)
                    weigh_values(1)
                    scores(5)
                    scores_transposed(4)
                    weigh_values(2)
                    scores(6)
                if tail:
                    project_heads()
                if middle:
                    scores_transposed(5)
                    weigh_values(3)
                    scores(7)
                    scores_transposed(6)
                    weigh_values(4)
                    scores_transposed(7)
                    weigh_values(5)
                    weigh_values(6)
                if front:
                    pe.wait_ge(constants_loaded, 2 * 16)
                    pe.wait_ge(layer.x_updated, nonneg(t - 1))
                    pe.matmul(bank_hv[:, 0:GROUPS * D], core.ones[0:1, :], bias_v, start=True, stop=False)
                    for c in range(EC):
                        last = pe.matmul(bank_hv[:, 0:GROUPS * D], layer.hT[:, c, :], wv[:, c, :],
                                         start=False, stop=(c == EC - 1))
                    last.then_inc(v_filled, 1)
            pipeline(pe, step)


def mx_mlp(nc, core, dram, out):
    n = 5
    INTER = 1024
    TILES = INTER // P
    HALVES = INTER // 512
    GATE_UP_JOBS, WEIGHT_JOBS = 2 * EC * INTER // 512, 3 * EC * INTER // 512
    with ExitStack() as ctx:
        layer = Layer(core, n, "mx", ctx)
        sem, sbuf = layer.sem, layer.sbuf
        raw = core.region[n % 2]
        turned = core.region[1 - n % 2]
        w_gate = turned[:, 0:EC * INTER].rearrange("p (c n) -> p c n", c=EC)
        w_up = turned[:, EC * INTER:2 * EC * INTER].rearrange("p (c n) -> p c n", c=EC)
        w_down = turned[:, 2 * EC * INTER:3 * EC * INTER].rearrange("p (i n) -> p i n", i=TILES)

        scratch = [Scratch(layer, f"inner{j}", INTER // HALVES) for j in range(HALVES)]
        scratch_h = Scratch(layer, "h", EMBED)
        h_q = sbuf("h_q", [P, EMBED])
        tanh = [sbuf(f"tanh{j}", [P, 512]) for j in range(HALVES)]
        gated = [sbuf(f"gated{j}", [P, 512]) for j in range(HALVES)]
        inner = [sbuf(f"inner{s}", [P, INTER]) for s in range(2)]
        inner_q = [sbuf(f"inner_q{s}", [P, INTER]) for s in range(2)]
        innerT = sbuf("innerT", [P, TILES, P])
        result = [sbuf(f"result{s}", [P, EMBED]) for s in range(2)]

        bank_h, bank_turn, bank_y = core.banks[0], core.banks[5:7], core.banks[7]
        bank_gate, bank_up = [core.banks[1], core.banks[3]], [core.banks[2], core.banks[4]]

        scale_chain, inner_scaled = sem("scale_chain"), sem("inner_scaled")
        round_chain, inner_rounded = sem("pool_chain"), sem("inner_rounded")
        h_chain, h_scaled, h_pool_chain, h_done = sem("h_chain"), sem("h_scaled"), sem("h_pool_chain"), sem("h_done")
        weights_filled, weights_ready = sem("weights_filled"), sem("weights_ready")
        half_filled, tanh_ready = sem("half_filled"), sem("tanh_ready")
        gated_ready, inner_ready = sem("gated_ready"), sem("inner_ready")
        innerT_filled, innerT_ready = sem("innerT_filled"), sem("innerT_ready")
        result_ready = sem("result_ready")
        stored = [sem(f"stored{s}") for s in range(2)]
        block = ctx.enter_context(nc.Block())

        @block.sync
        def _(sp):
            def step(t, s, front, middle, tail):
                if tail:
                    b = t - 2
                    sp.wait_ge(result_ready, b + 1)
                    sp.dma_start(out[bass.ds(b, 1), :, :].rearrange("b p e -> (b p) e"), result[s][:, :])\
                      .then_inc(stored[s], 16)
            pipeline(sp, step)
            for s in range(2):
                sp.wait_ge(stored[s], 16 * BATCHES // 2)

        @block.gpsimd
        def _(pool):
            inner_step = Chain(pool, round_chain, 2 * HALVES)
            h_step = Chain(pool, h_pool_chain, 2)

            def step(t, s, front, middle, tail):
                if front:
                    h_step.start(t)
                    pool.wait_ge(h_scaled, t + 1)
                    pool.wait_ge(layer.hT_filled, nonneg(t))
                    pool_round(pool, scratch_h, h_q[:, :], h_step, h_done)
                if middle:
                    b = t - 1
                    inner_step.start(b)
                    pool.wait_ge(innerT_filled, nonneg(HALVES * (b - 1)))
                    for j in range(HALVES):
                        pool.wait_ge(inner_scaled, HALVES * b + j + 1)
                        pool_round(pool, scratch[j], inner_q[1 - s][:, j * 512:(j + 1) * 512], inner_step,
                                   inner_rounded)
            pipeline(pool, step)

        @block.scalar
        def _(act):
            def weights_to_sbuf(jobs):
                for k in jobs:
                    act.wait_ge(weights_filled, k + 1)
                    act.activation(turned[:, k * 512:(k + 1) * 512], bank_turn[k % 2][:, :], ACT.Copy)\
                       .then_inc(weights_ready, 1)
            weights_to_sbuf(range(0, GATE_UP_JOBS))

            def step(t, s, front, middle, tail):
                for j in range(HALVES):
                    if middle:
                        i = HALVES * (t - 1) + j
                        act.wait_ge(half_filled, i + 1)
                        act.wait_ge(gated_ready, nonneg(i - HALVES + 1))
                        act.activation(tanh[j][:, :], bank_gate[j][:, :], ACT.Tanh, scale=0.5).then_inc(tanh_ready, 1)
                    if tail:
                        b = t - 2
                        act.wait_ge(innerT_filled, HALVES * b + j + 1)
                        act.wait_ge(layer.y_filled, nonneg(b))
                        act.activation(innerT[:, 4 * j:4 * j + 4, :],
                                       bank_turn[j].rearrange("p (i t) -> p i t", i=4), ACT.Copy)\
                           .then_inc(innerT_ready, 1)
                if isinstance(t, int) and t == 1:
                    weights_to_sbuf(range(GATE_UP_JOBS, WEIGHT_JOBS))
                if front:
                    act.wait_ge(half_filled, nonneg(HALVES * t))
                    layer.act_copy_hT(act, t, bank_h)
            pipeline(act, step)

        @block.vector
        def _(dve):
            inner_step = Chain(dve, scale_chain, 5 * HALVES)
            h_step = Chain(dve, h_chain, 5)

            def step(t, s, front, middle, tail):
                if front:
                    dve.wait_ge(h_chain, nonneg(5 * t))
                    dve.wait_ge(h_done, nonneg(t))
                    dve.tensor_scalar(layer.h[:, :], core.batch_x(t), core.column(core.mean, t),
                                      core.column(core.rstd, t), ALU.subtract, ALU.mult).then_inc(layer.h_ready, 1)
                    dve.wait_ge(layer.h_ready, t + 1)
                    h_step.start(t)
                    dve_scale(dve, layer.h[:, :], scratch_h, h_step, LEAST_SCALE, h_scaled)
                if middle:
                    b = t - 1
                    inner_step.start(b)
                    for j in range(HALVES):
                        i = HALVES * b + j
                        dve.wait_ge(tanh_ready, i + 1)
                        dve.wait_ge(inner_ready, nonneg(i - HALVES + 1))
                        dve.wait_ge(inner_scaled, nonneg(HALVES * (b - 1)))
                        dve.scalar_tensor_tensor(gated[j][:, :], tanh[j][:, :], 1.0, bank_gate[j][:, :],
                                                 ALU.add, ALU.mult).then_inc(gated_ready, 1)
                        dve.wait_ge(gated_ready, i + 1)
                        dve.tensor_tensor(inner[1 - s][:, j * 512:(j + 1) * 512], gated[j][:, :], bank_up[j][:, :],
                                          ALU.mult).then_inc(inner_ready, 1)
                        dve.wait_ge(inner_rounded, nonneg(i - HALVES + 1))
                        dve.wait_ge(inner_ready, i + 1)
                        dve_scale(dve, inner[1 - s][:, j * 512:(j + 1) * 512], scratch[j], inner_step,
                                  2 * LEAST_SCALE, inner_scaled)
                if tail:
                    b = t - 2
                    dve.wait_ge(layer.y_filled, b + 1)
                    dve.wait_ge(stored[s], nonneg(16 * (b // 2) if isinstance(b, int) else (b - s) * 8))
                    dve.scalar_tensor_tensor(result[s][:, :], bank_y[:, 0:EMBED], 0.5, core.batch_x(b),
                                             ALU.mult, ALU.add).then_inc(result_ready, 1)
            pipeline(dve, step)

        @block.tensor
        def _(pe):
            def turn_weights(jobs):
                for k in jobs:
                    pe.wait_ge(weights_ready, nonneg(k - 1))
                    for i in range(4):
                        if k < GATE_UP_JOBS:
                            w, c, half = k // (2 * EC), k // 2 % EC, k % 2
                            at = w * EC * INTER + (4 * half + i) * EMBED + c * P
                        else:
                            tile, c = 2 * (k - GATE_UP_JOBS) + i // EC, i % EC
                            at = 2 * EC * INTER + c * INTER + tile * P
                        last = pe.transpose(bank_turn[k % 2][:, i * P:(i + 1) * P], raw[:, at:at + P],
                                            core.ident[:, :])
                    last.then_inc(weights_filled, 1)
            turn_weights(range(0, GATE_UP_JOBS))
            pe.wait_ge(weights_ready, GATE_UP_JOBS)

            def step(t, s, front, middle, tail):
                def down(b, tiles):
                    for m in tiles:
                        if m % 4 == 0:
                            pe.wait_ge(innerT_ready, HALVES * b + m // 4 + 1)
                        last = pe.matmul(bank_y[:, 0:EMBED], innerT[:, m, :], w_down[:, m, :],
                                         start=(m == 0), stop=(m == TILES - 1))
                    return last

                for j in range(HALVES):
                    if middle:
                        b = t - 1
                        pe.wait_ge(layer.hT_ready, b + 1)
                        pe.wait_ge(inner_ready, nonneg(HALVES * (b - 1) + j + 1))
                        for bank, wt in ((bank_gate[j], w_gate), (bank_up[j], w_up)):
                            for c in range(EC):
                                last = pe.matmul(bank[:, :], layer.hT[:, c, :], wt[:, c, j * 512:(j + 1) * 512],
                                                 start=(c == 0), stop=(c == EC - 1))
                        last.then_inc(half_filled, 1)
                    if tail:
                        b = t - 2
                        pe.wait_ge(inner_rounded, HALVES * b + j + 1)
                        pe.wait_ge(innerT_ready, nonneg(HALVES * (b - 1) + j + 1))
                        for i in range(4):
                            m = 4 * j + i
                            last = pe.transpose(bank_turn[j][:, i * P:(i + 1) * P], inner_q[s][:, m * P:(m + 1) * P],
                                                core.ident[:, :])
                        last.then_inc(innerT_filled, 1)
                if isinstance(t, int) and t == 1:
                    turn_weights(range(GATE_UP_JOBS, WEIGHT_JOBS))
                    pe.wait_ge(weights_ready, WEIGHT_JOBS)
                if tail:
                    pe.wait_ge(result_ready, nonneg(t - 2))
                    down(t - 2, range(0, TILES // 2))
                if front:
                    pe.wait_ge(layer.hT_ready, nonneg(t))
                    pe.wait_ge(h_done, t + 1)
                    for c in range(EC):
                        last = pe.transpose(bank_h[:, c * P:(c + 1) * P], h_q[:, c * P:(c + 1) * P], core.ident[:, :])
                    last.then_inc(layer.hT_filled, 1)
                if tail:
                    down(t - 2, range(TILES // 2, TILES)).then_inc(layer.y_filled, 1)
            pipeline(pe, step)


def rotary_tables(tokens, embed, head_dim):
    f32 = np.float32
    inverse = f32(1.0) / f32(10000.0) ** (np.arange(0, head_dim, 2, dtype=f32) / f32(head_dim))
    angles = np.outer(np.arange(tokens, dtype=f32), inverse)
    angles = np.concatenate([angles, angles], axis=-1).astype(f32)
    feature = np.arange(embed)
    sign = np.where(feature % 2 == 0, -1, 1).astype(f32)
    cosine = np.cos(angles).astype(f32).T[feature % head_dim]
    sine = np.sin(angles).astype(f32).T[feature % head_dim] * sign[:, None]
    return [np.ascontiguousarray(a.reshape(-1, P, tokens).transpose(1, 0, 2).reshape(P, -1))
            for a in (cosine, sine)]


def constants():
    p, f = np.arange(P)[:, None], np.arange(P)[None, :]
    cosine, sine = rotary_tables(P, EMBED, 16)
    later, earlier = np.where(f > p, NEG, 0), np.where(f < p, NEG, 0)
    rows_of_parity = p % 32 // 16 == np.arange(2)[None, :]
    return {
        "identity": np.eye(P, dtype=np.float32),
        "causal_constants": np.concatenate([cosine, sine, later, earlier, rows_of_parity], axis=1)
                              .astype(np.float32),
    }


def chunks(w):
    k, n = w.shape
    return w.reshape(k // P, P, n).transpose(1, 0, 2).reshape(P, -1)


def per_query_head(w):
    return np.repeat(w.reshape(*w.shape[:-1], 8, 1, 8), 4, axis=-2).reshape(*w.shape[:-1], -1)


def packed_weights(v):
    wqkv = v["L0_attn_Wqkv"]
    swapped = wqkv.reshape(3, EMBED // 2, 2, EMBED)[:, :, ::-1].reshape(3, EMBED, EMBED)
    wq, wk, wv = wqkv.reshape(3, EMBED, EMBED)
    layers = [
        [chunks(wq.T), chunks(swapped[0].T), chunks(wk.T), chunks(swapped[1].T), chunks(wv.T),
         chunks(v["L0_attn_Wout"].T)],
        [chunks(v["L0_xattn_Wq"]), v["L0_xattn_Wk"], v["L0_xattn_Wv"], chunks(v["L0_xattn_Wo"])],
        [chunks(v["L0_ffn_sh_gate"].T), chunks(v["L0_ffn_sh_up"].T), chunks(v["L0_ffn_sh_down"].T),
         chunks(v["L0_ffn_r_gate"].T), chunks(v["L0_ffn_r_up"].T), chunks(v["L0_ffn_r_down"].T),
         chunks(v["L0_ffn_router_weight"].T)],
        [chunks(v["L1_attn_Wq"]), chunks(per_query_head(v["L1_attn_Wk"])), chunks(v["L1_attn_Wo"]),
         chunks(v["L1_attn_Wv"])],
        [chunks(v["L1_xattn_Wq"]), v["L1_xattn_Wk"], v["L1_xattn_Wv"], chunks(v["L1_xattn_Wo"])],
        [v["L1_ffn_gate_w"].reshape(-1, P, EMBED).transpose(1, 0, 2).reshape(P, -1),
         v["L1_ffn_up_w"].reshape(-1, P, EMBED).transpose(1, 0, 2).reshape(P, -1),
         v["L1_ffn_down_w"].reshape(EC, P, -1).transpose(1, 0, 2).reshape(P, -1)],
    ]
    return [np.concatenate(parts, axis=1) for parts in layers]


def build(nc, core_inputs, out):
    with ExitStack() as ctx:
        core = Core(nc, ctx)
        weights = [core_inputs[f"weights_{n}"] for n in range(6) if f"weights_{n}" in core_inputs]
        setup(nc, core, core_inputs["x"], core_inputs["identity"], weights)
        with nc.sbuf_tensor("high_weights", [P, SPLIT_COLUMNS], F32R) as high_weights, \
                nc.sbuf_tensor("low_weights", [P, SPLIT_COLUMNS], F32R) as low_weights:
            causal_attention(nc, core, core_inputs, weights[0], weights[1], high_weights, low_weights)
            cross_attention(nc, core, 1, core_inputs, weights[2], True, (high_weights, low_weights))
        gated_mlp(nc, core, core_inputs, weights[3])
        grouped_attention(nc, core, core_inputs, weights[4])
        cross_attention(nc, core, 4, core_inputs, weights[5], False)
        mx_mlp(nc, core, core_inputs, out)


def kernel(**inputs):
    import concourse.bacc as bacc
    from concourse.bass_utils import run_bass_kernel_spmd

    values = {name: np.asarray(a) for name, a in inputs.items()}
    arrays = {"x": values["x"], "context": values["ctx_1024"], **constants()}
    arrays["gains"] = np.stack([values["L0_xattn_gq"], values["L0_xattn_gk"]], axis=1)
    head_of_row = (np.arange(P)[:, None] % 32 // 8 == np.arange(4)[None, :]).astype(np.float32)
    arrays["grouped_columns"] = np.concatenate(
        [values["L1_attn_bq"].reshape(EC, P).T, per_query_head(values["L1_attn_bk"]).reshape(EC, P).T, head_of_row],
        axis=1)
    arrays["grouped_rows"] = np.concatenate([values["L1_attn_bv"], values["L1_attn_bo"]])[None, :]
    arrays["mask"] = values["mask_BxS2_bf1"].T.view(np.uint8)
    for n, w in enumerate(packed_weights(values)):
        arrays[f"weights_{n}"] = w
    nc = bacc.Bacc("TRN2", target_bir_lowering=False, num_devices=1)
    arrays = {name: np.ascontiguousarray(a) for name, a in arrays.items()}
    drams = {name: nc.dram_tensor(f"in_{name}", a.shape, mybir.dt.from_np(a.dtype), kind="ExternalInput").ap()
             for name, a in arrays.items()}
    out = nc.dram_tensor("out", arrays["x"].shape, F32, kind="ExternalOutput").ap()
    build(nc, drams, out)
    r = run_bass_kernel_spmd(nc, [{f"in_{name}": a for name, a in arrays.items()}], core_ids=[0])
    return r.results[0]["out"]
```
